# Optimizing a Trainium2 kernel written in Bass

```python
import numpy as np
import jax
import jax.numpy as jnp

def _softmax(x, axis=-1):
    return jax.nn.softmax(x, axis=axis)

def _gelu(x):
    return jax.nn.gelu(x, approximate=True)

def _silu(x):
    return jax.nn.silu(x)

def _sigmoid(x):
    return jax.nn.sigmoid(x)

def _layernorm(x, axis=-1, eps=1e-05):
    m = jnp.mean(x, axis=axis, keepdims=True)
    v = jnp.var(x, axis=axis, keepdims=True)
    return (x - m) / jnp.sqrt(v + eps)

def _scatter_add(tgt, idx, src, axis=0):
    return tgt.at[idx].add(src)

def _segment_sum(src, seg, n):
    return jax.ops.segment_sum(src, seg, n)
kernel_name = 'mk_seq_preln_d2_jaxref_r8_e3ba84'

def setup_inputs(seed: int=0):
    np.random.seed(seed)
    _w = jnp.asarray

    def _L0_attn_setup():
        import jax, jax.numpy as jnp
        import numpy as np
        FEATS = 128
        HEAD = 16
        HEAD_DIM = FEATS // HEAD
        EPS = 1e-12

        def _l2norm(t):
            n = jnp.sqrt(jnp.sum(t * t, axis=-1, keepdims=True))
            return t / jnp.maximum(n, EPS)
        key = jax.random.key(seed)
        ks = jax.random.split(key, 10)
        s = 0.02
        inp = {'x': jax.random.normal(ks[0], (4, 256, FEATS), dtype=jnp.float32), 'Wq': jax.random.normal(ks[1], (FEATS, FEATS), dtype=jnp.float32) * s, 'bq': jnp.zeros((FEATS,), dtype=jnp.float32), 'Wk': jax.random.normal(ks[2], (FEATS, FEATS), dtype=jnp.float32) * s, 'bk': jnp.zeros((FEATS,), dtype=jnp.float32), 'Wv': jax.random.normal(ks[3], (FEATS, FEATS), dtype=jnp.float32) * s, 'bv': jnp.zeros((FEATS,), dtype=jnp.float32), 'Wo': jax.random.normal(ks[4], (FEATS, FEATS), dtype=jnp.float32) * s, 'bo': jnp.zeros((FEATS,), dtype=jnp.float32), 'm': jnp.full((HEAD,), 0.5, dtype=jnp.float32)}
        return inp
    _L0_attn_in = _L0_attn_setup()

    def _L0_ffn_setup():
        import jax, jax.numpy as jnp
        import numpy as np
        DIM = 128
        INTER = 128
        N_EXPERTS = 8
        TOPK = 2
        N_SHARED = 2
        key = jax.random.key(seed)
        ks = jax.random.split(key, 10)
        s = 0.02
        return {'x': jax.random.normal(ks[0], (4, 256, DIM), dtype=jnp.float32), 'gate_w': jax.random.normal(ks[1], (N_EXPERTS, DIM), dtype=jnp.float32) * s, 'gate_bias': jax.random.normal(ks[2], (N_EXPERTS,), dtype=jnp.float32) * s, 'w1': jax.random.normal(ks[3], (N_EXPERTS, INTER, DIM), dtype=jnp.float32) * s, 'w3': jax.random.normal(ks[4], (N_EXPERTS, INTER, DIM), dtype=jnp.float32) * s, 'w2': jax.random.normal(ks[5], (N_EXPERTS, DIM, INTER), dtype=jnp.float32) * s, 'sw1': jax.random.normal(ks[6], (N_SHARED * INTER, DIM), dtype=jnp.float32) * s, 'sw3': jax.random.normal(ks[7], (N_SHARED * INTER, DIM), dtype=jnp.float32) * s, 'sw2': jax.random.normal(ks[8], (DIM, N_SHARED * INTER), dtype=jnp.float32) * s}
    _L0_ffn_in = _L0_ffn_setup()

    def _L1_attn_setup():
        import jax, jax.numpy as jnp
        import numpy as np
        EMBED_DIM = 128
        NUM_HEADS = 16
        HEAD_DIM = EMBED_DIM // NUM_HEADS
        WINDOW_SIZE = 32
        SCALE = 1.0 / np.sqrt(HEAD_DIM)

        def _band_mask(T):
            i = jnp.arange(T)[:, None]
            j = jnp.arange(T)[None, :]
            full = j > i
            band = full & (j >= i - (WINDOW_SIZE - 1))
            return band
        key = jax.random.key(seed)
        kx, kq, kk, kv, ko = jax.random.split(key, 5)
        B, T, C = (2, 256, EMBED_DIM)
        x = jax.random.normal(kx, (B, T, C), dtype=jnp.float32)
        s = 1.0 / np.sqrt(C)
        Wq = jax.random.uniform(kq, (C, C), dtype=jnp.float32, minval=-s, maxval=s)
        Wk = jax.random.uniform(kk, (C, C), dtype=jnp.float32, minval=-s, maxval=s)
        Wv = jax.random.uniform(kv, (C, C), dtype=jnp.float32, minval=-s, maxval=s)
        Wo = jax.random.uniform(ko, (C, C), dtype=jnp.float32, minval=-s, maxval=s)
        return {'x': x, 'Wq': Wq, 'Wk': Wk, 'Wv': Wv, 'Wo': Wo}
    _L1_attn_in = _L1_attn_setup()

    def _L1_ffn_setup():
        import jax, jax.numpy as jnp
        import numpy as np
        import math
        B, L, D = (4, 512, 128)
        F = 512
        E = 16
        CAP_FACTOR = 1.0
        EPS = 1e-05
        key = jax.random.key(seed)
        ks = jax.random.split(key, 8)
        std = 0.02
        return {'x': jax.random.normal(ks[0], (B, L, D), dtype=jnp.float32), 'norm_weight': jnp.ones((D,), dtype=jnp.float32), 'router_weight': jax.random.normal(ks[1], (E, D), dtype=jnp.float32) * std, 'router_bias': jnp.zeros((E,), dtype=jnp.float32), 'fc1_weight': jax.random.normal(ks[2], (E, F, D), dtype=jnp.float32) * std, 'fc1_bias': jnp.zeros((E, F), dtype=jnp.float32), 'fc2_weight': jax.random.normal(ks[3], (E, D, F), dtype=jnp.float32) * std, 'fc2_bias': jnp.zeros((E, D), dtype=jnp.float32)}
    _L1_ffn_in = _L1_ffn_setup()
    _d = {'L0_attn_x': _L0_attn_in['x'], 'L0_attn_Wq': _L0_attn_in['Wq'], 'L0_attn_bq': _L0_attn_in['bq'], 'L0_attn_Wk': _L0_attn_in['Wk'], 'L0_attn_bk': _L0_attn_in['bk'], 'L0_attn_Wv': _L0_attn_in['Wv'], 'L0_attn_bv': _L0_attn_in['bv'], 'L0_attn_Wo': _L0_attn_in['Wo'], 'L0_attn_bo': _L0_attn_in['bo'], 'L0_attn_m': _L0_attn_in['m'], 'L0_ffn_gate_w': _L0_ffn_in['gate_w'], 'L0_ffn_gate_bias': _L0_ffn_in['gate_bias'], 'L0_ffn_w1': _L0_ffn_in['w1'], 'L0_ffn_w3': _L0_ffn_in['w3'], 'L0_ffn_w2': _L0_ffn_in['w2'], 'L0_ffn_sw1': _L0_ffn_in['sw1'], 'L0_ffn_sw3': _L0_ffn_in['sw3'], 'L0_ffn_sw2': _L0_ffn_in['sw2'], 'L1_attn_Wq': _L1_attn_in['Wq'], 'L1_attn_Wk': _L1_attn_in['Wk'], 'L1_attn_Wv': _L1_attn_in['Wv'], 'L1_attn_Wo': _L1_attn_in['Wo'], 'L1_ffn_norm_weight': _L1_ffn_in['norm_weight'], 'L1_ffn_router_weight': _L1_ffn_in['router_weight'], 'L1_ffn_router_bias': _L1_ffn_in['router_bias'], 'L1_ffn_fc1_weight': _L1_ffn_in['fc1_weight'], 'L1_ffn_fc1_bias': _L1_ffn_in['fc1_bias'], 'L1_ffn_fc2_weight': _L1_ffn_in['fc2_weight'], 'L1_ffn_fc2_bias': _L1_ffn_in['fc2_bias']}
    _x0 = _d['L0_attn_x']
    _d['L0_attn_x'] = jax.random.normal(jax.random.fold_in(jax.random.key(seed), 1), (16, 512, 128), dtype=_x0.dtype)
    del _x0
    return _d

def reference(L0_attn_x, L0_attn_Wq, L0_attn_bq, L0_attn_Wk, L0_attn_bk, L0_attn_Wv, L0_attn_bv, L0_attn_Wo, L0_attn_bo, L0_attn_m, L0_ffn_gate_w, L0_ffn_gate_bias, L0_ffn_w1, L0_ffn_w3, L0_ffn_w2, L0_ffn_sw1, L0_ffn_sw3, L0_ffn_sw2, L1_attn_Wq, L1_attn_Wk, L1_attn_Wv, L1_attn_Wo, L1_ffn_norm_weight, L1_ffn_router_weight, L1_ffn_router_bias, L1_ffn_fc1_weight, L1_ffn_fc1_bias, L1_ffn_fc2_weight, L1_ffn_fc2_bias):

    def _L0_attn_ref(x, Wq, bq, Wk, bk, Wv, bv, Wo, bo, m):
        import jax, jax.numpy as jnp
        import numpy as np
        FEATS = 128
        HEAD = 16
        HEAD_DIM = FEATS // HEAD
        EPS = 1e-12

        def _l2norm(t):
            n = jnp.sqrt(jnp.sum(t * t, axis=-1, keepdims=True))
            return t / jnp.maximum(n, EPS)
        b, n, f = x.shape

        def proj(W, bias):
            y = x @ W + bias
            return y.reshape(b, n, HEAD, HEAD_DIM).transpose(0, 2, 1, 3)
        q = _l2norm(proj(Wq, bq))
        k = _l2norm(proj(Wk, bk))
        v = proj(Wv, bv)
        sim = jnp.einsum('bhid,bhjd->bhij', q, k)
        sigma_m = jax.nn.sigmoid(m).reshape(1, HEAD, 1, 1)
        scaling = jnp.asarray(n, dtype=x.dtype) ** sigma_m
        attn = sim / scaling
        out = jnp.einsum('bhij,bhjd->bhid', attn, v)
        out = out.transpose(0, 2, 1, 3).reshape(b, n, f)
        return out @ Wo + bo

    def _L0_ffn_ref(x, gate_w, gate_bias, w1, w3, w2, sw1, sw3, sw2):
        import jax, jax.numpy as jnp
        import numpy as np
        DIM = 128
        INTER = 128
        N_EXPERTS = 8
        TOPK = 2
        N_SHARED = 2
        shape = x.shape
        xt = x.reshape(-1, shape[-1])
        scores = jax.nn.softmax((xt @ gate_w.T).astype(jnp.float32), axis=-1)
        _, idx = jax.lax.top_k(scores + gate_bias, TOPK)
        weights = jnp.take_along_axis(scores, idx, axis=1).astype(x.dtype)
        y = jnp.zeros_like(xt)
        for e in range(N_EXPERTS):
            gate_e = jnp.sum(jnp.where(idx == e, weights, 0.0), axis=1)
            h = jax.nn.silu(xt @ w1[e].T) * (xt @ w3[e].T)
            y = y + gate_e[:, None] * (h @ w2[e].T)
        z = jax.nn.silu(xt @ sw1.T) * (xt @ sw3.T) @ sw2.T
        return (y + z).reshape(shape)

    def _L1_attn_ref(x, Wq, Wk, Wv, Wo):
        import jax, jax.numpy as jnp
        import numpy as np
        EMBED_DIM = 128
        NUM_HEADS = 16
        HEAD_DIM = EMBED_DIM // NUM_HEADS
        WINDOW_SIZE = 32
        SCALE = 1.0 / np.sqrt(HEAD_DIM)

        def _band_mask(T):
            i = jnp.arange(T)[:, None]
            j = jnp.arange(T)[None, :]
            full = j > i
            band = full & (j >= i - (WINDOW_SIZE - 1))
            return band
        B, T, C = x.shape
        H, D = (NUM_HEADS, HEAD_DIM)
        q = jnp.einsum('btc,oc->bto', x, Wq).reshape(B, T, H, D)
        k = jnp.einsum('btc,oc->bto', x, Wk).reshape(B, T, H, D)
        v = jnp.einsum('btc,oc->bto', x, Wv).reshape(B, T, H, D)
        att = jnp.einsum('bqhd,bkhd->bhqk', q, k) * SCALE
        mask = _band_mask(T)
        att = jnp.where(mask[None, None, :, :], -jnp.inf, att)
        att = jax.nn.softmax(att, axis=-1)
        out = jnp.einsum('bhqk,bkhd->bqhd', att, v).reshape(B, T, C)
        return jnp.einsum('btc,oc->bto', out, Wo)

    def _L1_ffn_ref(x, norm_weight, router_weight, router_bias, fc1_weight, fc1_bias, fc2_weight, fc2_bias):
        import jax, jax.numpy as jnp
        import numpy as np
        import math
        B, L, D = (4, 512, 128)
        F = 512
        E = 16
        CAP_FACTOR = 1.0
        EPS = 1e-05
        b, l, d = x.shape
        n_tokens = b * l
        n_experts = router_weight.shape[0]
        capacity = max(1, math.ceil(CAP_FACTOR * n_tokens / n_experts))
        top_k = min(capacity, n_tokens)
        xf = x.reshape(n_tokens, d)
        rms = jnp.sqrt(jnp.mean(xf * xf, axis=-1, keepdims=True) + EPS)
        xn = xf / rms * norm_weight
        logits = xn @ router_weight.T + router_bias
        probs = jax.nn.softmax(logits, axis=-1)
        _, idx = jax.lax.top_k(logits.T, top_k)
        xe = xn[idx]
        h = jnp.einsum('ecd,efd->ecf', xe, fc1_weight) + fc1_bias[:, None, :]
        h = jax.nn.gelu(h, approximate=False)
        y = jnp.einsum('ecf,edf->ecd', h, fc2_weight) + fc2_bias[:, None, :]
        gates = jnp.take_along_axis(probs.T, idx, axis=1)
        flat_idx = idx.reshape(-1)
        contrib = (y * gates[:, :, None]).reshape(-1, d)
        output = jnp.zeros((n_tokens, d), dtype=x.dtype).at[flat_idx].add(contrib)
        gate_sums = jnp.zeros((n_tokens, 1), dtype=x.dtype).at[flat_idx].add(gates.reshape(-1, 1))
        assigned = gate_sums > 0
        output = jnp.where(assigned, output / jnp.where(assigned, gate_sums, 1.0), output)
        return output.reshape(b, l, d)
    x = L0_attn_x
    x = x + _L0_attn_ref(_layernorm(x, axis=-1), L0_attn_Wq, L0_attn_bq, L0_attn_Wk, L0_attn_bk, L0_attn_Wv, L0_attn_bv, L0_attn_Wo, L0_attn_bo, L0_attn_m)
    x = x + _L0_ffn_ref(_layernorm(x, axis=-1), L0_ffn_gate_w, L0_ffn_gate_bias, L0_ffn_w1, L0_ffn_w3, L0_ffn_w2, L0_ffn_sw1, L0_ffn_sw3, L0_ffn_sw2)
    x = x + _L1_attn_ref(_layernorm(x, axis=-1), L1_attn_Wq, L1_attn_Wk, L1_attn_Wv, L1_attn_Wo)
    x = x + _L1_ffn_ref(_layernorm(x, axis=-1), L1_ffn_norm_weight, L1_ffn_router_weight, L1_ffn_router_bias, L1_ffn_fc1_weight, L1_ffn_fc1_bias, L1_ffn_fc2_weight, L1_ffn_fc2_bias)
    return x

_drawn_inputs = setup_inputs


def setup_inputs(seed=0):
    import zlib

    import numpy as np

    out = dict(_drawn_inputs(seed))
    spreads = {'L0_attn_bq': (0.0, 0.414),
     'L0_attn_bk': (0.0, 0.1),
     'L0_attn_bv': (0.0, 0.1),
     'L0_attn_bo': (0.0, 0.1),
     'L0_attn_m': (0.5, 0.6),
     'L1_ffn_norm_weight': (1.0, 0.6),
     'L1_ffn_router_bias': (0.0, 2.0),
     'L1_ffn_fc1_bias': (0.0, 0.465),
     'L1_ffn_fc2_bias': (0.0, 0.304)}
    factors = {'L0_ffn_gate_w': 8.0,
     'L0_ffn_gate_bias': 8.0,
     'L0_ffn_w1': 8.0,
     'L0_ffn_w3': 8.0,
     'L0_ffn_w2': 8.0,
     'L0_ffn_sw1': 4.682,
     'L0_ffn_sw3': 4.79,
     'L0_ffn_sw2': 4.686,
     'L1_attn_Wq': 3.133,
     'L1_attn_Wk': 3.044,
     'L1_ffn_fc1_weight': 3.35}
    for name, (base, spread) in spreads.items():
        noise = np.random.default_rng([zlib.crc32(name.encode()), seed]).standard_normal(out[name].shape)
        drawn = base * np.exp(spread * noise) if base else spread * noise
        out[name] = jnp.asarray(drawn.astype(out[name].dtype))
    for name, factor in factors.items():
        out[name] = (out[name] * factor).astype(out[name].dtype)
    return out
```

```python
import numpy as np
import concourse.bass as bass
import concourse.mybir as mybir
from contextlib import ExitStack

F32, BF16, I32 = mybir.dt.float32, mybir.dt.bfloat16, mybir.dt.int32
ALU = mybir.AluOpType
ACT = mybir.ActivationFunctionType
X = mybir.AxisListType.X

P = 128
BATCH, SEQ, D = 16, 512, 128
Q = SEQ // P
TOK = BATCH * SEQ
TILES = TOK // P
HEADS, HD = 16, 8
E0, TOPK, SHARED = 8, 2, 2
U0 = E0 + SHARED
E1, FF = 16, 512
CAP = TOK // E1
FC = FF // P
CC = CAP // P
EPS = 1e-5
L2_EPS_SQ = 1e-24
SCALE = float(1.0 / np.sqrt(HD))
MASKED = -1.0e38
PARTS = 3
QK_ROWS = PARTS * PARTS * HD
MX_ROW = QK_ROWS
K_ROWS = QK_ROWS + PARTS
FILLS = HEADS // 2 * 5
ROW = D + E1
CROW = D + 4
GJ = TILES // 8


def build_kernel(nc, a, out, debug=None):
    ctx = ExitStack()
    with ctx:
        def sb(name, shape, dt=F32):
            return ctx.enter_context(nc.sbuf_tensor(name, shape, dt))

        early = ExitStack()

        def sb1(name, shape, dt=F32):
            return early.enter_context(nc.sbuf_tensor(name, shape, dt))

        def sem(name):
            return ctx.enter_context(nc.semaphore(name))

        qk_parts = nc.dram_tensor("qk_parts", (BATCH, 2, PARTS, P, SEQ), BF16, kind="Internal").ap()
        xn_rows = nc.dram_tensor("xn_rows", (TOK, ROW), F32, kind="Internal").ap()
        sum_rows = nc.dram_tensor("sum_rows", (TOK, CROW), F32, kind="Internal").ap()
        lists = nc.dram_tensor("lists", (E1, CAP), I32, kind="Internal").ap()

        fa = [ctx.enter_context(nc.psum_tensor(f"fa{i}", [P, 512], F32)) for i in range(3)]
        facc = ctx.enter_context(nc.psum_tensor("facc", [P, 512], F32))
        ba = [ctx.enter_context(nc.psum_tensor(f"ba{i}", [P, 512], F32)) for i in range(3)]
        bo = ctx.enter_context(nc.psum_tensor("bo", [P, 512], F32))

        ident = sb("ident", [P, P])
        zrow = sb("zrow", [P, CROW])
        identb = sb("identb", [P, P], BF16)
        mask_q = sb("mask_q", [P, P], BF16)
        mask_k = sb("mask_k", [P, P], BF16)
        pick = sb("pick", [P, E0, P], BF16)
        blockdiag = sb("blockdiag", [P, HEADS, HD])
        below = sb("below", [P, E0, E0])
        above = sb("above", [P, E0, E0])
        same_e = sb("same_e", [P, P])
        earlier_e = sb("earlier_e", [P, P])
        mhalf = sb("mhalf", [P, P])
        iota32 = sb("iota32", [P, 32])
        iota16 = sb("iota16", [P, 16])
        pcol = sb("pcol", [P, 1])
        tcol = sb("tcol", [P, 8, GJ])
        x3 = sb("x3", [P, TILES, D])
        logits_flat = sb("logits", [P, TILES, E1])
        w_kvq = sb1("w_kvq", [P, 3 * D])
        b_kvq = sb1("b_kvq", [P, 3 * D])
        w_o0 = sb1("w_o0", [P, D])
        b_o0 = sb1("b_o0", [P, D])
        m_b = sb1("m_b", [P, HEADS])
        inv_scaling = sb1("inv_scaling", [P, HEADS])
        kv_scale = sb1("kv_scale", [P, HEADS, HD])
        gate_w = sb1("gate_w", [P, E0])
        gate_b = sb1("gate_b", [P, E0])
        w1 = sb1("w1", [P, U0, P])
        w3 = sb1("w3", [P, U0, P])
        w2 = sb1("w2", [P, U0, P])
        w_q1 = sb1("w_q1", [P, D])
        w_k1 = sb1("w_k1", [P, D])
        w_v1 = sb1("w_v1", [P, D])
        w_o1 = sb1("w_o1", [P, D])
        norm_w = sb1("norm_w", [P, D])
        router_w = sb1("router_w", [P, E1])
        router_b = sb1("router_b", [P, E1])
        xin = sb1("xin", [P, Q, D])
        xres = sb1("xres", [P, Q, D])
        f_st = sb1("f_st", [P, Q, 6])
        f_mv = sb1("f_mv", [P, Q, 2])
        f_ve = sb1("f_ve", [P, P])
        f_rs = sb1("f_rs", [P, P])
        f_n = sb1("f_n", [P, Q, D])
        f_nT = sb1("f_nT", [P, SEQ])
        kvq = sb1("kvq", [P, Q, 3 * D])
        sq = sb1("sq", [P, Q, 2 * D])
        qnT = sb1("qnT", [P, SEQ])
        kvm = sb1("kvm", [P, P])
        kvo = sb1("kvo", [P, P])
        x1 = sb1("x1", [P, Q, D])
        lg = sb1("lg", [P, Q, E0])
        lm = sb1("lm", [P, Q])
        ls = sb1("ls", [P, Q])
        sc = sb1("sc", [P, Q, E0])
        bs = sb1("bs", [P, Q, E0])
        ge = sb1("ge", [P, Q, E0, E0])
        gt = sb1("gt", [P, Q, E0, E0])
        rank = sb1("rank", [P, Q, E0])
        gates = sb1("gates", [P, Q, E0])
        gres = sb1("gres", [P, Q, E0])
        gparts = sb1("gparts", [P, Q, PARTS, E0], BF16)
        gT = sb1("gT", [P, SEQ], BF16)
        sil = sb1("sil", [P, 2, SEQ])
        th = sb1("th", [P, 2, SEQ])
        hh = sb1("hh", [P, 2, SEQ])
        yT = sb1("yT", [P, SEQ])
        x2 = sb1("x2", [P, Q, D])
        xb = sb1("xb", [P, Q, D])
        b_st = sb1("b_st", [P, Q, 6])
        b_mv = sb1("b_mv", [P, Q, 2])
        b_ve = sb1("b_ve", [P, Q])
        b_rs = sb1("b_rs", [P, Q])
        b_n = sb1("b_n", [P, Q, D])
        b_nT = sb1("b_nT", [P, SEQ])
        qkp = sb1("qkp", [P, 2, PARTS, SEQ], BF16)
        qkr = sb1("qkr", [P, 2, SEQ])
        vp = sb1("vp", [P, Q, HEADS, 32])
        QT = sb1("QT", [P, HEADS, SEQ], BF16)
        KT = sb1("KT", [P, HEADS, SEQ], BF16)
        nm = sb1("nm", [P, Q, HEADS])
        nmr = sb1("nmr", [P, Q, HEADS])
        nmp = sb1("nmp", [P, Q, PARTS, HEADS], BF16)
        nmT = sb1("nmT", [PARTS * HEADS, SEQ], BF16)
        probs = sb1("probs", [P, 3, 5, SEQ])
        oT = sb1("oT", [P, SEQ])
        rden = sb1("rden", [P, Q, 4])
        ao = sb1("ao", [P, Q, D])
        row = sb1("row", [P, Q, ROW])
        l1 = sb1("l1", [P, Q, E1])
        ysq = sb1("ysq", [P, Q])
        l1m = sb1("l1m", [P, Q])

        early.close()
        ones = sb("ones", [P, TOK // 8])
        LT = sb("LT", [P, TOK // 8])
        above_t = sb("above_t", [P, TOK // 8])
        equal_t = sb("equal_t", [P, TOK // 8])
        place = sb("place", [P, TOK // 8])
        chosen = sb("chosen", [P, TOK // 8])
        key, cand, flip, bits, bit, okm = (sb(n, [P, 1], I32) for n in ("key", "cand", "flip", "bits", "bit", "okm"))
        cnt, more, off_eq, off_sel = (sb(n, [P, 1]) for n in ("cnt", "more", "off_eq", "off_sel"))
        slot = sb("slot", [P, 8, P], I32)
        hi_i, lo_i = sb("hi_i", [P, 8, P], I32), sb("lo_i", [P, 8, P], I32)
        hi, lo = sb("hi", [P, 8, P], BF16), sb("lo", [P, 8, P], BF16)
        hot_hi = sb("hot_hi", [P, 2, P, 32], BF16)
        hot_lo = sb("hot_lo", [P, 2, 2, P, 16], BF16)
        hot = sb("hot", [P, 2, P, 16], BF16)
        found = sb("found", [P, 4, 2, 64])
        idx = sb("idx", [P, 4, 16], I32)
        idx_pc = sb("idx_pc", [P, E1, CC], I32)
        cur = [sb(f"cur{i}", [P, CC], I32) for i in range(2)]
        got = [sb(f"got{i}", [P, CC, ROW]) for i in range(2)]
        gate = [sb(f"gate{i}", [P, CC]) for i in range(2)]
        xe = [sb(f"xe{i}", [P, CAP]) for i in range(2)]
        fc1 = [sb(f"fc1_{i}", [P, FF]) for i in range(2)]
        fc2 = [sb(f"fc2_{i}", [P, FC, D]) for i in range(2)]
        fb2 = [sb(f"fb2_{i}", [P, D]) for i in range(2)]
        fb1 = sb("fb1", [P, E1, FC])
        fb1c = [sb(f"fb1c{i}", [P, FC]) for i in range(2)]
        hT = [sb(f"hT{i}", [P, FC, CAP]) for i in range(2)]
        ysum = [sb(f"ysum{i}", [P, CC, D]) for i in range(2)]
        contrib = [sb(f"contrib{i}", [P, CC, CROW]) for i in range(2)]
        sums = sb("sums", [P, TILES, CROW])
        gsum = sb("gsum", [P, TILES])
        logits_gj = sb("logits_gj", [P, 8, P])

        names = """s_wfront s_wback s_cst s_one s_scal s_x s_lnf s_xres s_varf s_rsf s_T1 s_nT1 s_kvq s_kvqe s_sq
            s_kqn s_kvt s_kvm s_qT s_qnT s_kvo s_kvoc s_at0 s_x1 s_x1n s_T2 s_nT2 s_lgm s_lge s_exf s_lgx s_gp s_gTp s_gT
            s_h1 s_h3 s_gb s_sil s_t s_h s_ym s_yT s_yTt s_x2 s_fc
            s_lnb s_xb s_varb s_rsb s_T3 s_nT3 s_q s_k s_v s_p1 s_r1 s_p2 s_p3 s_vp s_qkw s_qk s_S s_red s_nmp s_nmt
            s_nmT s_mx s_st s_exp s_pv s_oT s_tr s_norm s_aTt s_aT s_wo s_x3 s_y s_ysq s_row s_T4 s_nT4 s_l1 s_l1c
            s_l1x s_ex1 s_prob s_rowd s_bc s_zero
            s_LTt s_LTc s_cnt s_tot s_sr s_gtc s_gtt s_eqt s_selt s_rc s_slT s_slot s_hot s_list s_bit s_rc2 s_gatec s_fs s_gj s_found s_idx s_bc1 s_ldw s_ldr
            s_cur s_got0 s_got1 s_xet s_xe s_fw0 s_fw1 s_up s_hT s_dn s_ys s_con s_sc s_ec s_sum0 s_sum1 s_sum2 s_sum3 s_fin s_out s_fb""".split()
        S = {n: sem(n) for n in names}
        block = ctx.enter_context(nc.Block())
        FW = 16 * 15
        BW = 16 * 6

        def apart(eng):
            eng.nop(nofuse=True)

        def bcast_rows(v, n):
            return v.rearrange("(o n) -> o n", o=1)[0].partition_broadcast(P)

        def looped(engine, front, x_phase, back_front, y_phase):
            front(0)
            x_phase(0, None)
            with engine.Fori(0, BATCH - 1) as i:
                back_front(i)
                front(i + 1)
                x_phase(i + 1, i)
                y_phase(i)
            back_front(BATCH - 1)
            x_phase(None, BATCH - 1)
            y_phase(BATCH - 1)

        @block.sync
        def _(sp):
            for dst, src in (
                (w_kvq[:, 0:D], a["L0_attn_Wk"]), (w_kvq[:, D:2 * D], a["L0_attn_Wv"]), (w_kvq[:, 2 * D:], a["L0_attn_Wq"]),
                (b_kvq[:, 0:D], bcast_rows(a["L0_attn_bk"], D)), (b_kvq[:, D:2 * D], bcast_rows(a["L0_attn_bv"], D)),
                (b_kvq[:, 2 * D:], bcast_rows(a["L0_attn_bq"], D)),
                (w_o0[:], a["L0_attn_Wo"]), (b_o0[:], bcast_rows(a["L0_attn_bo"], D)), (m_b[:], bcast_rows(a["L0_attn_m"], HEADS)),
                (gate_w[:], a["L0_ffn_gate_w"]), (gate_b[:], bcast_rows(a["L0_ffn_gate_bias"], E0)),
            ):
                sp.dma_start(dst, src).then_inc(S["s_wfront"], 16)
            sp.dma_start(xin[:], a["L0_attn_x"][0].rearrange("(q p) d -> p q d", p=P)).then_inc(S["s_x"], 16)
            for dst, src in ((w1, "w1"), (w3, "w3"), (w2, "w2")):
                sp.dma_start(dst[:], a["L0_" + src]).then_inc(S["s_wfront"], 16)
            sp.dma_start(norm_w[:], bcast_rows(a["L1_ffn_norm_weight"], D)).then_inc(S["s_wfront"], 16)
            for dst, name in ((w_q1, "L1_attn_Wq"), (w_k1, "L1_attn_Wk"), (w_v1, "L1_attn_Wv"), (w_o1, "L1_attn_Wo"),
                              (router_w, "L1_ffn_router_weight")):
                sp.dma_start(dst[:], a[name]).then_inc(S["s_wback"], 16)
            sp.dma_start(router_b[:], bcast_rows(a["L1_ffn_router_bias"], E1)).then_inc(S["s_wback"], 16)
            sp.wait_ge(S["s_cst"], 1)
            sp.dma_start(sum_rows.rearrange("(t p) c -> p t c", p=P),
                         zrow[:, None, :].to_broadcast([P, TILES, CROW])).then_inc(S["s_zero"], 16)

            def back_dmas(b):
                for w in range(2):
                    sp.wait_ge(S["s_p3"], 2 * b + w + 1)
                    apart(sp)
                    sp.dma_start(qk_parts[b, w].rearrange("c p t -> p c t"), qkp[:, w]).then_inc(S["s_qkw"], 16)
                sp.wait_ge(S["s_qkw"], 32 * b + 32)
                apart(sp)
                sp.wait_ge(S["s_st"], FILLS * b)
                apart(sp)
                for i in range(PARTS):
                    for j in range(PARTS):
                        r = (i * PARTS + j) * HD
                        sp.dma_start(QT[r:r + HD], qk_parts[b, 0, i].rearrange("(h d) t -> d h t", d=HD)).then_inc(S["s_qk"], 16)
                        sp.dma_start(KT[r:r + HD], qk_parts[b, 1, j].rearrange("(h d) t -> d h t", d=HD)).then_inc(S["s_qk"], 16)

            def max_dmas(b):
                sp.wait_ge(S["s_nmT"], b + 1)
                apart(sp)
                for c in range(PARTS):
                    sp.dma_start(QT[MX_ROW + c:MX_ROW + c + 1], nmT[c * HEADS:(c + 1) * HEADS, :]).then_inc(S["s_mx"], 16)

            def row_dmas(b):
                sp.wait_ge(S["s_prob"], b + 1)
                apart(sp)
                sp.dma_start(xn_rows[bass.ts(b, SEQ)].rearrange("(q p) c -> p q c", p=P), row[:]).then_inc(S["s_rowd"], 16)

            def load_x(b):
                sp.wait_ge(S["s_lnf"], b)
                sp.wait_ge(S["s_xres"], b)
                apart(sp)
                sp.dma_start(xin[:], a["L0_attn_x"][b].rearrange("(q p) d -> p q d", p=P)).then_inc(S["s_x"], 16)

            with sp.Fori(0, BATCH - 1) as i:
                load_x(i + 1)
                back_dmas(i)
                max_dmas(i)
                row_dmas(i)
            back_dmas(BATCH - 1)
            max_dmas(BATCH - 1)
            row_dmas(BATCH - 1)
            sp.wait_ge(S["s_rowd"], 16 * BATCH)
            if debug == "x3":
                sp.dma_start(out.rearrange("b (q p) d -> p (b q) d", p=P), x3[:]).then_inc(S["s_zero"], 16)
                sp.wait_ge(S["s_zero"], 32)
                return

            sp.wait_ge(S["s_prob"], BATCH)
            sp.dma_start(fb1[:], a["L1_ffn_fc1_bias"]).then_inc(S["s_fb"], 16)
            sp.wait_ge(S["s_idx"], 16)
            sp.dma_start(lists.rearrange("(g e) (h l) -> (e h) g l", g=4, l=16), idx[:]).then_inc(S["s_ldw"], 16)
            sp.wait_ge(S["s_ldw"], 16)
            sp.dma_start(idx_pc[:], lists.rearrange("e (p c) -> p e c", c=CC)).then_inc(S["s_ldr"], 16)
            with sp.Fori(0, E1 // 2) as i:
                for k in range(2):
                    sp.wait_ge(S["s_ys"], 2 * i + max(k - 1, 0))
                    apart(sp)
                    sp.dma_start(fc1[k][:], a["L1_ffn_fc1_weight"][:, 2 * i + k]).then_inc(S[f"s_fw{k}"], 16)
                    sp.dma_start(fc2[k][:], a["L1_ffn_fc2_weight"][:, 2 * i + k]).then_inc(S[f"s_fw{k}"], 16)
                    sp.dma_start(fb2[k][:], a["L1_ffn_fc2_bias"][2 * i + k].partition_broadcast(P)).then_inc(S[f"s_fw{k}"], 16)
            sp.wait_ge(S["s_sc"], 16 * CC * E1)
            n = TILES // 4
            rows = sum_rows.rearrange("(t p) c -> p t c", p=P)
            for k in range(4):
                sp.dma_start(sums[:, k * n:(k + 1) * n], rows[:, k * n:(k + 1) * n]).then_inc(S[f"s_sum{k}"], 16)
            for k in range(4):
                sp.wait_ge(S["s_fin"], k + 1)
                sp.dma_start(out.rearrange("b (q p) d -> p (b q) d", p=P)[:, k * n:(k + 1) * n], x3[:, k * n:(k + 1) * n]).then_inc(S["s_out"], 16)
            sp.wait_ge(S["s_out"], 64)

        @block.gpsimd
        def _(pool):
            c = [1]

            def const(ins):
                c[0] += 1
                ins.then_inc(S["s_cst"], 1)
                pool.wait_ge(S["s_cst"], c[0])

            pool.memset(zrow[:], 0.0).then_inc(S["s_cst"], 1)
            pool.wait_ge(S["s_cst"], 1)
            for t in (ident, identb):
                const(pool.memset(t[:], 0.0))
                const(pool.affine_select(t[:], t[:], [[-1, P]], ALU.not_equal, 1.0, base=0, channel_multiplier=1))
            const(pool.memset(mask_q[:], 0.0))
            const(pool.affine_select(mask_q[:], mask_q[:], [[-1, P]], ALU.is_ge, MASKED, base=0, channel_multiplier=1))
            const(pool.memset(mask_k[:], 0.0))
            const(pool.affine_select(mask_k[:], mask_k[:], [[1, P]], ALU.is_ge, MASKED, base=0, channel_multiplier=-1))
            const(pool.memset(pick[:], 0.0))
            for part in range(PARTS):
                const(pool.affine_select(pick[:], pick[:], [[-1, E0], [0, P]], ALU.not_equal, 1.0, base=-E0 * part, channel_multiplier=1))
            const(pool.memset(blockdiag[:], 1.0))
            const(pool.affine_select(blockdiag[:], blockdiag[:], [[-HD, HEADS], [0, HD]], ALU.is_ge, 0.0, base=0, channel_multiplier=1))
            const(pool.affine_select(blockdiag[:], blockdiag[:], [[HD, HEADS], [0, HD]], ALU.is_ge, 0.0, base=HD - 1, channel_multiplier=-1))
            const(pool.memset(below[:], 1.0))
            const(pool.affine_select(below[:], below[:], [[1, E0], [-1, E0]], ALU.is_ge, 0.0, base=-1, channel_multiplier=0))
            const(pool.memset(above[:], 1.0))
            const(pool.affine_select(above[:], above[:], [[-1, E0], [1, E0]], ALU.is_ge, 0.0, base=-1, channel_multiplier=0))
            for m in range(-7, 8):
                if m == -7:
                    const(pool.memset(same_e[:], 0.0))
                    const(pool.memset(earlier_e[:], 0.0))
                const(pool.affine_select(same_e[:], same_e[:], [[-1, P]], ALU.not_equal, 1.0, base=E1 * m, channel_multiplier=1))
                if m > 0:
                    const(pool.affine_select(earlier_e[:], earlier_e[:], [[-1, P]], ALU.not_equal, 1.0, base=E1 * m, channel_multiplier=1))
            const(pool.iota(iota32[:], [[1, 32]], base=0, channel_multiplier=0, allow_small_or_imprecise_dtypes=True))
            const(pool.iota(iota16[:], [[1, 16]], base=0, channel_multiplier=0, allow_small_or_imprecise_dtypes=True))
            const(pool.iota(pcol[:], [[1, 1]], base=0, channel_multiplier=1, allow_small_or_imprecise_dtypes=True))
            const(pool.iota(tcol[:], [[1, 8], [8, GJ]], base=0, channel_multiplier=0, allow_small_or_imprecise_dtypes=True))
            const(pool.memset(mhalf[:], -0.5))
            const(pool.memset(gT[:], 0.0))
            const(pool.memset(KT[64:96], 1.0))
            const(pool.memset(vp[:], 0.0))
            const(pool.memset(vp[:, :, :, HD:HD + 1], 1.0))
            pool.memset(nmT[:], 0.0).then_inc(S["s_one"], 1)

            def power(dst, src, ready, done, count):
                pool.wait_ge(S[ready], count)
                pool.tensor_tensor(dst, src, mhalf[:, 0:src.shape[-1]], ALU.pow).then_inc(S[done], 1)

            def front(b):
                pool.wait_ge(S["s_x"], 16 * b + 16)
                pool.wait_ge(S["s_wfront"], FW)
                pool.wait_ge(S["s_x1"], b)
                pool.tensor_tensor(xres[:], xin[:], b_o0[:, None, :].to_broadcast([P, Q, D]), ALU.add).then_inc(S["s_xres"], 1)
                power(f_rs[:, 0:Q], f_ve[:, 0:Q], "s_varf", "s_rsf", 3 * b + 1)
                power(f_rs[:], f_ve[:], "s_varf", "s_rsf", 3 * b + 2)
                power(f_rs[:, 0:Q], f_ve[:, 0:Q], "s_varf", "s_rsf", 3 * b + 3)

            def back_front(b):
                pool.wait_ge(S["s_x2"], b + 1)
                pool.wait_ge(S["s_x3"], b)
                apart(pool)
                pool.tensor_copy(xb[:], x2[:]).then_inc(S["s_xb"], 1)
                power(b_rs[:], b_ve[:], "s_varb", "s_rsb", 3 * b + 1)
                for w in range(2):
                    pool.wait_ge(S["s_r1"], 2 * b + w + 1)
                    apart(pool)
                    pool.tensor_copy(qkp[:, w, 1], qkr[:, w]).then_inc(S["s_p2"], 1)
                    pool.wait_ge(S["s_p2"], 2 * b + w + 1)
                    pool.tensor_tensor(qkp[:, w, 2], qkr[:, w], qkp[:, w, 1], ALU.subtract).then_inc(S["s_p3"], 1)

            def y_phase(b):
                power(b_rs[:], b_ve[:], "s_varb", "s_rsb", 3 * b + 2)
                power(b_rs[:], b_ve[:], "s_varb", "s_rsb", 3 * b + 3)

            looped(pool, front, lambda f, b: None, back_front, y_phase)
            if debug == "x3":
                return
            pool.wait_ge(S["s_prob"], BATCH)
            pool.wait_ge(S["s_rowd"], 16 * BATCH)
            pool.memset(ones[:], 1.0).then_inc(S["s_ec"], 1)
            pool.memset(key[:], 0).then_inc(S["s_ec"], 1)
            pool.memset(bit[:], -2 ** 31).then_inc(S["s_ec"], 1)
            for k in range(2):
                pool.memset(contrib[k][:], 0.0).then_inc(S["s_ec"], 1)

            def gather(e, k, c):
                pool.indirect_dma_start(got[k][:, c], None, xn_rows, bass.IndirectOffsetOnAxis(cur[k][:, c:c + 1], 0)).then_inc(S[f"s_got{k}"], 16)

            pool.wait_ge(S["s_zero"], 16)
            pool.wait_ge(S["s_cur"], 1)
            for c in range(CC):
                gather(0, 0, c)

            def pool_expert(i, k, more_rows=True):
                e = 2 * i + k
                if more_rows:
                    pool.wait_ge(S["s_cur"], e + 2)
                    apart(pool)
                    for c in range(CC):
                        gather(e + 1, 1 - k, c)
                pool.wait_ge(S["s_con"], e + 1)
                pool.wait_ge(S["s_sc"], 16 * CC * e)
                apart(pool)
                for c in range(CC):
                    pool.indirect_dma_start(sum_rows, bass.IndirectOffsetOnAxis(cur[k][:, c:c + 1], 0), contrib[k][:, c], None,
                                            compute_op=ALU.add).then_inc(S["s_sc"], 16)

            with pool.Fori(0, E1 // 2 - 1) as i:
                pool_expert(i, 0)
                pool_expert(i, 1)
            pool_expert(E1 // 2 - 1, 0)
            pool_expert(E1 // 2 - 1, 1, False)

        def scores(pe, b, n, by_key):
            pair, f = divmod(n, 5)
            h = 2 * pair + (f // 2 if f < 4 else 0)
            bank = ba[n % 3]
            if f in (0, 2):
                groups = [(h, 3 if not by_key else 0, 0)]
            elif f in (1, 3):
                groups = [(h, 2, 0), (h, 0, 384)] if not by_key else [(h, 1, 0), (h, 3, 384)]
            else:
                groups = [(h, 1, 0), (h + 1, 1, 256)] if not by_key else [(h, 2, 0), (h + 1, 2, 256)]
            for head, blk, col in groups:
                if by_key:
                    w = SEQ - blk * P
                    pe.matmul(bank[:, col:col + w], lhsT=KT[0:K_ROWS, head, blk * P:(blk + 1) * P],
                              rhs=QT[0:K_ROWS, head, blk * P:], start=True, stop=False)
                    last = pe.matmul(bank[:, col:col + P], lhsT=identb[:], rhs=mask_k[:], start=False, stop=True)
                else:
                    w = (blk + 1) * P
                    pe.matmul(bank[:, col:col + w], lhsT=QT[0:QK_ROWS, head, blk * P:(blk + 1) * P],
                              rhs=KT[0:QK_ROWS, head, 0:w], start=True, stop=False)
                    last = pe.matmul(bank[:, col + w - P:col + w], lhsT=identb[:], rhs=mask_q[:], start=False, stop=True)
            last.then_inc(S["s_st" if by_key else "s_S"], 1)

        def prob_block(h, blk):
            slot, k = (h // 2) % 3, h % 2
            if blk == 0:
                return probs[:, slot, 2 * k, :]
            if blk == 1:
                return probs[:, slot, 2 * k + 1, 0:384]
            if blk == 3:
                return probs[:, slot, 2 * k + 1, 384:512]
            return probs[:, slot, 4, 256 * k:256 * k + 256]

        @block.tensor
        def _(pe):
            def transposes(bank, src, done):
                for q in range(Q):
                    last = pe.transpose(bank[:, q * P:(q + 1) * P], src[:, q], ident[:])
                last.then_inc(S[done], 1)

            def front(b):
                pe.wait_ge(S["s_lnf"], b + 1)
                transposes(fa[0], f_n, "s_T1")
                pe.wait_ge(S["s_nT1"], b + 1)
                for q in range(Q):
                    if q == 3:
                        pe.wait_ge(S["s_kvqe"], Q * b + 1)
                    pe.matmul(fa[(q + 1) % 3][:, 0:3 * D], lhsT=f_nT[:, q * P:(q + 1) * P], rhs=w_kvq[:],
                              start=True, stop=True).then_inc(S["s_kvq"], 1)
                pe.wait_ge(S["s_kqn"], b + 1)
                pe.wait_ge(S["s_kvqe"], Q * b + Q)
                for q in range(Q):
                    last = pe.matmul(fa[2][:, 0:P], lhsT=kvq[:, q, D:2 * D], rhs=kvq[:, q, 0:D], start=q == 0, stop=q == Q - 1)
                last.then_inc(S["s_kvt"], 1)
                for q in range(Q):
                    last = pe.transpose(fa[0][:, q * P:(q + 1) * P], kvq[:, q, 2 * D:3 * D], ident[:])
                last.then_inc(S["s_qT"], 1)
                pe.wait_ge(S["s_kvm"], b + 1)
                pe.matmul(fa[1][:, 0:D], lhsT=kvm[:], rhs=w_o0[:], start=True, stop=True).then_inc(S["s_kvo"], 1)
                pe.wait_ge(S["s_qnT"], b + 1)
                pe.wait_ge(S["s_kvoc"], b + 1)
                for q in range(Q):
                    last = pe.matmul(fa[2][:, q * D:(q + 1) * D], lhsT=qnT[:, q * P:(q + 1) * P], rhs=kvo[:], start=True, stop=True)
                last.then_inc(S["s_at0"], 1)
                pe.wait_ge(S["s_lnf"], b + 1)
                pe.wait_ge(S["s_x1n"], b + 1)
                transposes(fa[0], f_n, "s_T2")
                pe.wait_ge(S["s_nT2"], b + 1)
                for q in range(Q):
                    last = pe.matmul(fa[1][:, q * E0:(q + 1) * E0], lhsT=f_nT[:, q * P:(q + 1) * P], rhs=gate_w[:], start=True, stop=True)
                last.then_inc(S["s_lgm"], 1)
                pe.wait_ge(S["s_gp"], b + 1)
                apart(pe)
                for q in range(Q):
                    last = pe.transpose(fa[2][:].bitcast(BF16)[0:PARTS * E0, q * P:(q + 1) * P],
                                        gparts[:, q].rearrange("p c e -> p (c e)"), identb[:])
                last.then_inc(S["s_gTp"], 1)

            def up(b, e):
                if e == 0:
                    pe.wait_ge(S["s_gT"], b + 1)
                    pe.wait_ge(S["s_lge"], b + 1)
                else:
                    pe.wait_ge(S["s_sil"], U0 * b + e)
                pe.matmul(fa[0][:], lhsT=w1[:, e], rhs=f_nT[:], start=True, stop=True).then_inc(S["s_h1"], 1)
                if 0 < e <= E0:
                    pe.wait_ge(S["s_t"], E0 * b + e)
                elif e > E0:
                    pe.wait_ge(S["s_h"], U0 * b + e)
                pe.matmul(fa[1][:], lhsT=w3[:, e], rhs=f_nT[:], start=True, stop=True).then_inc(S["s_h3"], 1)
                if e < E0:
                    if e > 0:
                        pe.wait_ge(S["s_h"], U0 * b + e)
                    pe.matmul(fa[2][:], lhsT=pick[:, e], rhs=gT[:], start=True, stop=True).then_inc(S["s_gb"], 1)

            def down(b, e):
                pe.wait_ge(S["s_h"], U0 * b + e + 1)
                if e == 0:
                    pe.wait_ge(S["s_yT"], b)
                pe.matmul(facc[:], lhsT=w2[:, e], rhs=hh[:, e % 2], start=e == 0, stop=e == U0 - 1).then_inc(S["s_ym"], 1)

            def back_front(b):
                pe.wait_ge(S["s_lnb"], b + 1)
                if_free(b)
                transposes(ba[0], b_n, "s_T3")
                pe.wait_ge(S["s_nT3"], b + 1)
                pe.matmul(ba[1][:], lhsT=w_q1[:], rhs=b_nT[:], start=True, stop=True).then_inc(S["s_q"], 1)
                pe.matmul(ba[2][:], lhsT=w_k1[:], rhs=b_nT[:], start=True, stop=True).then_inc(S["s_k"], 1)
                for q in range(Q):
                    last = pe.matmul(ba[0][:, q * D:(q + 1) * D], lhsT=b_nT[:, q * P:(q + 1) * P], rhs=w_v1[:], start=True, stop=True)
                last.then_inc(S["s_v"], 1)

            def if_free(b):
                pe.wait_ge(S["s_x3"], b)
                pe.wait_ge(S["s_l1c"], b)

            def x_phase(f, b):
                for step in range(U0 + 1):
                    if f is not None:
                        if step < U0:
                            up(f, step)
                    if b is not None and step < HEADS // 2:
                        for n in range(5 * step, 5 * step + 5):
                            if n == 0:
                                pe.wait_ge(S["s_qk"], 16 * 2 * PARTS * PARTS * (b + 1))
                                pe.wait_ge(S["s_vp"], b + 1)
                                pe.wait_ge(S["s_r1"], 2 * b + 2)
                            if n >= 3:
                                pe.wait_ge(S["s_red"], FILLS * b + n - 2)
                            scores(pe, b, n, False)
                    if f is not None and step > 0:
                        down(f, step - 1)
                if f is not None:
                    pe.wait_ge(S["s_yT"], f + 1)
                    for q in range(Q):
                        last = pe.transpose(fa[0][:, q * P:(q + 1) * P], yT[:, q * P:(q + 1) * P], ident[:])
                    last.then_inc(S["s_yTt"], 1)

            def y_phase(b):
                pe.wait_ge(S["s_nmp"], b + 1)
                pe.wait_ge(S["s_nT4"], b)
                apart(pe)
                for q in range(Q):
                    last = pe.transpose(bo[:].bitcast(BF16)[0:PARTS * HEADS, q * P:(q + 1) * P],
                                        nmp[:, q].rearrange("p c h -> p (c h)"), identb[:])
                last.then_inc(S["s_nmt"], 1)
                pe.wait_ge(S["s_mx"], 16 * PARTS * (b + 1))
                pe.wait_ge(S["s_red"], FILLS * (b + 1))

                def pair_scores(pair):
                    for n in range(5 * pair, 5 * pair + 5):
                        if n >= 3:
                            pe.wait_ge(S["s_exp"], FILLS * b + n - 2)
                        scores(pe, b, n, True)

                pair_scores(0)
                pair_scores(1)
                for k in range(4):
                    if k < 3:
                        pair_scores(2 * k + 2)
                    pe.wait_ge(S["s_exp"], FILLS * b + 10 * k + 10)
                    if k > 0:
                        pe.wait_ge(S["s_norm"], 4 * b + k)
                    for blk in range(Q):
                        for j in range(4):
                            last = pe.matmul(bo[32 * j:32 * j + 32, blk * P:], lhsT=vp[:, blk, 4 * k + j],
                                             rhs=prob_block(4 * k + j, blk), start=blk == 0, stop=blk == Q - 1)
                    last.then_inc(S["s_pv"], 1)
                    if k < 3:
                        pair_scores(2 * k + 3)
                    pe.wait_ge(S["s_oT"], 4 * b + k + 1)
                    for q in range(Q):
                        last = pe.transpose(bo[:, q * P:(q + 1) * P], oT[:, q * P:(q + 1) * P], ident[:])
                    last.then_inc(S["s_tr"], 1)
                pe.wait_ge(S["s_norm"], 4 * b + 4)
                transposes(bo, ao, "s_aTt")
                pe.wait_ge(S["s_aT"], b + 1)
                for q in range(Q):
                    last = pe.matmul(ba[0][:, q * D:(q + 1) * D], lhsT=b_nT[:, q * P:(q + 1) * P], rhs=w_o1[:], start=True, stop=True)
                last.then_inc(S["s_wo"], 1)
                pe.wait_ge(S["s_row"], b + 1)
                for q in range(Q):
                    last = pe.transpose(bo[:, q * P:(q + 1) * P], row[:, q, 0:D], ident[:])
                last.then_inc(S["s_T4"], 1)
                pe.wait_ge(S["s_nT4"], b + 1)
                for q in range(Q):
                    last = pe.matmul(ba[1][:, q * E1:(q + 1) * E1], lhsT=b_nT[:, q * P:(q + 1) * P], rhs=router_w[:], start=True, stop=True)
                last.then_inc(S["s_l1"], 1)

            pe.wait_ge(S["s_wfront"], FW)
            pe.wait_ge(S["s_wback"], BW)
            pe.wait_ge(S["s_one"], 1)
            looped(pe, front, x_phase, back_front, y_phase)
            if debug == "x3":
                return
            pe.wait_ge(S["s_gj"], 1)
            for g in range(8):
                last = pe.transpose(fa[g // 4][:, (g % 4) * P:(g % 4 + 1) * P], logits_gj[:, g], ident[:])
            last.then_inc(S["s_LTt"], 1)

            def across(col, pattern, src, ready, n, done):
                pe.wait_ge(S[ready], n)
                pe.matmul(fa[2][:, col:col + 1], lhsT=pattern[:], rhs=src[:], start=True, stop=True).then_inc(S[done], 1)

            with pe.Fori(0, 32) as i:
                across(0, same_e, cnt, "s_cnt", i + 1, "s_tot")
            across(0, same_e, cnt, "s_gtc", 1, "s_gtt")
            across(0, earlier_e, cnt, "s_gtc", 2, "s_gtt")
            across(0, earlier_e, cnt, "s_gtc", 3, "s_gtt")
            pe.wait_ge(S["s_rc"], 1)
            for g in range(8):
                last = pe.transpose(fa[g // 4][:, (g % 4) * P:(g % 4 + 1) * P], place[:, g * P:(g + 1) * P], ident[:])
            last.then_inc(S["s_slT"], 1)
            lists_of = [ba[0], ba[1], ba[2], bo]
            for g in range(8):
                pe.wait_ge(S["s_hot"], g + 1)
                for j in range(GJ):
                    for q in range(4):
                        col = j * E1 + 4 * q
                        last = pe.matmul(lists_of[q][:, 0:P], lhsT=hot_hi[:, g % 2, col:col + 4].rearrange("p e h -> p (e h)"),
                                         rhs=hot_lo[:, g % 2, :, col:col + 4].rearrange("p w e l -> p w (e l)"),
                                         start=g == 0 and j == 0, stop=g == 7 and j == GJ - 1)
                last.then_inc(S["s_list"], 1)

            def pe_expert(i, k):
                e = 2 * i + k
                pe.wait_ge(S[f"s_got{k}"], 16 * CC * (i + 1))
                pe.wait_ge(S["s_found"], 4)
                for c in range(CC):
                    last = pe.transpose(fa[0][:, c * P:(c + 1) * P], got[k][:, c, 0:D], ident[:])
                last.then_inc(S["s_xet"], 1)
                pe.wait_ge(S["s_xe"], e + 1)
                pe.wait_ge(S[f"s_fw{k}"], 48 * (i + 1))
                pe.wait_ge(S["s_hT"], FC * e)
                for f in range(FC):
                    pe.matmul([fa[1], fa[2], ba[0], ba[1]][f][:], lhsT=fc1[k][:, f * P:(f + 1) * P], rhs=xe[k][:], start=True, stop=True)\
                      .then_inc(S["s_up"], 1)
                pe.wait_ge(S["s_hT"], FC * e + FC)
                pe.wait_ge(S["s_ys"], e)
                for c in range(CC):
                    for f in range(FC):
                        last = pe.matmul(ba[2][:, c * D:(c + 1) * D], lhsT=hT[k][:, f, c * P:(c + 1) * P], rhs=fc2[k][:, f], start=f == 0, stop=f == FC - 1)
                last.then_inc(S["s_dn"], 1)

            with pe.Fori(0, E1 // 2) as i:
                pe_expert(i, 0)
                pe_expert(i, 1)

        @block.scalar
        def _(act):
            def copy(dst, src, ready, n, done):
                act.wait_ge(S[ready], n)
                act.activation(dst, src, ACT.Copy).then_inc(S[done], 1)

            act.wait_ge(S["s_wfront"], FW)
            act.activation(inv_scaling[:], m_b[:], ACT.Exp, scale=-1.0).then_inc(S["s_scal"], 1)
            act.wait_ge(S["s_scal"], 3)
            act.activation(inv_scaling[:], inv_scaling[:], ACT.Exp, scale=-float(np.log(SEQ))).then_inc(S["s_scal"], 1)

            def front(b):
                copy(f_nT[:], fa[0][:], "s_T1", b + 1, "s_nT1")
                act.wait_ge(S["s_kvqe"], Q * b + Q)
                act.activation(sq[:].rearrange("p q (w d) -> p q w d", w=2), kvq[:].rearrange("p q (w d) -> p q w d", w=3)[:, :, 0:3:2],
                               ACT.Square).then_inc(S["s_sq"], 1)
                copy(qnT[:], fa[0][:], "s_qT", b + 1, "s_qnT")
                copy(kvo[:], fa[1][:, 0:D], "s_kvo", b + 1, "s_kvoc")
                copy(f_nT[:], fa[0][:], "s_T2", b + 1, "s_nT2")
                act.wait_ge(S["s_lgx"], b + 1)
                act.activation(sc[:], lg[:], ACT.Exp).then_inc(S["s_exf"], 1)
                copy(gT[0:PARTS * E0, :], fa[2][:].bitcast(BF16)[0:PARTS * E0, 0:SEQ], "s_gTp", b + 1, "s_gT")

            def back_front(b):
                copy(b_nT[:], ba[0][:], "s_T3", b + 1, "s_nT3")
                act.wait_ge(S["s_qkw"], 32 * b)
                copy(qkp[:, 0, 0], ba[1][:], "s_q", b + 1, "s_p1")
                copy(qkp[:, 1, 0], ba[2][:], "s_k", b + 1, "s_p1")
                copy(vp[:, :, :, 0:HD], ba[0][:].rearrange("p (q h d) -> p q h d", q=Q, h=HEADS), "s_v", b + 1, "s_vp")

            def x_phase(f, b):
                if f is not None:
                    for e in range(U0):
                        act.wait_ge(S["s_h1"], U0 * f + e + 1)
                        if e < 2:
                            act.wait_ge(S["s_h"], U0 * f)
                        else:
                            act.wait_ge(S["s_t"], E0 * f + e - 1)
                        act.activation(sil[:, e % 2], fa[0][:], ACT.Silu).then_inc(S["s_sil"], 1)
                    copy(yT[:], facc[:], "s_ym", U0 * f + U0, "s_yT")

            def y_phase(b):
                copy(nmT[:], bo[:].bitcast(BF16)[0:PARTS * HEADS, 0:SEQ], "s_nmt", b + 1, "s_nmT")
                for n in range(FILLS):
                    pair, f = divmod(n, 5)
                    act.wait_ge(S["s_st"], FILLS * b + n + 1)
                    if f == 0:
                        act.wait_ge(S["s_pv"], 4 * b + max(pair - 1, 0) // 2)
                    act.activation(probs[:, pair % 3, f], ba[n % 3][:], ACT.Exp, scale=SCALE).then_inc(S["s_exp"], 1)
                copy(b_nT[:], bo[:], "s_aTt", b + 1, "s_aT")
                act.wait_ge(S["s_y"], b + 1)
                for q in range(Q):
                    act.activation(b_n[:, q], row[:, q, 0:D], ACT.Square, accum_out=ysq[:, q:q + 1]).then_inc(S["s_ysq"], 1)
                copy(b_nT[:], bo[:], "s_T4", b + 1, "s_nT4")
                act.wait_ge(S["s_l1x"], b + 1)
                act.activation(l1[:], l1[:], ACT.Exp).then_inc(S["s_ex1"], 1)

            looped(act, front, x_phase, back_front, y_phase)
            if debug == "x3":
                return
            act.wait_ge(S["s_prob"], BATCH)
            act.wait_ge(S["s_rowd"], 16 * BATCH)
            copy(LT[:, 512:], fa[1][:], "s_LTt", 1, "s_LTc")
            for q, bank in enumerate([ba[0], ba[1], ba[2], bo]):
                copy(found[:, q].rearrange("p w l -> p (w l)"), bank[:, 0:P], "s_list", 8, "s_found")
            act.wait_ge(S["s_fb"], 16)

            def act_expert(i, k):
                e = 2 * i + k
                act.activation(fb1c[k][:], fb1[:, e], ACT.Copy).then_inc(S["s_bc1"], 1)
                copy(xe[k][:], fa[0][:], "s_xet", e + 1, "s_xe")
                act.wait_ge(S["s_bc1"], e + 1)
                for f in range(FC):
                    act.wait_ge(S["s_up"], FC * e + f + 1)
                    act.activation(hT[k][:, f], [fa[1], fa[2], ba[0], ba[1]][f][:], ACT.Gelu, bias=fb1c[k][:, f:f + 1]).then_inc(S["s_hT"], 1)

            with act.Fori(0, E1 // 2) as i:
                act_expert(i, 0)
                act_expert(i, 1)

        @block.vector
        def _(dve):
            class Steps:

                def __init__(self, name, per_batch):
                    self.sem, self.per, self.n, self.b = S[name], per_batch, 0, 0

                def start(self, b):
                    assert self.n in (0, self.per), self.n
                    self.b, self.n = b, 0

                def __call__(self, ins, wait=True):
                    self.n += 1
                    ins.then_inc(self.sem, 1)
                    if wait:
                        dve.wait_ge(self.sem, self.b * self.per + self.n)
                        apart(dve)

            fc, bc = Steps("s_fc", 32), Steps("s_bc", 26)

            def stats(step, x, st, mv):
                for q in range(Q):
                    step(dve.bn_stats(st[:, q], x[:, q]), q == Q - 1)
                for q in range(Q):
                    step(dve.bn_aggr(mv[:, q], st[:, q]), q == Q - 1)

            def center(dst, x, mv, rs, done):
                for q in range(Q):
                    last = dve.tensor_scalar(dst(q), x[:, q], mv[:, q, 0:1], rs[:, q:q + 1], ALU.subtract, ALU.mult)
                last.then_inc(S[done], 1)

            dve.wait_ge(S["s_wfront"], FW)
            dve.wait_ge(S["s_scal"], 1)
            dve.tensor_scalar(inv_scaling[:], inv_scaling[:], 1.0, None, ALU.add).then_inc(S["s_scal"], 1)
            dve.wait_ge(S["s_scal"], 2)
            dve.reciprocal(inv_scaling[:], inv_scaling[:]).then_inc(S["s_scal"], 1)
            dve.wait_ge(S["s_scal"], 4)
            dve.wait_ge(S["s_one"], 1)
            dve.tensor_tensor(kv_scale[:], blockdiag[:], inv_scaling[:, :, None].to_broadcast([P, HEADS, HD]), ALU.mult).then_inc(S["s_scal"], 1)
            dve.wait_ge(S["s_scal"], 5)

            def front(b):
                fc.start(b)
                dve.wait_ge(S["s_x"], 16 * b + 16)
                stats(fc, xin, f_st, f_mv)
                dve.tensor_scalar(f_ve[:, 0:Q], f_mv[:, :, 1], EPS, None, ALU.add).then_inc(S["s_varf"], 1)
                dve.wait_ge(S["s_rsf"], 3 * b + 1)
                center(lambda q: f_n[:, q], xin, f_mv, f_rs, "s_lnf")
                for q in range(Q):
                    dve.wait_ge(S["s_kvq"], Q * b + q + 1)
                    dve.tensor_tensor(kvq[:, q], fa[(q + 1) % 3][:, 0:3 * D], b_kvq[:], ALU.add).then_inc(S["s_kvqe"], 1)
                dve.wait_ge(S["s_sq"], b + 1)
                fc(dve.tensor_reduce(f_ve[:], sq[:].rearrange("p q (g d) -> p (q g) d", d=HD), X, ALU.add))
                dve.tensor_scalar(f_ve[:], f_ve[:], L2_EPS_SQ, None, ALU.max).then_inc(S["s_varf"], 1)
                dve.wait_ge(S["s_rsf"], 3 * b + 2)
                rs4 = f_rs[:].rearrange("p (q w h) -> p q w h", q=Q, w=2)
                for w in range(2):
                    last = dve.tensor_tensor(kvq[:, :, 2 * w * D:(2 * w + 1) * D].rearrange("p q (h d) -> p q h d", d=HD),
                                             kvq[:, :, 2 * w * D:(2 * w + 1) * D].rearrange("p q (h d) -> p q h d", d=HD),
                                             rs4[:, :, w, :, None].to_broadcast([P, Q, HEADS, HD]), ALU.mult)
                last.then_inc(S["s_kqn"], 1)
                dve.wait_ge(S["s_kvt"], b + 1)
                dve.tensor_tensor(kvm[:], fa[2][:, 0:P], kv_scale[:].rearrange("p h d -> p (h d)"), ALU.mult).then_inc(S["s_kvm"], 1)
                dve.wait_ge(S["s_at0"], b + 1)
                dve.wait_ge(S["s_xres"], b + 1)
                dve.tensor_tensor(x1[:], fa[2][:].rearrange("p (q d) -> p q d", q=Q), xres[:], ALU.add).then_inc(S["s_x1"], 1)
                dve.wait_ge(S["s_x1"], b + 1)
                stats(fc, x1, f_st, f_mv)
                dve.tensor_scalar(f_ve[:, 0:Q], f_mv[:, :, 1], EPS, None, ALU.add).then_inc(S["s_varf"], 1)
                dve.wait_ge(S["s_rsf"], 3 * b + 3)
                center(lambda q: f_n[:, q], x1, f_mv, f_rs, "s_x1n")
                dve.wait_ge(S["s_lgm"], b + 1)
                dve.tensor_copy(lg[:], fa[1][:, 0:Q * E0].rearrange("p (q e) -> p q e", q=Q)).then_inc(S["s_lge"], 1)
                dve.wait_ge(S["s_lge"], b + 1)
                fc(dve.tensor_reduce(lm[:], lg[:], X, ALU.max))
                dve.tensor_tensor(lg[:], lg[:], lm[:, :, None].to_broadcast([P, Q, E0]), ALU.subtract).then_inc(S["s_lgx"], 1)
                dve.wait_ge(S["s_exf"], b + 1)
                fc(dve.tensor_reduce(ls[:], sc[:], X, ALU.add))
                fc(dve.reciprocal(ls[:], ls[:]))
                fc(dve.tensor_tensor(sc[:], sc[:], ls[:, :, None].to_broadcast([P, Q, E0]), ALU.mult))
                fc(dve.tensor_tensor(bs[:], sc[:], gate_b[:, None, :].to_broadcast([P, Q, E0]), ALU.add))
                other = bs[:, :, None, :].to_broadcast([P, Q, E0, E0])
                own = bs[:, :, :, None].to_broadcast([P, Q, E0, E0])
                fc(dve.tensor_tensor(ge[:], other, own, ALU.is_ge), False)
                fc(dve.tensor_tensor(gt[:], other, own, ALU.is_gt))
                fc(dve.tensor_tensor(ge[:], ge[:], below[:, None].to_broadcast([P, Q, E0, E0]), ALU.mult), False)
                fc(dve.tensor_tensor(gt[:], gt[:], above[:, None].to_broadcast([P, Q, E0, E0]), ALU.mult))
                fc(dve.tensor_tensor(ge[:], ge[:], gt[:], ALU.add))
                fc(dve.tensor_reduce(rank[:], ge[:], X, ALU.add))
                fc(dve.scalar_tensor_tensor(gates[:], rank[:], TOPK - 0.5, sc[:], ALU.is_lt, ALU.mult))
                fc(dve.tensor_copy(gparts[:, :, 0], gates[:]))
                fc(dve.tensor_tensor(gres[:], gates[:], gparts[:, :, 0], ALU.subtract))
                fc(dve.tensor_copy(gparts[:, :, 1], gres[:]))
                dve.tensor_tensor(gparts[:, :, 2], gres[:], gparts[:, :, 1], ALU.subtract).then_inc(S["s_gp"], 1)

            def gate_product(b, e, second):
                if not second:
                    dve.wait_ge(S["s_sil"], U0 * b + e + 1)
                    dve.wait_ge(S["s_h3"], U0 * b + e + 1)
                    if e < E0:
                        dve.tensor_tensor(th[:, e % 2], sil[:, e % 2], fa[1][:], ALU.mult).then_inc(S["s_t"], 1)
                        return
                if not second or e < E0:
                    dve.wait_ge(S["s_ym"], U0 * b + max(e - 1, 0))
                    if e < E0:
                        dve.wait_ge(S["s_gb"], E0 * b + e + 1)
                        dve.wait_ge(S["s_t"], E0 * b + e + 1)
                        dve.tensor_tensor(hh[:, e % 2], th[:, e % 2], fa[2][:], ALU.mult).then_inc(S["s_h"], 1)
                    else:
                        dve.tensor_tensor(hh[:, e % 2], sil[:, e % 2], fa[1][:], ALU.mult).then_inc(S["s_h"], 1)

            def maxima(b, n):
                pair, f = divmod(n, 5)
                h, bank = 2 * pair + (f // 2 if f < 4 else 0), ba[n % 3]
                dve.wait_ge(S["s_S"], FILLS * b + n + 1)
                if f in (0, 2):
                    last = dve.tensor_reduce(nm[:, 3, h:h + 1], bank[:], X, ALU.max, negate=True)
                elif f in (1, 3):
                    dve.tensor_reduce(nm[:, 2, h:h + 1], bank[:, 0:384], X, ALU.max, negate=True)
                    last = dve.tensor_reduce(nm[:, 0, h:h + 1], bank[:, 384:512], X, ALU.max, negate=True)
                else:
                    last = dve.tensor_reduce(nm[:, 1, h:h + 2], bank[:].rearrange("p (h k) -> p h k", h=2), X, ALU.max, negate=True)
                last.then_inc(S["s_red"], 1)

            def x_phase(f, b):
                for e in range(U0):
                    if f is not None:
                        gate_product(f, e, False)
                    if b is not None and e < HEADS // 2:
                        maxima(b, 5 * e)
                    if f is not None:
                        gate_product(f, e, True)
                    if b is not None and e < HEADS // 2:
                        for n in range(5 * e + 1, 5 * e + 5):
                            maxima(b, n)
                if b is not None:
                    dve.wait_ge(S["s_red"], FILLS * (b + 1))
                    bc(dve.tensor_copy(nmp[:, :, 0], nm[:]))
                    bc(dve.tensor_tensor(nmr[:], nm[:], nmp[:, :, 0], ALU.subtract))
                    bc(dve.tensor_copy(nmp[:, :, 1], nmr[:]))
                    dve.tensor_tensor(nmp[:, :, 2], nmr[:], nmp[:, :, 1], ALU.subtract).then_inc(S["s_nmp"], 1)
                if f is not None:
                    dve.wait_ge(S["s_yTt"], f + 1)
                    dve.wait_ge(S["s_xb"], f)
                    dve.tensor_tensor(x2[:], fa[0][:].rearrange("p (q d) -> p q d", q=Q), x1[:], ALU.add).then_inc(S["s_x2"], 1)

            def back_front(b):
                bc.start(b)
                dve.wait_ge(S["s_x2"], b + 1)
                stats(bc, x2, b_st, b_mv)
                dve.tensor_scalar(b_ve[:], b_mv[:, :, 1], EPS, None, ALU.add).then_inc(S["s_varb"], 1)
                dve.wait_ge(S["s_rsb"], 3 * b + 1)
                center(lambda q: b_n[:, q], x2, b_mv, b_rs, "s_lnb")
                for w in range(2):
                    dve.wait_ge(S["s_p1"], 2 * b + w + 1)
                    dve.tensor_tensor(qkr[:, w], ba[1 + w][:], qkp[:, w, 0], ALU.subtract).then_inc(S["s_r1"], 1)

            def y_phase(b):
                for k in range(4):
                    dve.wait_ge(S["s_pv"], 4 * b + k + 1)
                    dve.tensor_copy(oT[:], bo[:]).then_inc(S["s_oT"], 1)
                    dve.wait_ge(S["s_tr"], 4 * b + k + 1)
                    o4 = bo[:].rearrange("p (q j r) -> p q j r", q=Q, j=4)
                    bc(dve.reciprocal(rden[:], o4[:, :, :, HD]))
                    dve.tensor_tensor(ao[:, :, 4 * k * HD:4 * (k + 1) * HD].rearrange("p q (j d) -> p q j d", d=HD),
                                      o4[:, :, :, 0:HD], rden[:, :, :, None].to_broadcast([P, Q, 4, HD]), ALU.mult).then_inc(S["s_norm"], 1)
                dve.wait_ge(S["s_wo"], b + 1)
                dve.wait_ge(S["s_xb"], b + 1)
                x3b = x3[:, bass.ts(b, Q)]
                dve.tensor_tensor(x3b, ba[0][:].rearrange("p (q d) -> p q d", q=Q), xb[:], ALU.add).then_inc(S["s_x3"], 1)
                dve.wait_ge(S["s_x3"], b + 1)
                apart(dve)
                stats(bc, x3b, b_st, b_mv)
                dve.tensor_scalar(b_ve[:], b_mv[:, :, 1], EPS, None, ALU.add).then_inc(S["s_varb"], 1)
                dve.wait_ge(S["s_rsb"], 3 * b + 2)
                dve.wait_ge(S["s_rowd"], 16 * b)
                center(lambda q: row[:, q, 0:D], x3b, b_mv, b_rs, "s_y")
                dve.wait_ge(S["s_ysq"], Q * b + Q)
                dve.tensor_scalar(b_ve[:], ysq[:], 1.0 / D, EPS, ALU.mult, ALU.add).then_inc(S["s_varb"], 1)
                dve.wait_ge(S["s_rsb"], 3 * b + 3)
                dve.wait_ge(S["s_y"], b + 1)
                for q in range(Q):
                    last = dve.scalar_tensor_tensor(row[:, q, 0:D], row[:, q, 0:D], b_rs[:, q:q + 1], norm_w[:], ALU.mult, ALU.mult)
                last.then_inc(S["s_row"], 1)
                dve.wait_ge(S["s_l1"], b + 1)
                lb = logits_flat[:, bass.ts(b, Q)]
                dve.tensor_tensor(lb, ba[1][:, 0:Q * E1].rearrange("p (q e) -> p q e", q=Q),
                                  router_b[:, None, :].to_broadcast([P, Q, E1]), ALU.add).then_inc(S["s_l1c"], 1)
                dve.wait_ge(S["s_l1c"], b + 1)
                apart(dve)
                bc(dve.tensor_reduce(l1m[:], lb, X, ALU.max))
                dve.tensor_tensor(l1[:], lb, l1m[:, :, None].to_broadcast([P, Q, E1]), ALU.subtract).then_inc(S["s_l1x"], 1)
                dve.wait_ge(S["s_ex1"], b + 1)
                bc(dve.tensor_reduce(l1m[:], l1[:], X, ALU.add))
                bc(dve.reciprocal(l1m[:], l1m[:]))
                dve.tensor_tensor(row[:, :, D:], l1[:], l1m[:, :, None].to_broadcast([P, Q, E1]), ALU.mult).then_inc(S["s_prob"], 1)

            looped(dve, front, x_phase, back_front, y_phase)
            if debug == "x3":
                return
            dve.wait_ge(S["s_prob"], BATCH)
            dve.wait_ge(S["s_rowd"], 16 * BATCH)
            dve.tensor_copy(logits_gj[:].rearrange("p g (j e) -> p g j e", j=GJ),
                            logits_flat[:].rearrange("p (j g) e -> p g j e", g=8)).then_inc(S["s_gj"], 1)
            dve.wait_ge(S["s_LTt"], 1)
            dve.tensor_copy(LT[:, 0:512], fa[0][:]).then_inc(S["s_LTc"], 1)
            dve.wait_ge(S["s_LTc"], 2)
            dve.wait_ge(S["s_ec"], 5)
            sr = Steps("s_sr", 5)
            TOP = -2 ** 31

            def as_float(step, src):
                step(dve.tensor_scalar(flip[:], src[:], 31, -1, ALU.arith_shift_right, ALU.bitwise_xor))
                step(dve.scalar_tensor_tensor(bits[:], flip[:], TOP, src[:], ALU.bitwise_or, ALU.bitwise_xor))

            with dve.Fori(0, 32) as i:
                sr.start(i)
                sr(dve.tensor_tensor(cand[:], key[:], bit[:], ALU.bitwise_or))
                as_float(sr, cand)
                dve.tensor_scalar(above_t[:], LT[:], bits[:].bitcast(F32), None, ALU.is_ge, ALU.add, accum_out=cnt[:]).then_inc(S["s_cnt"], 1)
                dve.wait_ge(S["s_tot"], i + 1)
                sr(dve.tensor_scalar(okm[:], fa[2][:, 0:1], CAP - 0.5, -1.0, ALU.is_ge, ALU.mult))
                sr(dve.scalar_tensor_tensor(key[:], okm[:], bit[:], key[:], ALU.bitwise_and, ALU.bitwise_or))
                dve.tensor_scalar(bit[:], bit[:], 1, None, ALU.logical_shift_right).then_inc(S["s_bit"], 1)
                dve.wait_ge(S["s_bit"], i + 1)
            ec = Steps("s_eqt", 10)
            as_float(ec, key)
            thr = bits[:].bitcast(F32)
            dve.tensor_scalar(above_t[:], LT[:], thr, None, ALU.is_gt, ALU.add, accum_out=cnt[:]).then_inc(S["s_gtc"], 1)
            ec(dve.tensor_scalar(equal_t[:], LT[:], thr, None, ALU.is_equal, ALU.add, accum_out=off_eq[:]))
            dve.wait_ge(S["s_gtt"], 1)
            ec(dve.tensor_scalar(more[:], fa[2][:, 0:1], -1.0, float(CAP), ALU.mult, ALU.add))
            dve.tensor_copy(cnt[:], off_eq[:]).then_inc(S["s_gtc"], 1)
            dve.wait_ge(S["s_gtt"], 2)
            ec(dve.tensor_copy(off_eq[:], fa[2][:, 0:1]))
            ec(dve.tensor_tensor_scan(place[:], ones[:], equal_t[:], off_eq[:], ALU.mult, ALU.add))
            ec(dve.scalar_tensor_tensor(equal_t[:], place[:], more[:], equal_t[:], ALU.is_le, ALU.mult))
            dve.scalar_tensor_tensor(chosen[:], above_t[:], 0.0, equal_t[:], ALU.add, ALU.add, accum_out=cnt[:]).then_inc(S["s_gtc"], 1)
            dve.wait_ge(S["s_gtt"], 3)
            ec(dve.tensor_copy(off_sel[:], fa[2][:, 0:1]))
            ec(dve.tensor_tensor_scan(place[:], ones[:], chosen[:], off_sel[:], ALU.mult, ALU.add))
            dve.tensor_tensor(place[:], place[:], chosen[:], ALU.mult).then_inc(S["s_rc"], 1)
            dve.wait_ge(S["s_slT"], 1)
            sl = Steps("s_slot", 6)
            for half in range(2):
                sl(dve.tensor_scalar(slot[:, 4 * half:4 * half + 4].rearrange("p g c -> p (g c)"), fa[half][:], -1.0, None, ALU.add), half == 1)
            sl(dve.tensor_scalar(hi_i[:], slot[:], 4, None, ALU.arith_shift_right), False)
            sl(dve.tensor_scalar(lo_i[:], slot[:], 15, None, ALU.bitwise_and))
            sl(dve.tensor_copy(hi[:], hi_i[:]), False)
            sl(dve.tensor_copy(lo[:], lo_i[:]))
            hs = Steps("s_rc2", 8)
            for g in range(8):
                if g >= 2:
                    dve.wait_ge(S["s_list"], g - 1)
                    dve.wait_ge(S["s_hot"], g - 1)
                dve.tensor_tensor(hot_hi[:, g % 2], hi[:, g, :, None].to_broadcast([P, P, 32]), iota32[:, None, :].to_broadcast([P, P, 32]), ALU.is_equal)
                hs(dve.tensor_tensor(hot[:, g % 2], lo[:, g, :, None].to_broadcast([P, P, 16]), iota16[:, None, :].to_broadcast([P, P, 16]), ALU.is_equal))
                dve.tensor_scalar(hot_lo[:, g % 2, 0], hot[:, g % 2], pcol[:], None, ALU.mult)
                dve.tensor_tensor(hot_lo[:, g % 2, 1].rearrange("p (j e) l -> p j (e l)", j=GJ), hot[:, g % 2].rearrange("p (j e) l -> p j (e l)", j=GJ),
                                  tcol[:, g, :, None].to_broadcast([P, GJ, E1 * 16]), ALU.mult).then_inc(S["s_hot"], 1)
            dve.wait_ge(S["s_found"], 4)
            for q in range(4):
                for j in range(4):
                    r = slice(32 * j, 32 * j + 32)
                    dve.scalar_tensor_tensor(idx[r, q], found[r, q, 1, 16 * j:16 * j + 16], float(P), found[r, q, 0, 16 * j:16 * j + 16],
                                             ALU.mult, ALU.add).then_inc(S["s_idx"], 1)

            def current(i, k):
                if not (isinstance(i, int) and i == 0):
                    dve.wait_ge(S["s_sc"], 16 * CC * (2 * i + k - 1))
                dve.tensor_copy(cur[k][:], idx_pc[:, 2 * i + k]).then_inc(S["s_cur"], 1)

            def dve_expert(i, k, more_rows=True):
                e = 2 * i + k
                dve.wait_ge(S[f"s_got{k}"], 16 * CC * (i + 1))
                dve.tensor_copy(gate[k][:], got[k][:, :, D + e]).then_inc(S["s_gatec"], 1)
                dve.wait_ge(S["s_dn"], e + 1)
                dve.wait_ge(S[f"s_fw{k}"], 48 * (i + 1))
                dve.tensor_tensor(ysum[k][:], ba[2][:].rearrange("p (c d) -> p c d", c=CC), fb2[k][:, None, :].to_broadcast([P, CC, D]), ALU.add)\
                   .then_inc(S["s_ys"], 1)
                dve.wait_ge(S["s_ys"], e + 1)
                dve.wait_ge(S["s_gatec"], e + 1)
                if not isinstance(i, int) or i > 0 or k > 0:
                    pass
                dve.tensor_tensor(contrib[k][:, :, 0:D], ysum[k][:], gate[k][:, :, None].to_broadcast([P, CC, D]), ALU.mult)
                dve.tensor_copy(contrib[k][:, :, D], gate[k][:]).then_inc(S["s_con"], 1)

            dve.wait_ge(S["s_ldr"], 16)
            current(0, 0)
            current(0, 1)
            with dve.Fori(0, E1 // 2 - 1) as i:
                dve_expert(i, 0)
                current(i + 1, 0)
                dve_expert(i, 1)
                current(i + 1, 1)
            dve_expert(E1 // 2 - 1, 0)
            dve_expert(E1 // 2 - 1, 1)
            fs = Steps("s_fs", 8)
            n = TILES // 4
            for k in range(4):
                dve.wait_ge(S[f"s_sum{k}"], 16)
                t = slice(k * n, (k + 1) * n)
                fs(dve.scalar_tensor_tensor(gsum[:, t], sums[:, t, D], 0.0, sums[:, t, D], ALU.is_le, ALU.add))
                fs(dve.reciprocal(gsum[:, t], gsum[:, t]))
                for m in range(k * n, (k + 1) * n):
                    last = dve.scalar_tensor_tensor(x3[:, m], sums[:, m, 0:D], gsum[:, m:m + 1], x3[:, m], ALU.mult, ALU.add)
                last.then_inc(S["s_fin"], 1)


def layout(i):
    i = {n: np.asarray(v) for n, v in i.items()}
    o = dict(i)
    o["L0_ffn_gate_w"] = i["L0_ffn_gate_w"].T
    for n in ("Wq", "Wk", "Wv", "Wo"):
        o["L1_attn_" + n] = i["L1_attn_" + n].T
    for n in ("w1", "w3"):
        routed = i["L0_ffn_" + n].transpose(2, 0, 1)
        shared = i["L0_ffn_s" + n].reshape(SHARED, P, D).transpose(2, 0, 1)
        o["L0_" + n] = np.concatenate([routed, shared], axis=1)
        del o["L0_ffn_" + n], o["L0_ffn_s" + n]
    routed = i["L0_ffn_w2"].transpose(2, 0, 1)
    shared = i["L0_ffn_sw2"].T.reshape(SHARED, P, D).transpose(1, 0, 2)
    o["L0_w2"] = np.concatenate([routed, shared], axis=1)
    del o["L0_ffn_w2"], o["L0_ffn_sw2"]
    o["L1_ffn_router_weight"] = i["L1_ffn_router_weight"].T
    o["L1_ffn_fc1_weight"] = i["L1_ffn_fc1_weight"].transpose(2, 0, 1)
    o["L1_ffn_fc1_bias"] = i["L1_ffn_fc1_bias"].reshape(E1, FC, P).transpose(2, 0, 1)
    o["L1_ffn_fc2_weight"] = i["L1_ffn_fc2_weight"].reshape(E1, D, FC, P).transpose(3, 0, 2, 1)
    return {n: np.ascontiguousarray(v) for n, v in o.items()}


def kernel(**inputs):
    import concourse.bacc as bacc
    from concourse.bass_utils import run_bass_kernel_spmd

    nc = bacc.Bacc("TRN2", target_bir_lowering=False, num_devices=1)
    arrays = layout(inputs)
    a = {n: nc.dram_tensor("in_" + n, v.shape, mybir.dt.from_np(v.dtype), kind="ExternalInput").ap() for n, v in arrays.items()}
    out = nc.dram_tensor("out", (BATCH, SEQ, D), F32, kind="ExternalOutput").ap()
    build_kernel(nc, a, out)
    r = run_bass_kernel_spmd(nc, [{"in_" + n: v for n, v in arrays.items()}], core_ids=[0])
    return r.results[0]["out"]
```

```python
import numpy as np
import concourse.bass as bass
import concourse.mybir as mybir
from contextlib import ExitStack

F32, BF16, I32 = mybir.dt.float32, mybir.dt.bfloat16, mybir.dt.int32
ALU = mybir.AluOpType
ACT = mybir.ActivationFunctionType
X = mybir.AxisListType.X

P = 128
BATCH, SEQ, D = 16, 512, 128
Q = SEQ // P
TOK = BATCH * SEQ
TILES = TOK // P
HEADS, HD = 16, 8
E0, TOPK, SHARED = 8, 2, 2
U0 = E0 + SHARED
E1, FF = 16, 512
CAP = TOK // E1
FC = FF // P
CC = CAP // P
EPS = 1e-5
L2_EPS_SQ = 1e-24
SCALE = float(1.0 / np.sqrt(HD))
MASKED = -1.0e38
PARTS = 3
QK_ROWS = PARTS * PARTS * HD
MX_ROW = QK_ROWS
K_ROWS = QK_ROWS + PARTS
FILLS = HEADS // 2 * 5
ROW = D + E1
CROW = D + 4
GJ = TILES // 8


def build_kernel(nc, a, out, debug=None):
    ctx = ExitStack()
    with ctx:
        def sb(name, shape, dt=F32):
            return ctx.enter_context(nc.sbuf_tensor(name, shape, dt))

        early = ExitStack()

        def sb1(name, shape, dt=F32):
            return early.enter_context(nc.sbuf_tensor(name, shape, dt))

        def sem(name):
            return ctx.enter_context(nc.semaphore(name))

        qk_parts = nc.dram_tensor("qk_parts", (BATCH, 2, PARTS, P, SEQ), BF16, kind="Internal").ap()
        xn_rows = nc.dram_tensor("xn_rows", (TOK, ROW), F32, kind="Internal").ap()
        sum_rows = nc.dram_tensor("sum_rows", (TOK, CROW), F32, kind="Internal").ap()
        lists = nc.dram_tensor("lists", (E1, CAP), I32, kind="Internal").ap()

        fa = [ctx.enter_context(nc.psum_tensor(f"fa{i}", [P, 512], F32)) for i in range(3)]
        facc = ctx.enter_context(nc.psum_tensor("facc", [P, 512], F32))
        ba = [ctx.enter_context(nc.psum_tensor(f"ba{i}", [P, 512], F32)) for i in range(3)]
        bo = ctx.enter_context(nc.psum_tensor("bo", [P, 512], F32))

        ident = sb("ident", [P, P])
        zrow = sb("zrow", [P, CROW])
        identb = sb("identb", [P, P], BF16)
        mask_q = sb("mask_q", [P, P], BF16)
        mask_k = sb("mask_k", [P, P], BF16)
        pick = sb("pick", [P, E0, P], BF16)
        blockdiag = sb("blockdiag", [P, HEADS, HD])
        below = sb("below", [P, E0, E0])
        above = sb("above", [P, E0, E0])
        same_e = sb("same_e", [P, P])
        earlier_e = sb("earlier_e", [P, P])
        mhalf = sb("mhalf", [P, P])
        iota32 = sb("iota32", [P, 32])
        iota16 = sb("iota16", [P, 16])
        pcol = sb("pcol", [P, 1])
        tcol = sb("tcol", [P, 8, GJ])
        x3 = sb("x3", [P, TILES, D])
        logits_flat = sb("logits", [P, TILES, E1])
        w_kvq = sb1("w_kvq", [P, 3 * D])
        b_kvq = sb1("b_kvq", [P, 3 * D])
        w_o0 = sb1("w_o0", [P, D])
        b_o0 = sb1("b_o0", [P, D])
        m_b = sb1("m_b", [P, HEADS])
        inv_scaling = sb1("inv_scaling", [P, HEADS])
        kv_scale = sb1("kv_scale", [P, HEADS, HD])
        gate_w = sb1("gate_w", [P, E0])
        gate_b = sb1("gate_b", [P, E0])
        w1 = sb1("w1", [P, U0, P])
        w3 = sb1("w3", [P, U0, P])
        w2 = sb1("w2", [P, U0, P])
        w_q1 = sb1("w_q1", [P, D])
        w_k1 = sb1("w_k1", [P, D])
        w_v1 = sb1("w_v1", [P, D])
        w_o1 = sb1("w_o1", [P, D])
        norm_w = sb1("norm_w", [P, D])
        router_w = sb1("router_w", [P, E1])
        router_b = sb1("router_b", [P, E1])
        xin = sb1("xin", [P, Q, D])
        xres = sb1("xres", [P, Q, D])
        f_st = sb1("f_st", [P, Q, 6])
        f_mv = sb1("f_mv", [P, Q, 2])
        f_ve = sb1("f_ve", [P, Q])
        f_rs = sb1("f_rs", [P, Q])
        n2 = sb1("n2", [P, P])
        rn = sb1("rn", [P, P])
        rt = sb1("rt", [P, P])
        f_n = sb1("f_n", [P, Q, D])
        f_nT = sb1("f_nT", [P, SEQ])
        kvq = sb1("kvq", [P, Q, 3 * D])
        sq = sb1("sq", [P, Q, 2 * D])
        qnT = sb1("qnT", [P, SEQ])
        kvm = sb1("kvm", [P, P])
        kvo = sb1("kvo", [P, P])
        x1 = sb1("x1", [P, Q, D])
        lg = sb1("lg", [P, Q, E0])
        lm = sb1("lm", [P, Q])
        ls = sb1("ls", [P, Q])
        sc = sb1("sc", [P, Q, E0])
        bs = sb1("bs", [P, Q, E0])
        ge = sb1("ge", [P, Q, E0, E0])
        gt = sb1("gt", [P, Q, E0, E0])
        rank = sb1("rank", [P, Q, E0])
        gates = sb1("gates", [P, Q, E0])
        gres = sb1("gres", [P, Q, E0])
        gparts = sb1("gparts", [P, Q, PARTS, E0], BF16)
        gT = sb1("gT", [P, SEQ], BF16)
        sil = sb1("sil", [P, 2, SEQ])
        th = sb1("th", [P, 2, SEQ])
        hh = sb1("hh", [P, 2, SEQ])
        yT = sb1("yT", [P, SEQ])
        b_st = sb1("b_st", [P, Q, 6])
        b_mv = sb1("b_mv", [P, Q, 2])
        b_ve = sb1("b_ve", [P, Q])
        b_rs = sb1("b_rs", [P, Q])
        b_n = sb1("b_n", [P, Q, D])
        b_nT = sb1("b_nT", [P, SEQ])
        qkp = sb1("qkp", [P, 2, PARTS, SEQ], BF16)
        qkr = sb1("qkr", [P, 2, SEQ])
        vp = sb1("vp", [P, Q, HEADS, 32])
        QT = sb1("QT", [P, HEADS, SEQ], BF16)
        KT = sb1("KT", [P, HEADS, SEQ], BF16)
        nm = sb1("nm", [P, Q, HEADS])
        nmr = sb1("nmr", [P, Q, HEADS])
        nmp = sb1("nmp", [P, Q, PARTS, HEADS], BF16)
        nmT = sb1("nmT", [PARTS * HEADS, SEQ], BF16)
        probs = sb1("probs", [P, 3, 5, SEQ])
        oT = sb1("oT", [P, SEQ])
        rden = sb1("rden", [P, Q, 4])
        ao = sb1("ao", [P, Q, D])
        row = sb1("row", [P, Q, ROW])
        l1 = sb1("l1", [P, Q, E1])
        ysq = sb1("ysq", [P, Q])
        l1m = sb1("l1m", [P, Q])

        early.close()
        ones = sb("ones", [P, TOK // 8])
        LT = sb("LT", [P, TOK // 8])
        above_t = sb("above_t", [P, TOK // 8])
        equal_t = sb("equal_t", [P, TOK // 8])
        place = sb("place", [P, TOK // 8])
        chosen = sb("chosen", [P, TOK // 8])
        key, cand, flip, bits, bit, okm = (sb(n, [P, 1], I32) for n in ("key", "cand", "flip", "bits", "bit", "okm"))
        cnt, more, off_eq, off_sel = (sb(n, [P, 1]) for n in ("cnt", "more", "off_eq", "off_sel"))
        slot = sb("slot", [P, 8, P], I32)
        hi_i, lo_i = sb("hi_i", [P, 8, P], I32), sb("lo_i", [P, 8, P], I32)
        hi, lo = sb("hi", [P, 8, P], BF16), sb("lo", [P, 8, P], BF16)
        hot_hi = sb("hot_hi", [P, 2, P, 32], BF16)
        hot_lo = sb("hot_lo", [P, 2, 2, P, 16], BF16)
        hot = sb("hot", [P, 2, P, 16], BF16)
        found = sb("found", [P, 4, 2, 64])
        idx = sb("idx", [P, 4, 16], I32)
        idx_pc = sb("idx_pc", [P, E1, CC], I32)
        cur = [sb(f"cur{i}", [P, CC], I32) for i in range(2)]
        got = [sb(f"got{i}", [P, CC, ROW]) for i in range(2)]
        gate = [sb(f"gate{i}", [P, CC]) for i in range(2)]
        xe = [sb(f"xe{i}", [P, CAP]) for i in range(2)]
        fc1 = [sb(f"fc1_{i}", [P, FF]) for i in range(2)]
        fc2 = [sb(f"fc2_{i}", [P, FC, D]) for i in range(2)]
        fb2 = [sb(f"fb2_{i}", [P, D]) for i in range(2)]
        fb1 = sb("fb1", [P, E1, FC])
        fb1c = [sb(f"fb1c{i}", [P, FC]) for i in range(2)]
        hT = [sb(f"hT{i}", [P, FC, CAP]) for i in range(2)]
        ysum = [sb(f"ysum{i}", [P, CC, D]) for i in range(2)]
        contrib = [sb(f"contrib{i}", [P, CC, CROW]) for i in range(2)]
        sums = sb("sums", [P, TILES, CROW])
        gsum = sb("gsum", [P, TILES])
        logits_gj = sb("logits_gj", [P, 8, P])

        names = """s_wfront s_wback s_cst s_one s_scal s_x s_lnf s_xres s_varf s_rsf s_T1 s_nT1 s_kvq s_kvqe s_sq
            s_kqn s_kvt s_kvm s_qT s_qnT s_kvo s_kvoc s_at0 s_x1 s_x1n s_T2 s_nT2 s_lgm s_lge s_exf s_lgx s_gp s_gTp s_gT
            s_h1 s_h3 s_gb s_sil s_t s_h s_ym s_yT s_yTt s_x2 s_fc
            s_lnb s_xb s_varb s_rsb s_T3 s_nT3 s_q s_k s_v s_p1 s_r1 s_p2 s_p3 s_vp s_qkw s_qk s_S s_red s_nmp s_nmt
            s_nmT s_mx s_st s_exp s_pv s_oT s_tr s_norm s_aTt s_aT s_wo s_x3 s_y s_ysq s_row s_T4 s_nT4 s_l1 s_l1c
            s_l1x s_ex1 s_prob s_rowd s_bc s_zero
            s_vart s_rst s_rc1 s_tc s_rden s_LTt s_LTc s_cnt s_tot s_sr s_gtc s_gtt s_eqt s_selt s_rc s_slT s_slot s_hot s_list s_bit s_rc2 s_gatec s_fs s_gj s_found s_idx s_bc1 s_ldw s_ldr
            s_cur s_got0 s_got1 s_xet s_xe s_fw0 s_fw1 s_up s_hT s_dn s_ys s_con s_sc s_ec s_sum0 s_sum1 s_sum2 s_sum3 s_fin s_out s_fb""".split()
        S = {n: sem(n) for n in names}
        block = ctx.enter_context(nc.Block())
        FW = 16 * 15
        BW = 16 * 6

        def apart(eng):
            eng.nop(nofuse=True)

        def bcast_rows(v, n):
            return v.rearrange("(o n) -> o n", o=1)[0].partition_broadcast(P)

        def looped(engine, x_phase, y_phase):
            y_phase(None, 0, None, None)
            x_phase(0, None, None)
            y_phase(None, 1, 0, None)
            x_phase(1, 0, None)
            y_phase(0, 2, 1, None)
            with engine.Fori(1, BATCH - 2) as i:
                x_phase(i + 1, i, i - 1)
                y_phase(i, i + 2, i + 1, i - 1)
            n = BATCH - 1
            x_phase(n, n - 1, n - 2)
            y_phase(n - 1, None, n, n - 2)
            x_phase(None, n, n - 1)
            y_phase(n, None, None, n - 1)
            x_phase(None, None, n)
            y_phase(None, None, None, n)

        @block.sync
        def _(sp):
            for dst, src in (
                (w_kvq[:, 0:D], a["L0_attn_Wk"]), (w_kvq[:, D:2 * D], a["L0_attn_Wv"]), (w_kvq[:, 2 * D:], a["L0_attn_Wq"]),
                (b_kvq[:, 0:D], bcast_rows(a["L0_attn_bk"], D)), (b_kvq[:, D:2 * D], bcast_rows(a["L0_attn_bv"], D)),
                (b_kvq[:, 2 * D:], bcast_rows(a["L0_attn_bq"], D)),
                (w_o0[:], a["L0_attn_Wo"]), (b_o0[:], bcast_rows(a["L0_attn_bo"], D)), (m_b[:], bcast_rows(a["L0_attn_m"], HEADS)),
                (gate_w[:], a["L0_ffn_gate_w"]), (gate_b[:], bcast_rows(a["L0_ffn_gate_bias"], E0)),
            ):
                sp.dma_start(dst, src).then_inc(S["s_wfront"], 16)
            sp.dma_start(xin[:], a["L0_attn_x"][0].rearrange("(q p) d -> p q d", p=P)).then_inc(S["s_x"], 16)
            for dst, src in ((w1, "w1"), (w3, "w3"), (w2, "w2")):
                sp.dma_start(dst[:], a["L0_" + src]).then_inc(S["s_wfront"], 16)
            sp.dma_start(norm_w[:], bcast_rows(a["L1_ffn_norm_weight"], D)).then_inc(S["s_wfront"], 16)
            for dst, name in ((w_q1, "L1_attn_Wq"), (w_k1, "L1_attn_Wk"), (w_v1, "L1_attn_Wv"), (w_o1, "L1_attn_Wo"),
                              (router_w, "L1_ffn_router_weight")):
                sp.dma_start(dst[:], a[name]).then_inc(S["s_wback"], 16)
            sp.dma_start(router_b[:], bcast_rows(a["L1_ffn_router_bias"], E1)).then_inc(S["s_wback"], 16)
            sp.wait_ge(S["s_cst"], 1)
            sp.dma_start(sum_rows.rearrange("(t p) c -> p t c", p=P),
                         zrow[:, None, :].to_broadcast([P, TILES, CROW])).then_inc(S["s_zero"], 16)

            def back_dmas(b):
                for w in range(2):
                    sp.wait_ge(S["s_p3"], 2 * b + w + 1)
                    apart(sp)
                    sp.dma_start(qk_parts[b, w].rearrange("c p t -> p c t"), qkp[:, w]).then_inc(S["s_qkw"], 16)
                sp.wait_ge(S["s_qkw"], 32 * b + 32)
                apart(sp)
                sp.wait_ge(S["s_st"], FILLS * b)
                apart(sp)
                for i in range(PARTS):
                    for j in range(PARTS):
                        r = (i * PARTS + j) * HD
                        sp.dma_start(QT[r:r + HD], qk_parts[b, 0, i].rearrange("(h d) t -> d h t", d=HD)).then_inc(S["s_qk"], 16)
                        sp.dma_start(KT[r:r + HD], qk_parts[b, 1, j].rearrange("(h d) t -> d h t", d=HD)).then_inc(S["s_qk"], 16)

            def max_dmas(b):
                sp.wait_ge(S["s_nmT"], b + 1)
                apart(sp)
                for c in range(PARTS):
                    sp.dma_start(QT[MX_ROW + c:MX_ROW + c + 1], nmT[c * HEADS:(c + 1) * HEADS, :]).then_inc(S["s_mx"], 16)

            def row_dmas(b):
                sp.wait_ge(S["s_prob"], b + 1)
                apart(sp)
                sp.dma_start(xn_rows[bass.ts(b, SEQ)].rearrange("(q p) c -> p q c", p=P), row[:]).then_inc(S["s_rowd"], 16)

            def load_x(b):
                sp.wait_ge(S["s_lnf"], b)
                sp.wait_ge(S["s_xres"], b)
                apart(sp)
                sp.dma_start(xin[:], a["L0_attn_x"][b].rearrange("(q p) d -> p q d", p=P)).then_inc(S["s_x"], 16)

            load_x(1)
            back_dmas(0)
            load_x(2)
            max_dmas(0)
            back_dmas(1)
            with sp.Fori(1, BATCH - 2) as i:
                load_x(i + 2)
                max_dmas(i)
                row_dmas(i - 1)
                back_dmas(i + 1)
            n = BATCH - 1
            max_dmas(n - 1)
            row_dmas(n - 2)
            back_dmas(n)
            max_dmas(n)
            row_dmas(n - 1)
            row_dmas(n)
            sp.wait_ge(S["s_rowd"], 16 * BATCH)
            if debug == "x3":
                sp.dma_start(out.rearrange("b (q p) d -> p (b q) d", p=P), x3[:]).then_inc(S["s_zero"], 16)
                sp.wait_ge(S["s_zero"], 32)
                return

            sp.wait_ge(S["s_prob"], BATCH)
            sp.dma_start(fb1[:], a["L1_ffn_fc1_bias"]).then_inc(S["s_fb"], 16)
            sp.wait_ge(S["s_idx"], 16)
            sp.dma_start(lists.rearrange("(g e) (h l) -> (e h) g l", g=4, l=16), idx[:]).then_inc(S["s_ldw"], 16)
            sp.wait_ge(S["s_ldw"], 16)
            sp.dma_start(idx_pc[:], lists.rearrange("e (p c) -> p e c", c=CC)).then_inc(S["s_ldr"], 16)
            with sp.Fori(0, E1 // 2) as i:
                for k in range(2):
                    sp.wait_ge(S["s_ys"], 2 * i + max(k - 1, 0))
                    apart(sp)
                    sp.dma_start(fc1[k][:], a["L1_ffn_fc1_weight"][:, 2 * i + k]).then_inc(S[f"s_fw{k}"], 16)
                    sp.dma_start(fc2[k][:], a["L1_ffn_fc2_weight"][:, 2 * i + k]).then_inc(S[f"s_fw{k}"], 16)
                    sp.dma_start(fb2[k][:], a["L1_ffn_fc2_bias"][2 * i + k].partition_broadcast(P)).then_inc(S[f"s_fw{k}"], 16)
            sp.wait_ge(S["s_sc"], 16 * CC * E1)
            n = TILES // 4
            rows = sum_rows.rearrange("(t p) c -> p t c", p=P)
            for k in range(4):
                sp.dma_start(sums[:, k * n:(k + 1) * n], rows[:, k * n:(k + 1) * n]).then_inc(S[f"s_sum{k}"], 16)
            for k in range(4):
                sp.wait_ge(S["s_fin"], k + 1)
                sp.dma_start(out.rearrange("b (q p) d -> p (b q) d", p=P)[:, k * n:(k + 1) * n], x3[:, k * n:(k + 1) * n]).then_inc(S["s_out"], 16)
            sp.wait_ge(S["s_out"], 64)

        @block.gpsimd
        def _(pool):
            c = [1]

            def const(ins):
                c[0] += 1
                ins.then_inc(S["s_cst"], 1)
                pool.wait_ge(S["s_cst"], c[0])

            pool.memset(zrow[:], 0.0).then_inc(S["s_cst"], 1)
            pool.wait_ge(S["s_cst"], 1)
            for t in (ident, identb):
                const(pool.memset(t[:], 0.0))
                const(pool.affine_select(t[:], t[:], [[-1, P]], ALU.not_equal, 1.0, base=0, channel_multiplier=1))
            const(pool.memset(mask_q[:], 0.0))
            const(pool.affine_select(mask_q[:], mask_q[:], [[-1, P]], ALU.is_ge, MASKED, base=0, channel_multiplier=1))
            const(pool.memset(mask_k[:], 0.0))
            const(pool.affine_select(mask_k[:], mask_k[:], [[1, P]], ALU.is_ge, MASKED, base=0, channel_multiplier=-1))
            const(pool.memset(pick[:], 0.0))
            for part in range(PARTS):
                const(pool.affine_select(pick[:], pick[:], [[-1, E0], [0, P]], ALU.not_equal, 1.0, base=-E0 * part, channel_multiplier=1))
            const(pool.memset(blockdiag[:], 1.0))
            const(pool.affine_select(blockdiag[:], blockdiag[:], [[-HD, HEADS], [0, HD]], ALU.is_ge, 0.0, base=0, channel_multiplier=1))
            const(pool.affine_select(blockdiag[:], blockdiag[:], [[HD, HEADS], [0, HD]], ALU.is_ge, 0.0, base=HD - 1, channel_multiplier=-1))
            const(pool.memset(below[:], 1.0))
            const(pool.affine_select(below[:], below[:], [[1, E0], [-1, E0]], ALU.is_ge, 0.0, base=-1, channel_multiplier=0))
            const(pool.memset(above[:], 1.0))
            const(pool.affine_select(above[:], above[:], [[-1, E0], [1, E0]], ALU.is_ge, 0.0, base=-1, channel_multiplier=0))
            for m in range(-7, 8):
                if m == -7:
                    const(pool.memset(same_e[:], 0.0))
                    const(pool.memset(earlier_e[:], 0.0))
                const(pool.affine_select(same_e[:], same_e[:], [[-1, P]], ALU.not_equal, 1.0, base=E1 * m, channel_multiplier=1))
                if m > 0:
                    const(pool.affine_select(earlier_e[:], earlier_e[:], [[-1, P]], ALU.not_equal, 1.0, base=E1 * m, channel_multiplier=1))
            const(pool.iota(iota32[:], [[1, 32]], base=0, channel_multiplier=0, allow_small_or_imprecise_dtypes=True))
            const(pool.iota(iota16[:], [[1, 16]], base=0, channel_multiplier=0, allow_small_or_imprecise_dtypes=True))
            const(pool.iota(pcol[:], [[1, 1]], base=0, channel_multiplier=1, allow_small_or_imprecise_dtypes=True))
            const(pool.iota(tcol[:], [[1, 8], [8, GJ]], base=0, channel_multiplier=0, allow_small_or_imprecise_dtypes=True))
            const(pool.memset(mhalf[:], -0.5))
            const(pool.memset(gT[:], 0.0))
            const(pool.memset(KT[64:96], 1.0))
            const(pool.memset(vp[:], 0.0))
            const(pool.memset(vp[:, :, :, HD:HD + 1], 1.0))
            pool.memset(nmT[:], 0.0).then_inc(S["s_one"], 1)

            def power(dst, src, ready, done, count):
                pool.wait_ge(S[ready], count)
                pool.tensor_tensor(dst, src, mhalf[:, 0:src.shape[-1]], ALU.pow).then_inc(S[done], 1)

            def x_phase(f, b, t):
                if t is not None:
                    power(b_rs[:], b_ve[:], "s_vart", "s_rst", 2 * t + 1)
                    power(b_rs[:], b_ve[:], "s_vart", "s_rst", 2 * t + 2)

            def y_phase(b, f, r, t):
                if r is not None:
                    power(b_rs[:], b_ve[:], "s_varb", "s_rsb", r + 1)
                if f is not None:
                    power(f_rs[:, 0:Q], f_ve[:, 0:Q], "s_varf", "s_rsf", 2 * f + 1)
                    pool.wait_ge(S["s_x"], 16 * f + 16)
                    pool.wait_ge(S["s_wfront"], FW)
                    pool.wait_ge(S["s_x1"], f)
                    pool.tensor_tensor(xres[:], xin[:], b_o0[:, None, :].to_broadcast([P, Q, D]), ALU.add).then_inc(S["s_xres"], 1)
                if r is not None:
                    for w in range(2):
                        pool.wait_ge(S["s_r1"], 2 * r + w + 1)
                        apart(pool)
                        pool.tensor_copy(qkp[:, w, 1], qkr[:, w]).then_inc(S["s_p2"], 1)
                        pool.wait_ge(S["s_p2"], 2 * r + w + 1)
                        pool.tensor_tensor(qkp[:, w, 2], qkr[:, w], qkp[:, w, 1], ALU.subtract).then_inc(S["s_p3"], 1)
                if f is not None:
                    power(f_rs[:, 0:Q], f_ve[:, 0:Q], "s_varf", "s_rsf", 2 * f + 2)

            looped(pool, x_phase, y_phase)
            if debug == "x3":
                return
            pool.wait_ge(S["s_prob"], BATCH)
            pool.wait_ge(S["s_rowd"], 16 * BATCH)
            pool.memset(ones[:], 1.0).then_inc(S["s_ec"], 1)
            pool.memset(key[:], 0).then_inc(S["s_ec"], 1)
            pool.memset(bit[:], -2 ** 31).then_inc(S["s_ec"], 1)
            for k in range(2):
                pool.memset(contrib[k][:], 0.0).then_inc(S["s_ec"], 1)

            def gather(e, k, c):
                pool.indirect_dma_start(got[k][:, c], None, xn_rows, bass.IndirectOffsetOnAxis(cur[k][:, c:c + 1], 0)).then_inc(S[f"s_got{k}"], 16)

            pool.wait_ge(S["s_zero"], 16)
            pool.wait_ge(S["s_cur"], 1)
            for c in range(CC):
                gather(0, 0, c)

            def pool_expert(i, k, more_rows=True):
                e = 2 * i + k
                if more_rows:
                    pool.wait_ge(S["s_cur"], e + 2)
                    apart(pool)
                    for c in range(CC):
                        gather(e + 1, 1 - k, c)
                pool.wait_ge(S["s_con"], e + 1)
                pool.wait_ge(S["s_sc"], 16 * CC * e)
                apart(pool)
                for c in range(CC):
                    pool.indirect_dma_start(sum_rows, bass.IndirectOffsetOnAxis(cur[k][:, c:c + 1], 0), contrib[k][:, c], None,
                                            compute_op=ALU.add).then_inc(S["s_sc"], 16)

            with pool.Fori(0, E1 // 2 - 1) as i:
                pool_expert(i, 0)
                pool_expert(i, 1)
            pool_expert(E1 // 2 - 1, 0)
            pool_expert(E1 // 2 - 1, 1, False)

        def scores(pe, b, n, by_key):
            pair, f = divmod(n, 5)
            h = 2 * pair + (f // 2 if f < 4 else 0)
            bank = ba[n % 3]
            if f in (0, 2):
                groups = [(h, 3 if not by_key else 0, 0)]
            elif f in (1, 3):
                groups = [(h, 2, 0), (h, 0, 384)] if not by_key else [(h, 1, 0), (h, 3, 384)]
            else:
                groups = [(h, 1, 0), (h + 1, 1, 256)] if not by_key else [(h, 2, 0), (h + 1, 2, 256)]
            for head, blk, col in groups:
                if by_key:
                    w = SEQ - blk * P
                    pe.matmul(bank[:, col:col + w], lhsT=KT[0:K_ROWS, head, blk * P:(blk + 1) * P],
                              rhs=QT[0:K_ROWS, head, blk * P:], start=True, stop=False)
                    last = pe.matmul(bank[:, col:col + P], lhsT=identb[:], rhs=mask_k[:], start=False, stop=True)
                else:
                    w = (blk + 1) * P
                    pe.matmul(bank[:, col:col + w], lhsT=QT[0:QK_ROWS, head, blk * P:(blk + 1) * P],
                              rhs=KT[0:QK_ROWS, head, 0:w], start=True, stop=False)
                    last = pe.matmul(bank[:, col + w - P:col + w], lhsT=identb[:], rhs=mask_q[:], start=False, stop=True)
            last.then_inc(S["s_st" if by_key else "s_S"], 1)

        def prob_block(h, blk):
            slot, k = (h // 2) % 3, h % 2
            if blk == 0:
                return probs[:, slot, 2 * k, :]
            if blk == 1:
                return probs[:, slot, 2 * k + 1, 0:384]
            if blk == 3:
                return probs[:, slot, 2 * k + 1, 384:512]
            return probs[:, slot, 4, 256 * k:256 * k + 256]

        @block.tensor
        def _(pe):
            def transposes(bank, src, done):
                for q in range(Q):
                    last = pe.transpose(bank[:, q * P:(q + 1) * P], src[:, q], ident[:])
                last.then_inc(S[done], 1)

            def f_turn_x(f):
                pe.wait_ge(S["s_lnf"], f + 1)
                pe.wait_ge(S["s_x2"], f)
                transposes(fa[0], f_n, "s_T1")

            def f_kvq(f):
                pe.wait_ge(S["s_nT1"], f + 1)
                for q in range(Q):
                    if q == 3:
                        pe.wait_ge(S["s_kvqe"], Q * f + 1)
                    pe.matmul(fa[(q + 1) % 3][:, 0:3 * D], lhsT=f_nT[:, q * P:(q + 1) * P], rhs=w_kvq[:],
                              start=True, stop=True).then_inc(S["s_kvq"], 1)

            def f_kv(f):
                pe.wait_ge(S["s_kqn"], f + 1)
                pe.wait_ge(S["s_kvqe"], Q * f + Q)
                for q in range(Q):
                    last = pe.matmul(fa[2][:, 0:P], lhsT=kvq[:, q, D:2 * D], rhs=kvq[:, q, 0:D], start=q == 0, stop=q == Q - 1)
                last.then_inc(S["s_kvt"], 1)
                for q in range(Q):
                    last = pe.transpose(fa[0][:, q * P:(q + 1) * P], kvq[:, q, 2 * D:3 * D], ident[:])
                last.then_inc(S["s_qT"], 1)

            def f_kvo(f):
                pe.wait_ge(S["s_kvm"], f + 1)
                pe.matmul(fa[1][:, 0:D], lhsT=kvm[:], rhs=w_o0[:], start=True, stop=True).then_inc(S["s_kvo"], 1)

            def f_out(f):
                pe.wait_ge(S["s_qnT"], f + 1)
                pe.wait_ge(S["s_kvoc"], f + 1)
                for q in range(Q):
                    last = pe.matmul(fa[2][:, q * D:(q + 1) * D], lhsT=qnT[:, q * P:(q + 1) * P], rhs=kvo[:], start=True, stop=True)
                last.then_inc(S["s_at0"], 1)

            def f_turn_x1(f):
                pe.wait_ge(S["s_x1n"], f + 1)
                transposes(fa[0], f_n, "s_T2")

            def f_gate(f):
                pe.wait_ge(S["s_nT2"], f + 1)
                for q in range(Q):
                    last = pe.matmul(fa[1][:, q * E0:(q + 1) * E0], lhsT=f_nT[:, q * P:(q + 1) * P], rhs=gate_w[:], start=True, stop=True)
                last.then_inc(S["s_lgm"], 1)

            def f_turn_gates(f):
                pe.wait_ge(S["s_gp"], f + 1)
                apart(pe)
                for q in range(Q):
                    last = pe.transpose(fa[2][:].bitcast(BF16)[0:PARTS * E0, q * P:(q + 1) * P],
                                        gparts[:, q].rearrange("p c e -> p (c e)"), identb[:])
                last.then_inc(S["s_gTp"], 1)

            def up(b, e):
                if e == 0:
                    pe.wait_ge(S["s_exf"], b + 1)
                else:
                    pe.wait_ge(S["s_sil"], U0 * b + e)
                pe.matmul(fa[0][:], lhsT=w1[:, e], rhs=f_nT[:], start=True, stop=True).then_inc(S["s_h1"], 1)
                if 0 < e <= E0:
                    pe.wait_ge(S["s_t"], E0 * b + e)
                elif e > E0:
                    pe.wait_ge(S["s_h"], U0 * b + e)
                pe.matmul(fa[1][:], lhsT=w3[:, e], rhs=f_nT[:], start=True, stop=True).then_inc(S["s_h3"], 1)
                if e < E0:
                    if e == 0:
                        pe.wait_ge(S["s_gT"], b + 1)
                    else:
                        pe.wait_ge(S["s_h"], U0 * b + e)
                    pe.matmul(fa[2][:], lhsT=pick[:, e], rhs=gT[:], start=True, stop=True).then_inc(S["s_gb"], 1)

            def down(b, e):
                pe.wait_ge(S["s_h"], U0 * b + e + 1)
                if e == 0:
                    pe.wait_ge(S["s_yT"], b)
                    pe.wait_ge(S["s_vp"], b)
                pe.matmul(facc[:], lhsT=w2[:, e], rhs=hh[:, e % 2], start=e == 0, stop=e == U0 - 1).then_inc(S["s_ym"], 1)

            def r_turn(r):
                pe.wait_ge(S["s_lnb"], r + 1)
                transposes(facc, b_n, "s_T3")

            def r_q(r):
                pe.wait_ge(S["s_nT3"], r + 1)
                pe.matmul(facc[:], lhsT=w_q1[:], rhs=b_nT[:], start=True, stop=True).then_inc(S["s_q"], 1)

            def r_k(r):
                pe.wait_ge(S["s_r1"], 2 * r + 1)
                pe.matmul(facc[:], lhsT=w_k1[:], rhs=b_nT[:], start=True, stop=True).then_inc(S["s_k"], 1)

            def r_v(r):
                pe.wait_ge(S["s_r1"], 2 * r + 2)
                for q in range(Q):
                    last = pe.matmul(facc[:, q * D:(q + 1) * D], lhsT=b_nT[:, q * P:(q + 1) * P], rhs=w_v1[:], start=True, stop=True)
                last.then_inc(S["s_v"], 1)

            def t_turn(t):
                pe.wait_ge(S["s_norm"], 4 * t + 4)
                transposes(bo, ao, "s_aTt")

            def t_out(t):
                pe.wait_ge(S["s_aT"], t + 1)
                for q in range(Q):
                    last = pe.matmul(bo[:, q * D:(q + 1) * D], lhsT=b_nT[:, q * P:(q + 1) * P], rhs=w_o1[:], start=True, stop=True)
                last.then_inc(S["s_wo"], 1)

            def t_turn_row(t):
                pe.wait_ge(S["s_row"], t + 1)
                for q in range(Q):
                    last = pe.transpose(bo[:, q * P:(q + 1) * P], row[:, q, 0:D], ident[:])
                last.then_inc(S["s_T4"], 1)

            def t_router(t):
                pe.wait_ge(S["s_nT4"], t + 1)
                for q in range(Q):
                    last = pe.matmul(bo[:, q * E1:(q + 1) * E1], lhsT=b_nT[:, q * P:(q + 1) * P], rhs=router_w[:], start=True, stop=True)
                last.then_inc(S["s_l1"], 1)

            T_STEPS = {0: t_turn, 1: t_out, 5: t_turn_row, 7: t_router}

            def x_phase(f, b, t):
                for step in range(U0 + 1):
                    if f is not None and step < U0:
                        up(f, step)
                    if t is not None and step in T_STEPS:
                        T_STEPS[step](t)
                    if b is not None and 1 <= step <= HEADS // 2:
                        for n in range(5 * (step - 1), 5 * step):
                            if n == 0:
                                pe.wait_ge(S["s_qk"], 16 * 2 * PARTS * PARTS * (b + 1))
                                pe.wait_ge(S["s_exp"], FILLS * b)
                            if n >= 3:
                                pe.wait_ge(S["s_red"], FILLS * b + n - 2)
                            scores(pe, b, n, False)
                    if f is not None and step > 0:
                        down(f, step - 1)
                if f is not None:
                    pe.wait_ge(S["s_yT"], f + 1)
                    for q in range(Q):
                        last = pe.transpose(fa[0][:, q * P:(q + 1) * P], yT[:, q * P:(q + 1) * P], ident[:])
                    last.then_inc(S["s_yTt"], 1)

            def y_phase(b, f, r, t):
                def turn_maxima():
                    pe.wait_ge(S["s_nmp"], b + 1)
                    pe.wait_ge(S["s_l1c"], b)
                    apart(pe)
                    for q in range(Q):
                        last = pe.transpose(bo[:].bitcast(BF16)[0:PARTS * HEADS, q * P:(q + 1) * P],
                                            nmp[:, q].rearrange("p c h -> p (c h)"), identb[:])
                    last.then_inc(S["s_nmt"], 1)

                def pair_scores(pair):
                    if pair == 0:
                        pe.wait_ge(S["s_mx"], 16 * PARTS * (b + 1))
                        pe.wait_ge(S["s_red"], FILLS * (b + 1))
                    for n in range(5 * pair, 5 * pair + 5):
                        if n >= 3:
                            pe.wait_ge(S["s_exp"], FILLS * b + n - 2)
                        scores(pe, b, n, True)

                def outputs(k):
                    pe.wait_ge(S["s_exp"], FILLS * b + 10 * k + 10)
                    if k > 0:
                        pe.wait_ge(S["s_norm"], 4 * b + k)
                    for blk in range(Q):
                        for j in range(4):
                            last = pe.matmul(bo[32 * j:32 * j + 32, blk * P:], lhsT=vp[:, blk, 4 * k + j],
                                             rhs=prob_block(4 * k + j, blk), start=blk == 0, stop=blk == Q - 1)
                    last.then_inc(S["s_pv"], 1)

                def turn_outputs(k):
                    pe.wait_ge(S["s_oT"], 4 * b + k + 1)
                    for q in range(Q):
                        last = pe.transpose(bo[:, q * P:(q + 1) * P], oT[:, q * P:(q + 1) * P], ident[:])
                    last.then_inc(S["s_tr"], 1)

                def if_b(step, *args):
                    if b is not None:
                        step(*args)

                def if_f(step):
                    if f is not None:
                        step(f)

                def if_r(step):
                    if r is not None:
                        step(r)

                if_b(turn_maxima)
                if_r(r_turn)
                if_f(f_turn_x)
                if_b(pair_scores, 0)
                if_r(r_q)
                if_f(f_kvq)
                if_b(pair_scores, 1)
                if_r(r_k)
                if_b(pair_scores, 2)
                if_b(outputs, 0)
                if_b(pair_scores, 3)
                if_b(turn_outputs, 0)
                if_f(f_kv)
                if_b(pair_scores, 4)
                if_f(f_kvo)
                if_b(outputs, 1)
                if_b(pair_scores, 5)
                if_b(turn_outputs, 1)
                if_f(f_out)
                if_b(pair_scores, 6)
                if_b(outputs, 2)
                if_f(f_turn_x1)
                if_b(pair_scores, 7)
                if_b(turn_outputs, 2)
                if_f(f_gate)
                if_r(r_v)
                if_b(outputs, 3)
                if_b(turn_outputs, 3)
                if_f(f_turn_gates)

            pe.wait_ge(S["s_wfront"], FW)
            pe.wait_ge(S["s_wback"], BW)
            pe.wait_ge(S["s_one"], 1)
            looped(pe, x_phase, y_phase)
            if debug == "x3":
                return
            pe.wait_ge(S["s_gj"], 1)
            for g in range(8):
                last = pe.transpose(fa[g // 4][:, (g % 4) * P:(g % 4 + 1) * P], logits_gj[:, g], ident[:])
            last.then_inc(S["s_LTt"], 1)

            def across(col, pattern, src, ready, n, done):
                pe.wait_ge(S[ready], n)
                pe.matmul(fa[2][:, col:col + 1], lhsT=pattern[:], rhs=src[:], start=True, stop=True).then_inc(S[done], 1)

            with pe.Fori(0, 32) as i:
                across(0, same_e, cnt, "s_cnt", i + 1, "s_tot")
            across(0, same_e, cnt, "s_gtc", 1, "s_gtt")
            across(0, earlier_e, cnt, "s_gtc", 2, "s_gtt")
            across(0, earlier_e, cnt, "s_gtc", 3, "s_gtt")
            pe.wait_ge(S["s_rc"], 1)
            for g in range(8):
                last = pe.transpose(fa[g // 4][:, (g % 4) * P:(g % 4 + 1) * P], place[:, g * P:(g + 1) * P], ident[:])
            last.then_inc(S["s_slT"], 1)
            lists_of = [ba[0], ba[1], ba[2], bo]
            for g in range(8):
                pe.wait_ge(S["s_hot"], g + 1)
                for j in range(GJ):
                    for q in range(4):
                        col = j * E1 + 4 * q
                        last = pe.matmul(lists_of[q][:, 0:P], lhsT=hot_hi[:, g % 2, col:col + 4].rearrange("p e h -> p (e h)"),
                                         rhs=hot_lo[:, g % 2, :, col:col + 4].rearrange("p w e l -> p w (e l)"),
                                         start=g == 0 and j == 0, stop=g == 7 and j == GJ - 1)
                last.then_inc(S["s_list"], 1)

            def pe_expert(i, k):
                e = 2 * i + k
                pe.wait_ge(S[f"s_got{k}"], 16 * CC * (i + 1))
                pe.wait_ge(S["s_found"], 4)
                for c in range(CC):
                    last = pe.transpose(fa[0][:, c * P:(c + 1) * P], got[k][:, c, 0:D], ident[:])
                last.then_inc(S["s_xet"], 1)
                pe.wait_ge(S["s_xe"], e + 1)
                pe.wait_ge(S[f"s_fw{k}"], 48 * (i + 1))
                pe.wait_ge(S["s_hT"], FC * e)
                for f in range(FC):
                    pe.matmul([fa[1], fa[2], ba[0], ba[1]][f][:], lhsT=fc1[k][:, f * P:(f + 1) * P], rhs=xe[k][:], start=True, stop=True)\
                      .then_inc(S["s_up"], 1)
                pe.wait_ge(S["s_hT"], FC * e + FC)
                pe.wait_ge(S["s_ys"], e)
                for c in range(CC):
                    for f in range(FC):
                        last = pe.matmul(ba[2][:, c * D:(c + 1) * D], lhsT=hT[k][:, f, c * P:(c + 1) * P], rhs=fc2[k][:, f], start=f == 0, stop=f == FC - 1)
                last.then_inc(S["s_dn"], 1)

            with pe.Fori(0, E1 // 2) as i:
                pe_expert(i, 0)
                pe_expert(i, 1)

        @block.scalar
        def _(act):
            def copy(dst, src, ready, n, done):
                act.wait_ge(S[ready], n)
                act.activation(dst, src, ACT.Copy).then_inc(S[done], 1)

            act.wait_ge(S["s_wfront"], FW)
            act.activation(inv_scaling[:], m_b[:], ACT.Exp, scale=-1.0).then_inc(S["s_scal"], 1)
            act.wait_ge(S["s_scal"], 3)
            act.activation(inv_scaling[:], inv_scaling[:], ACT.Exp, scale=-float(np.log(SEQ))).then_inc(S["s_scal"], 1)

            def x_phase(f, b, t):
                for e in range(U0):
                    if f is not None:
                        act.wait_ge(S["s_h1"], U0 * f + e + 1)
                        if e < 2:
                            act.wait_ge(S["s_h"], U0 * f)
                        else:
                            act.wait_ge(S["s_t"], E0 * f + e - 1)
                        act.activation(sil[:, e % 2], fa[0][:], ACT.Silu).then_inc(S["s_sil"], 1)
                    if t is not None:
                        if e == 0:
                            copy(b_nT[:], bo[:], "s_aTt", t + 1, "s_aT")
                        if e == 3:
                            act.wait_ge(S["s_y"], t + 1)
                            for q in range(Q):
                                act.activation(b_n[:, q], row[:, q, 0:D], ACT.Square, accum_out=ysq[:, q:q + 1]).then_inc(S["s_ysq"], 1)
                        if e == 5:
                            copy(b_nT[:], bo[:], "s_T4", t + 1, "s_nT4")
                if f is not None:
                    copy(yT[:], facc[:], "s_ym", U0 * f + U0, "s_yT")

            def y_phase(b, f, r, t):
                def exps(pair):
                    if b is None:
                        return
                    for f_ in range(5):
                        n = 5 * pair + f_
                        act.wait_ge(S["s_st"], FILLS * b + n + 1)
                        if f_ == 0:
                            act.wait_ge(S["s_pv"], 4 * b + max(pair - 1, 0) // 2)
                        act.activation(probs[:, pair % 3, f_], ba[n % 3][:], ACT.Exp, scale=SCALE).then_inc(S["s_exp"], 1)

                if t is not None:
                    act.wait_ge(S["s_l1x"], t + 1)
                    act.activation(l1[:], l1[:], ACT.Exp).then_inc(S["s_ex1"], 1)
                if b is not None:
                    copy(nmT[:], bo[:].bitcast(BF16)[0:PARTS * HEADS, 0:SEQ], "s_nmt", b + 1, "s_nmT")
                if r is not None:
                    copy(b_nT[:], facc[:], "s_T3", r + 1, "s_nT3")
                if f is not None:
                    copy(f_nT[:], fa[0][:], "s_T1", f + 1, "s_nT1")
                exps(0)
                if r is not None:
                    act.wait_ge(S["s_qkw"], 32 * r)
                    copy(qkp[:, 0, 0], facc[:], "s_q", r + 1, "s_p1")
                if f is not None:
                    act.wait_ge(S["s_kvqe"], Q * f + Q)
                    act.activation(sq[:].rearrange("p q (w d) -> p q w d", w=2), kvq[:].rearrange("p q (w d) -> p q w d", w=3)[:, :, 0:3:2],
                                   ACT.Square).then_inc(S["s_sq"], 1)
                exps(1)
                if r is not None:
                    copy(qkp[:, 1, 0], facc[:], "s_k", r + 1, "s_p1")
                exps(2)
                exps(3)
                if f is not None:
                    copy(qnT[:], fa[0][:], "s_qT", f + 1, "s_qnT")
                exps(4)
                if f is not None:
                    copy(kvo[:], fa[1][:, 0:D], "s_kvo", f + 1, "s_kvoc")
                exps(5)
                exps(6)
                exps(7)
                if f is not None:
                    copy(f_nT[:], fa[0][:], "s_T2", f + 1, "s_nT2")
                    act.wait_ge(S["s_lgx"], f + 1)
                    act.activation(sc[:], lg[:], ACT.Exp).then_inc(S["s_exf"], 1)
                if r is not None:
                    act.wait_ge(S["s_pv"], 4 * r)
                    copy(vp[:, :, :, 0:HD], facc[:].rearrange("p (q h d) -> p q h d", q=Q, h=HEADS), "s_v", r + 1, "s_vp")
                if f is not None:
                    copy(gT[0:PARTS * E0, :], fa[2][:].bitcast(BF16)[0:PARTS * E0, 0:SEQ], "s_gTp", f + 1, "s_gT")

            looped(act, x_phase, y_phase)
            if debug == "x3":
                return
            act.wait_ge(S["s_prob"], BATCH)
            act.wait_ge(S["s_rowd"], 16 * BATCH)
            copy(LT[:, 512:], fa[1][:], "s_LTt", 1, "s_LTc")
            for q, bank in enumerate([ba[0], ba[1], ba[2], bo]):
                copy(found[:, q].rearrange("p w l -> p (w l)"), bank[:, 0:P], "s_list", 8, "s_found")
            act.wait_ge(S["s_fb"], 16)

            def act_expert(i, k):
                e = 2 * i + k
                act.activation(fb1c[k][:], fb1[:, e], ACT.Copy).then_inc(S["s_bc1"], 1)
                copy(xe[k][:], fa[0][:], "s_xet", e + 1, "s_xe")
                act.wait_ge(S["s_bc1"], e + 1)
                for f in range(FC):
                    act.wait_ge(S["s_up"], FC * e + f + 1)
                    act.activation(hT[k][:, f], [fa[1], fa[2], ba[0], ba[1]][f][:], ACT.Gelu, bias=fb1c[k][:, f:f + 1]).then_inc(S["s_hT"], 1)

            with act.Fori(0, E1 // 2) as i:
                act_expert(i, 0)
                act_expert(i, 1)

        @block.vector
        def _(dve):
            class Steps:

                def __init__(self, name, per_batch):
                    self.sem, self.per, self.n, self.b = S[name], per_batch, 0, 0

                def start(self, b):
                    assert self.n in (0, self.per), self.n
                    self.b, self.n = b, 0

                def __call__(self, ins, wait=True):
                    self.n += 1
                    ins.then_inc(self.sem, 1)
                    if wait:
                        dve.wait_ge(self.sem, self.b * self.per + self.n)
                        apart(dve)

            fc, nc_, rc, tc = Steps("s_fc", 43), Steps("s_bc", 3), Steps("s_rc1", 8), Steps("s_tc", 11)

            def stats(step, x, st, mv):
                for q in range(Q):
                    step(dve.bn_stats(st[:, q], x[:, q]), q == Q - 1)
                for q in range(Q):
                    step(dve.bn_aggr(mv[:, q], st[:, q]), q == Q - 1)

            def center(dst, x, mv, rs, done):
                for q in range(Q):
                    last = dve.tensor_scalar(dst(q), x[:, q], mv[:, q, 0:1], rs[:, q:q + 1], ALU.subtract, ALU.mult)
                last.then_inc(S[done], 1)

            dve.wait_ge(S["s_wfront"], FW)
            dve.wait_ge(S["s_scal"], 1)
            dve.tensor_scalar(inv_scaling[:], inv_scaling[:], 1.0, None, ALU.add).then_inc(S["s_scal"], 1)
            dve.wait_ge(S["s_scal"], 2)
            dve.reciprocal(inv_scaling[:], inv_scaling[:]).then_inc(S["s_scal"], 1)
            dve.wait_ge(S["s_scal"], 4)
            dve.wait_ge(S["s_one"], 1)
            dve.tensor_tensor(kv_scale[:], blockdiag[:], inv_scaling[:, :, None].to_broadcast([P, HEADS, HD]), ALU.mult).then_inc(S["s_scal"], 1)
            dve.wait_ge(S["s_scal"], 5)

            def f_norm(f):
                fc.start(f)
                dve.wait_ge(S["s_x"], 16 * f + 16)
                stats(fc, xin, f_st, f_mv)
                dve.tensor_scalar(f_ve[:, 0:Q], f_mv[:, :, 1], EPS, None, ALU.add).then_inc(S["s_varf"], 1)

            def f_center(f):
                dve.wait_ge(S["s_rsf"], 2 * f + 1)
                center(lambda q: f_n[:, q], xin, f_mv, f_rs, "s_lnf")

            def f_bias(f):
                for q in range(Q):
                    dve.wait_ge(S["s_kvq"], Q * f + q + 1)
                    dve.tensor_tensor(kvq[:, q], fa[(q + 1) % 3][:, 0:3 * D], b_kvq[:], ALU.add).then_inc(S["s_kvqe"], 1)

            def f_l2(f):
                dve.wait_ge(S["s_sq"], f + 1)
                fc(dve.tensor_reduce(n2[:], sq[:].rearrange("p q (g d) -> p (q g) d", d=HD), X, ALU.add))
                fc(dve.tensor_scalar(n2[:], n2[:], L2_EPS_SQ, None, ALU.max))
                fc(dve.tensor_scalar(rn[:].bitcast(I32), n2[:].bitcast(I32), -0.5, float(0x5F3759DF), ALU.mult, ALU.add))
                for _ in range(3):
                    fc(dve.scalar_tensor_tensor(rt[:], n2[:], -0.5, rn[:], ALU.mult, ALU.mult))
                    fc(dve.tensor_tensor(rt[:], rt[:], rn[:], ALU.mult))
                    fc(dve.scalar_tensor_tensor(rn[:], rt[:], 1.5, rn[:], ALU.add, ALU.mult))
                rs4 = rn[:].rearrange("p (q w h) -> p q w h", q=Q, w=2)
                for w in range(2):
                    last = dve.tensor_tensor(kvq[:, :, 2 * w * D:(2 * w + 1) * D].rearrange("p q (h d) -> p q h d", d=HD),
                                             kvq[:, :, 2 * w * D:(2 * w + 1) * D].rearrange("p q (h d) -> p q h d", d=HD),
                                             rs4[:, :, w, :, None].to_broadcast([P, Q, HEADS, HD]), ALU.mult)
                last.then_inc(S["s_kqn"], 1)

            def f_kvm(f):
                dve.wait_ge(S["s_kvt"], f + 1)
                dve.tensor_tensor(kvm[:], fa[2][:, 0:P], kv_scale[:].rearrange("p h d -> p (h d)"), ALU.mult).then_inc(S["s_kvm"], 1)

            def f_x1(f):
                dve.wait_ge(S["s_at0"], f + 1)
                dve.wait_ge(S["s_xres"], f + 1)
                dve.tensor_tensor(x1[:], fa[2][:].rearrange("p (q d) -> p q d", q=Q), xres[:], ALU.add).then_inc(S["s_x1"], 1)
                dve.wait_ge(S["s_x1"], f + 1)
                apart(dve)
                stats(fc, x1, f_st, f_mv)
                dve.tensor_scalar(f_ve[:, 0:Q], f_mv[:, :, 1], EPS, None, ALU.add).then_inc(S["s_varf"], 1)
                dve.wait_ge(S["s_rsf"], 2 * f + 2)
                center(lambda q: f_n[:, q], x1, f_mv, f_rs, "s_x1n")

            def f_logits(f):
                dve.wait_ge(S["s_lgm"], f + 1)
                dve.tensor_copy(lg[:], fa[1][:, 0:Q * E0].rearrange("p (q e) -> p q e", q=Q)).then_inc(S["s_lge"], 1)
                dve.wait_ge(S["s_lge"], f + 1)
                fc(dve.tensor_reduce(lm[:], lg[:], X, ALU.max))
                dve.tensor_tensor(lg[:], lg[:], lm[:, :, None].to_broadcast([P, Q, E0]), ALU.subtract).then_inc(S["s_lgx"], 1)

            def f_gates(f):
                dve.wait_ge(S["s_exf"], f + 1)
                fc(dve.tensor_reduce(ls[:], sc[:], X, ALU.add))
                fc(dve.reciprocal(ls[:], ls[:]))
                fc(dve.tensor_tensor(sc[:], sc[:], ls[:, :, None].to_broadcast([P, Q, E0]), ALU.mult))
                fc(dve.tensor_tensor(bs[:], sc[:], gate_b[:, None, :].to_broadcast([P, Q, E0]), ALU.add))
                other = bs[:, :, None, :].to_broadcast([P, Q, E0, E0])
                own = bs[:, :, :, None].to_broadcast([P, Q, E0, E0])
                fc(dve.tensor_tensor(ge[:], other, own, ALU.is_ge), False)
                fc(dve.tensor_tensor(gt[:], other, own, ALU.is_gt))
                fc(dve.tensor_tensor(ge[:], ge[:], below[:, None].to_broadcast([P, Q, E0, E0]), ALU.mult), False)
                fc(dve.tensor_tensor(gt[:], gt[:], above[:, None].to_broadcast([P, Q, E0, E0]), ALU.mult))
                fc(dve.tensor_tensor(ge[:], ge[:], gt[:], ALU.add))
                fc(dve.tensor_reduce(rank[:], ge[:], X, ALU.add))
                fc(dve.scalar_tensor_tensor(gates[:], rank[:], TOPK - 0.5, sc[:], ALU.is_lt, ALU.mult))
                fc(dve.tensor_copy(gparts[:, :, 0], gates[:]))
                fc(dve.tensor_tensor(gres[:], gates[:], gparts[:, :, 0], ALU.subtract))
                fc(dve.tensor_copy(gparts[:, :, 1], gres[:]))
                dve.tensor_tensor(gparts[:, :, 2], gres[:], gparts[:, :, 1], ALU.subtract).then_inc(S["s_gp"], 1)

            def product(f, e):
                dve.wait_ge(S["s_sil"], U0 * f + e + 1)
                dve.wait_ge(S["s_h3"], U0 * f + e + 1)
                if e < E0:
                    dve.tensor_tensor(th[:, e % 2], sil[:, e % 2], fa[1][:], ALU.mult).then_inc(S["s_t"], 1)
                else:
                    dve.wait_ge(S["s_ym"], U0 * f + e - 1)
                    dve.tensor_tensor(hh[:, e % 2], sil[:, e % 2], fa[1][:], ALU.mult).then_inc(S["s_h"], 1)

            def gated(f, e):
                if e < E0:
                    dve.wait_ge(S["s_ym"], U0 * f + max(e - 1, 0))
                    dve.wait_ge(S["s_gb"], E0 * f + e + 1)
                    dve.wait_ge(S["s_t"], E0 * f + e + 1)
                    dve.tensor_tensor(hh[:, e % 2], th[:, e % 2], fa[2][:], ALU.mult).then_inc(S["s_h"], 1)

            def maxima(b, n):
                pair, f = divmod(n, 5)
                h, bank = 2 * pair + (f // 2 if f < 4 else 0), ba[n % 3]
                dve.wait_ge(S["s_S"], FILLS * b + n + 1)
                if f in (0, 2):
                    last = dve.tensor_reduce(nm[:, 3, h:h + 1], bank[:], X, ALU.max, negate=True)
                elif f in (1, 3):
                    dve.tensor_reduce(nm[:, 2, h:h + 1], bank[:, 0:384], X, ALU.max, negate=True)
                    last = dve.tensor_reduce(nm[:, 0, h:h + 1], bank[:, 384:512], X, ALU.max, negate=True)
                else:
                    last = dve.tensor_reduce(nm[:, 1, h:h + 2], bank[:].rearrange("p (h k) -> p h k", h=2), X, ALU.max, negate=True)
                last.then_inc(S["s_red"], 1)

            def x3_of(b):
                return x3[:, b * Q:(b + 1) * Q] if isinstance(b, int) else x3[:, bass.ts(b, Q)]

            def t_x3(t):
                tc.start(t)
                dve.wait_ge(S["s_wo"], t + 1)
                x3t = x3_of(t)
                dve.tensor_tensor(x3t, bo[:].rearrange("p (q d) -> p q d", q=Q), x3t, ALU.add).then_inc(S["s_x3"], 1)
                dve.wait_ge(S["s_x3"], t + 1)
                apart(dve)
                stats(tc, x3t, b_st, b_mv)
                dve.tensor_scalar(b_ve[:], b_mv[:, :, 1], EPS, None, ALU.add).then_inc(S["s_vart"], 1)

            def t_center(t):
                dve.wait_ge(S["s_rst"], 2 * t + 1)
                dve.wait_ge(S["s_rowd"], 16 * t)
                center(lambda q: row[:, q, 0:D], x3_of(t), b_mv, b_rs, "s_y")

            def t_rms(t):
                dve.wait_ge(S["s_ysq"], Q * t + Q)
                dve.tensor_scalar(b_ve[:], ysq[:], 1.0 / D, EPS, ALU.mult, ALU.add).then_inc(S["s_vart"], 1)
                dve.wait_ge(S["s_rst"], 2 * t + 2)
                dve.wait_ge(S["s_y"], t + 1)
                for q in range(Q):
                    last = dve.scalar_tensor_tensor(row[:, q, 0:D], row[:, q, 0:D], b_rs[:, q:q + 1], norm_w[:], ALU.mult, ALU.mult)
                last.then_inc(S["s_row"], 1)

            def t_logits(t):
                dve.wait_ge(S["s_l1"], t + 1)
                lb = logits_flat[:, t * Q:(t + 1) * Q] if isinstance(t, int) else logits_flat[:, bass.ts(t, Q)]
                dve.tensor_tensor(lb, bo[:, 0:Q * E1].rearrange("p (q e) -> p q e", q=Q),
                                  router_b[:, None, :].to_broadcast([P, Q, E1]), ALU.add).then_inc(S["s_l1c"], 1)
                dve.wait_ge(S["s_l1c"], t + 1)
                apart(dve)
                tc(dve.tensor_reduce(l1m[:], lb, X, ALU.max))
                dve.tensor_tensor(l1[:], lb, l1m[:, :, None].to_broadcast([P, Q, E1]), ALU.subtract).then_inc(S["s_l1x"], 1)

            def t_probs(t):
                dve.wait_ge(S["s_ex1"], t + 1)
                tc(dve.tensor_reduce(l1m[:], l1[:], X, ALU.add))
                tc(dve.reciprocal(l1m[:], l1m[:]))
                dve.tensor_tensor(row[:, :, D:], l1[:], l1m[:, :, None].to_broadcast([P, Q, E1]), ALU.mult).then_inc(S["s_prob"], 1)

            T_STEPS = {2: t_x3, 3: t_center, 4: t_rms, 8: t_logits}

            def x_phase(f, b, t):
                for e in range(U0):
                    if f is not None:
                        product(f, e)
                    if t is not None and e in T_STEPS:
                        T_STEPS[e](t)
                    if b is not None and 1 <= e <= HEADS // 2:
                        maxima(b, 5 * e - 5)
                    if f is not None:
                        gated(f, e)
                    if b is not None and 1 <= e <= HEADS // 2:
                        for n in range(5 * e - 4, 5 * e):
                            maxima(b, n)
                if b is not None:
                    nc_.start(b)
                    dve.wait_ge(S["s_red"], FILLS * (b + 1))
                    nc_(dve.tensor_copy(nmp[:, :, 0], nm[:]))
                    nc_(dve.tensor_tensor(nmr[:], nm[:], nmp[:, :, 0], ALU.subtract))
                    nc_(dve.tensor_copy(nmp[:, :, 1], nmr[:]))
                    dve.tensor_tensor(nmp[:, :, 2], nmr[:], nmp[:, :, 1], ALU.subtract).then_inc(S["s_nmp"], 1)
                if f is not None:
                    dve.wait_ge(S["s_yTt"], f + 1)
                    dve.tensor_tensor(x3_of(f), fa[0][:].rearrange("p (q d) -> p q d", q=Q), x1[:], ALU.add).then_inc(S["s_x2"], 1)

            def r_norm(r):
                rc.start(r)
                dve.wait_ge(S["s_x2"], r + 1)
                apart(dve)
                stats(rc, x3_of(r), b_st, b_mv)
                dve.tensor_scalar(b_ve[:], b_mv[:, :, 1], EPS, None, ALU.add).then_inc(S["s_varb"], 1)

            def r_center(r):
                dve.wait_ge(S["s_rsb"], r + 1)
                center(lambda q: b_n[:, q], x3_of(r), b_mv, b_rs, "s_lnb")

            def r_rest(r, w):
                dve.wait_ge(S["s_p1"], 2 * r + w + 1)
                dve.tensor_tensor(qkr[:, w], facc[:], qkp[:, w, 0], ALU.subtract).then_inc(S["s_r1"], 1)

            def y_phase(b, f, r, t):
                def outputs(k):
                    if b is None:
                        return
                    dve.wait_ge(S["s_pv"], 4 * b + k + 1)
                    dve.tensor_copy(oT[:], bo[:]).then_inc(S["s_oT"], 1)

                def norm(k):
                    if b is None:
                        return
                    dve.wait_ge(S["s_tr"], 4 * b + k + 1)
                    o4 = bo[:].rearrange("p (q j r) -> p q j r", q=Q, j=4)
                    dve.reciprocal(rden[:], o4[:, :, :, HD]).then_inc(S["s_rden"], 1)
                    dve.wait_ge(S["s_rden"], 4 * b + k + 1)
                    dve.tensor_tensor(ao[:, :, 4 * k * HD:4 * (k + 1) * HD].rearrange("p q (j d) -> p q j d", d=HD),
                                      o4[:, :, :, 0:HD], rden[:, :, :, None].to_broadcast([P, Q, 4, HD]), ALU.mult).then_inc(S["s_norm"], 1)

                def if_f(step):
                    if f is not None:
                        step(f)

                def if_r(step, *w):
                    if r is not None:
                        step(r, *w)

                if_r(r_norm)
                if_f(f_norm)
                if_r(r_center)
                if_f(f_center)
                if t is not None:
                    t_probs(t)
                if_r(r_rest, 0)
                if_f(f_bias)
                if_r(r_rest, 1)
                if_f(f_l2)
                outputs(0)
                norm(0)
                if_f(f_kvm)
                outputs(1)
                norm(1)
                if_f(f_x1)
                outputs(2)
                norm(2)
                if_f(f_logits)
                if_f(f_gates)
                outputs(3)
                norm(3)

            looped(dve, x_phase, y_phase)
            if debug == "x3":
                return
            dve.wait_ge(S["s_prob"], BATCH)
            dve.wait_ge(S["s_rowd"], 16 * BATCH)
            dve.tensor_copy(logits_gj[:].rearrange("p g (j e) -> p g j e", j=GJ),
                            logits_flat[:].rearrange("p (j g) e -> p g j e", g=8)).then_inc(S["s_gj"], 1)
            dve.wait_ge(S["s_LTt"], 1)
            dve.tensor_copy(LT[:, 0:512], fa[0][:]).then_inc(S["s_LTc"], 1)
            dve.wait_ge(S["s_LTc"], 2)
            dve.wait_ge(S["s_ec"], 5)
            sr = Steps("s_sr", 5)
            TOP = -2 ** 31

            def as_float(step, src):
                step(dve.tensor_scalar(flip[:], src[:], 31, -1, ALU.arith_shift_right, ALU.bitwise_xor))
                step(dve.scalar_tensor_tensor(bits[:], flip[:], TOP, src[:], ALU.bitwise_or, ALU.bitwise_xor))

            with dve.Fori(0, 32) as i:
                sr.start(i)
                sr(dve.tensor_tensor(cand[:], key[:], bit[:], ALU.bitwise_or))
                as_float(sr, cand)
                dve.tensor_scalar(above_t[:], LT[:], bits[:].bitcast(F32), None, ALU.is_ge, ALU.add, accum_out=cnt[:]).then_inc(S["s_cnt"], 1)
                dve.wait_ge(S["s_tot"], i + 1)
                sr(dve.tensor_scalar(okm[:], fa[2][:, 0:1], CAP - 0.5, -1.0, ALU.is_ge, ALU.mult))
                sr(dve.scalar_tensor_tensor(key[:], okm[:], bit[:], key[:], ALU.bitwise_and, ALU.bitwise_or))
                dve.tensor_scalar(bit[:], bit[:], 1, None, ALU.logical_shift_right).then_inc(S["s_bit"], 1)
                dve.wait_ge(S["s_bit"], i + 1)
            ec = Steps("s_eqt", 10)
            as_float(ec, key)
            thr = bits[:].bitcast(F32)
            dve.tensor_scalar(above_t[:], LT[:], thr, None, ALU.is_gt, ALU.add, accum_out=cnt[:]).then_inc(S["s_gtc"], 1)
            ec(dve.tensor_scalar(equal_t[:], LT[:], thr, None, ALU.is_equal, ALU.add, accum_out=off_eq[:]))
            dve.wait_ge(S["s_gtt"], 1)
            ec(dve.tensor_scalar(more[:], fa[2][:, 0:1], -1.0, float(CAP), ALU.mult, ALU.add))
            dve.tensor_copy(cnt[:], off_eq[:]).then_inc(S["s_gtc"], 1)
            dve.wait_ge(S["s_gtt"], 2)
            ec(dve.tensor_copy(off_eq[:], fa[2][:, 0:1]))
            ec(dve.tensor_tensor_scan(place[:], ones[:], equal_t[:], off_eq[:], ALU.mult, ALU.add))
            ec(dve.scalar_tensor_tensor(equal_t[:], place[:], more[:], equal_t[:], ALU.is_le, ALU.mult))
            dve.scalar_tensor_tensor(chosen[:], above_t[:], 0.0, equal_t[:], ALU.add, ALU.add, accum_out=cnt[:]).then_inc(S["s_gtc"], 1)
            dve.wait_ge(S["s_gtt"], 3)
            ec(dve.tensor_copy(off_sel[:], fa[2][:, 0:1]))
            ec(dve.tensor_tensor_scan(place[:], ones[:], chosen[:], off_sel[:], ALU.mult, ALU.add))
            dve.tensor_tensor(place[:], place[:], chosen[:], ALU.mult).then_inc(S["s_rc"], 1)
            dve.wait_ge(S["s_slT"], 1)
            sl = Steps("s_slot", 6)
            for half in range(2):
                sl(dve.tensor_scalar(slot[:, 4 * half:4 * half + 4].rearrange("p g c -> p (g c)"), fa[half][:], -1.0, None, ALU.add), half == 1)
            sl(dve.tensor_scalar(hi_i[:], slot[:], 4, None, ALU.arith_shift_right), False)
            sl(dve.tensor_scalar(lo_i[:], slot[:], 15, None, ALU.bitwise_and))
            sl(dve.tensor_copy(hi[:], hi_i[:]), False)
            sl(dve.tensor_copy(lo[:], lo_i[:]))
            hs = Steps("s_rc2", 8)
            for g in range(8):
                if g >= 2:
                    dve.wait_ge(S["s_list"], g - 1)
                    dve.wait_ge(S["s_hot"], g - 1)
                dve.tensor_tensor(hot_hi[:, g % 2], hi[:, g, :, None].to_broadcast([P, P, 32]), iota32[:, None, :].to_broadcast([P, P, 32]), ALU.is_equal)
                hs(dve.tensor_tensor(hot[:, g % 2], lo[:, g, :, None].to_broadcast([P, P, 16]), iota16[:, None, :].to_broadcast([P, P, 16]), ALU.is_equal))
                dve.tensor_scalar(hot_lo[:, g % 2, 0], hot[:, g % 2], pcol[:], None, ALU.mult)
                dve.tensor_tensor(hot_lo[:, g % 2, 1].rearrange("p (j e) l -> p j (e l)", j=GJ), hot[:, g % 2].rearrange("p (j e) l -> p j (e l)", j=GJ),
                                  tcol[:, g, :, None].to_broadcast([P, GJ, E1 * 16]), ALU.mult).then_inc(S["s_hot"], 1)
            dve.wait_ge(S["s_found"], 4)
            for q in range(4):
                for j in range(4):
                    r = slice(32 * j, 32 * j + 32)
                    dve.scalar_tensor_tensor(idx[r, q], found[r, q, 1, 16 * j:16 * j + 16], float(P), found[r, q, 0, 16 * j:16 * j + 16],
                                             ALU.mult, ALU.add).then_inc(S["s_idx"], 1)

            def current(i, k):
                if not (isinstance(i, int) and i == 0):
                    dve.wait_ge(S["s_sc"], 16 * CC * (2 * i + k - 1))
                dve.tensor_copy(cur[k][:], idx_pc[:, 2 * i + k]).then_inc(S["s_cur"], 1)

            def dve_expert(i, k, more_rows=True):
                e = 2 * i + k
                dve.wait_ge(S[f"s_got{k}"], 16 * CC * (i + 1))
                dve.tensor_copy(gate[k][:], got[k][:, :, D + e]).then_inc(S["s_gatec"], 1)
                dve.wait_ge(S["s_dn"], e + 1)
                dve.wait_ge(S[f"s_fw{k}"], 48 * (i + 1))
                dve.tensor_tensor(ysum[k][:], ba[2][:].rearrange("p (c d) -> p c d", c=CC), fb2[k][:, None, :].to_broadcast([P, CC, D]), ALU.add)\
                   .then_inc(S["s_ys"], 1)
                dve.wait_ge(S["s_ys"], e + 1)
                dve.wait_ge(S["s_gatec"], e + 1)
                if not isinstance(i, int) or i > 0 or k > 0:
                    pass
                dve.tensor_tensor(contrib[k][:, :, 0:D], ysum[k][:], gate[k][:, :, None].to_broadcast([P, CC, D]), ALU.mult)
                dve.tensor_copy(contrib[k][:, :, D], gate[k][:]).then_inc(S["s_con"], 1)

            dve.wait_ge(S["s_ldr"], 16)
            current(0, 0)
            current(0, 1)
            with dve.Fori(0, E1 // 2 - 1) as i:
                dve_expert(i, 0)
                current(i + 1, 0)
                dve_expert(i, 1)
                current(i + 1, 1)
            dve_expert(E1 // 2 - 1, 0)
            dve_expert(E1 // 2 - 1, 1)
            fs = Steps("s_fs", 8)
            n = TILES // 4
            for k in range(4):
                dve.wait_ge(S[f"s_sum{k}"], 16)
                t = slice(k * n, (k + 1) * n)
                fs(dve.scalar_tensor_tensor(gsum[:, t], sums[:, t, D], 0.0, sums[:, t, D], ALU.is_le, ALU.add))
                fs(dve.reciprocal(gsum[:, t], gsum[:, t]))
                for m in range(k * n, (k + 1) * n):
                    last = dve.scalar_tensor_tensor(x3[:, m], sums[:, m, 0:D], gsum[:, m:m + 1], x3[:, m], ALU.mult, ALU.add)
                last.then_inc(S["s_fin"], 1)


def layout(i):
    i = {n: np.asarray(v) for n, v in i.items()}
    o = dict(i)
    o["L0_ffn_gate_w"] = i["L0_ffn_gate_w"].T
    for n in ("Wq", "Wk", "Wv", "Wo"):
        o["L1_attn_" + n] = i["L1_attn_" + n].T
    for n in ("w1", "w3"):
        routed = i["L0_ffn_" + n].transpose(2, 0, 1)
        shared = i["L0_ffn_s" + n].reshape(SHARED, P, D).transpose(2, 0, 1)
        o["L0_" + n] = np.concatenate([routed, shared], axis=1)
        del o["L0_ffn_" + n], o["L0_ffn_s" + n]
    routed = i["L0_ffn_w2"].transpose(2, 0, 1)
    shared = i["L0_ffn_sw2"].T.reshape(SHARED, P, D).transpose(1, 0, 2)
    o["L0_w2"] = np.concatenate([routed, shared], axis=1)
    del o["L0_ffn_w2"], o["L0_ffn_sw2"]
    o["L1_ffn_router_weight"] = i["L1_ffn_router_weight"].T
    o["L1_ffn_fc1_weight"] = i["L1_ffn_fc1_weight"].transpose(2, 0, 1)
    o["L1_ffn_fc1_bias"] = i["L1_ffn_fc1_bias"].reshape(E1, FC, P).transpose(2, 0, 1)
    o["L1_ffn_fc2_weight"] = i["L1_ffn_fc2_weight"].reshape(E1, D, FC, P).transpose(3, 0, 2, 1)
    return {n: np.ascontiguousarray(v) for n, v in o.items()}


def kernel(**inputs):
    import concourse.bacc as bacc
    from concourse.bass_utils import run_bass_kernel_spmd

    nc = bacc.Bacc("TRN2", target_bir_lowering=False, num_devices=1)
    arrays = layout(inputs)
    a = {n: nc.dram_tensor("in_" + n, v.shape, mybir.dt.from_np(v.dtype), kind="ExternalInput").ap() for n, v in arrays.items()}
    out = nc.dram_tensor("out", (BATCH, SEQ, D), F32, kind="ExternalOutput").ap()
    build_kernel(nc, a, out)
    r = run_bass_kernel_spmd(nc, [{"in_" + n: v for n, v in arrays.items()}], core_ids=[0])
    return r.results[0]["out"]
```

```python
import numpy as np
import concourse.bass as bass
import concourse.mybir as mybir
from contextlib import ExitStack

F32, BF16, I32, I16 = mybir.dt.float32, mybir.dt.bfloat16, mybir.dt.int32, mybir.dt.int16
ALU = mybir.AluOpType
ACT = mybir.ActivationFunctionType
X = mybir.AxisListType.X

P = 128
BATCH, SEQ, D = 16, 512, 128
Q = SEQ // P
TOK = BATCH * SEQ
TILES = TOK // P
HEADS, HD = 16, 8
E0, TOPK, SHARED = 8, 2, 2
U0 = E0 + SHARED
E1, FF = 16, 512
CAP = TOK // E1
FC = FF // P
CC = CAP // P
EPS = 1e-5
L2_EPS_SQ = 1e-24
SCALE = float(1.0 / np.sqrt(HD))
MASKED = -1.0e38
PARTS = 3
QK_ROWS = PARTS * PARTS * HD
MX_ROW = QK_ROWS
K_ROWS = QK_ROWS + PARTS
FILLS = HEADS // 2 * 5
ROW = D + E1
CROW = D + 4
GJ = TILES // 8


def build_kernel(nc, a, out):
    ctx = ExitStack()
    with ctx:
        def sb(name, shape, dt=F32):
            return ctx.enter_context(nc.sbuf_tensor(name, shape, dt))

        early = ExitStack()

        def sb1(name, shape, dt=F32):
            return early.enter_context(nc.sbuf_tensor(name, shape, dt))

        def sem(name):
            return ctx.enter_context(nc.semaphore(name))

        qk_parts = nc.dram_tensor("qk_parts", (BATCH, 2, PARTS, P, SEQ), BF16, kind="Internal").ap()
        xn_rows = nc.dram_tensor("xn_rows", (TOK, ROW), F32, kind="Internal").ap()
        sum_rows = nc.dram_tensor("sum_rows", (TOK, CROW), F32, kind="Internal").ap()
        lists = nc.dram_tensor("lists", (E1, CAP), I32, kind="Internal").ap()

        fa = [ctx.enter_context(nc.psum_tensor(f"fa{i}", [P, 512], F32)) for i in range(3)]
        facc = ctx.enter_context(nc.psum_tensor("facc", [P, 512], F32))
        ba = [ctx.enter_context(nc.psum_tensor(f"ba{i}", [P, 512], F32)) for i in range(3)]
        bo = ctx.enter_context(nc.psum_tensor("bo", [P, 512], F32))

        ident = sb("ident", [P, P])
        zrow = sb("zrow", [P, CROW])
        identb = sb("identb", [P, P], BF16)
        mask_q = sb("mask_q", [P, P], BF16)
        mask_k = sb("mask_k", [P, P], BF16)
        pick = sb("pick", [P, E0, P], BF16)
        blockdiag = sb("blockdiag", [P, HEADS, HD])
        below = sb("below", [P, E0, E0])
        same_e = sb("same_e", [P, P])
        earlier_e = sb("earlier_e", [P, P])
        mhalf = sb("mhalf", [P, P])
        pcol = sb("pcol", [P, 1])
        tcol = sb("tcol", [P, 8, GJ])
        own4 = sb("own4", [P, 4])
        x3 = sb("x3", [P, TILES, D])
        logits_flat = sb("logits", [P, TILES, E1])
        w_kvq = sb1("w_kvq", [P, 3 * D])
        b_kvq = sb1("b_kvq", [P, 3 * D])
        w_o0 = sb1("w_o0", [P, D])
        b_o0 = sb1("b_o0", [P, D])
        m_b = sb1("m_b", [P, HEADS])
        inv_scaling = sb1("inv_scaling", [P, HEADS])
        kv_scale = sb1("kv_scale", [P, HEADS, HD])
        gate_w = sb1("gate_w", [P, E0])
        gate_b = sb1("gate_b", [P, E0])
        w1 = sb1("w1", [P, U0, P])
        w3 = sb1("w3", [P, U0, P])
        w2 = sb1("w2", [P, U0, P])
        w_q1 = sb1("w_q1", [P, D])
        w_k1 = sb1("w_k1", [P, D])
        w_v1 = sb1("w_v1", [P, D])
        w_o1 = sb1("w_o1", [P, D])
        norm_w = sb1("norm_w", [P, D])
        router_w = sb1("router_w", [P, E1])
        router_b = sb1("router_b", [P, E1])
        xin = sb1("xin", [P, Q, D])
        xres = sb1("xres", [P, Q, D])
        f_st = sb1("f_st", [P, Q, 6])
        f_mv = sb1("f_mv", [P, Q, 2])
        f_ve = sb1("f_ve", [P, Q])
        f_rs = sb1("f_rs", [P, Q])
        n2 = sb1("n2", [P, Q, 2 * HEADS])
        rn = sb1("rn", [P, Q, 2 * HEADS])
        rt = sb1("rt", [P, Q, 2 * HEADS])
        f_n = sb1("f_n", [P, Q, D])
        f_nT = sb1("f_nT", [P, SEQ])
        kvq = sb1("kvq", [P, Q, 3 * D])
        sq = sb1("sq", [P, Q, 2 * D])
        qnT = sb1("qnT", [P, SEQ])
        kvm = sb1("kvm", [P, P])
        kvo = sb1("kvo", [P, P])
        x1 = sb1("x1", [P, Q, D])
        lg = sb1("lg", [P, Q, E0])
        lm = sb1("lm", [P, Q])
        ls = sb1("ls", [P, Q])
        sc = sb1("sc", [P, Q, E0])
        bs = sb1("bs", [P, Q, E0])
        eq = sb1("eq", [P, Q, E0, E0])
        gt = sb1("gt", [P, Q, E0, E0])
        rank = sb1("rank", [P, Q, E0])
        gates = sb1("gates", [P, Q, E0])
        gres = sb1("gres", [P, Q, E0])
        gparts = sb1("gparts", [P, Q, PARTS, E0], BF16)
        gT = sb1("gT", [P, SEQ], BF16)
        sil = sb1("sil", [P, 2, SEQ])
        th = sb1("th", [P, 2, SEQ])
        gb = sb1("gb", [P, 2, SEQ])
        hh = sb1("hh", [P, 2, SEQ])
        yT = sb1("yT", [P, SEQ])
        b_st = sb1("b_st", [P, Q, 6])
        b_mv = sb1("b_mv", [P, Q, 2])
        b_ve = sb1("b_ve", [P, Q])
        b_rs = sb1("b_rs", [P, Q])
        b_n = sb1("b_n", [P, Q, D])
        b_nT = sb1("b_nT", [P, SEQ])
        qkp = sb1("qkp", [P, 2, PARTS, SEQ], BF16)
        qkr = sb1("qkr", [P, 2, SEQ])
        vp = sb1("vp", [P, Q, HEADS, 32])
        QT = sb1("QT", [P, HEADS, SEQ], BF16)
        KT = sb1("KT", [P, HEADS, SEQ], BF16)
        nm = sb1("nm", [P, Q, HEADS])
        nmr = sb1("nmr", [P, Q, HEADS])
        nmp = sb1("nmp", [P, 2, Q, PARTS, HEADS // 2], BF16)
        nmT = sb1("nmT", [PARTS * HEADS // 2, 2, SEQ], BF16)
        probs = sb1("probs", [P, 3, 5, SEQ])
        oT = sb1("oT", [P, SEQ])
        rden = sb1("rden", [P, Q, 4])
        ao = sb1("ao", [P, Q, D])
        row = sb1("row", [P, Q, ROW])
        l1 = sb1("l1", [P, Q, E1])
        ysq = sb1("ysq", [P, Q])
        l1m = sb1("l1m", [P, Q])

        early.close()
        W = TOK // 8
        idx = sb("idx", [P, 4, 16], I32)
        idx_pc = sb("idx_pc", [P, E1, CC], I32)
        cur = [sb(f"cur{i}", [P, CC], I32) for i in range(4)]
        logits_gj = sb("logits_gj", [P, 8, P])
        choice = ExitStack()

        def sb2(name, shape, dt=F32):
            return choice.enter_context(nc.sbuf_tensor(name, shape, dt))

        keys = sb2("keys", [P, W], I32)
        half_i = sb2("half_i", [P, W], I32)
        search = ExitStack()

        def sb3(name, shape, dt=F32):
            return search.enter_context(nc.sbuf_tensor(name, shape, dt))

        steps3 = sb2("steps3", [P, 3])
        cand = sb2("cand", [P, 3])
        cnts = sb2("cnts", [P, 3])
        signs = sb2("signs", [P, W], BF16)
        minus3 = sb2("minus3", [P, 1])
        targets = sb2("targets", [P, 3])
        okm = sb2("okm", [P, 3])
        digit, step, found_high, found_low, target = (sb2(n, [P, 1]) for n in ("digit", "step", "found_high", "found_low", "target"))
        thr_hi, thr_lo, flip, bits = (sb2(n, [P, 1], I32) for n in ("thr_hi", "thr_lo", "flip", "bits"))
        cnt, more, off_eq, off_sel = (sb2(n, [P, 1]) for n in ("cnt", "more", "off_eq", "off_sel"))
        hi, lo = sb2("hi", [P, W], BF16), sb2("lo", [P, W], BF16)
        tile_of = sb2("tile_of", [P, 8, GJ, E1], BF16)
        ones = sb3("ones", [P, W])
        LT = sb3("LT", [P, W])
        above_t = sb3("above_t", [P, W])
        equal_t = sb3("equal_t", [P, W])
        place = sb3("place", [P, W])
        chosen = sb3("chosen", [P, W])
        low = sb3("low", [P, W])
        high16, low16 = sb3("high16", [P, W], I16), sb3("low16", [P, W], I16)
        passed = sb3("passed", [P, 3, W], BF16)
        search.close()
        hot_hi = sb2("hot_hi", [P, W // 4, 32, 4], BF16)
        hot_lo = sb2("hot_lo", [P, 2, 16, W], BF16)
        diag = sb2("diag", [P, 4, 2, 4, 16])
        found = sb2("found", [P, 4, 2, 16])
        choice.close()
        got = [sb(f"got{i}", [P, CC, ROW]) for i in range(2)]
        gate = [sb(f"gate{i}", [P, CC]) for i in range(2)]
        xe = [sb(f"xe{i}", [P, CAP]) for i in range(2)]
        fc1 = [sb(f"fc1_{i}", [P, FF]) for i in range(2)]
        fc2 = [sb(f"fc2_{i}", [P, FC, D]) for i in range(2)]
        fb2 = [sb(f"fb2_{i}", [P, D]) for i in range(2)]
        fb1 = sb("fb1", [P, E1, FC])
        fb1c = [sb(f"fb1c{i}", [P, FC]) for i in range(2)]
        hT = [sb(f"hT{i}", [P, FC, CAP]) for i in range(2)]
        ysum = [sb(f"ysum{i}", [P, CC, D]) for i in range(2)]
        contrib = [sb(f"contrib{i}", [P, CC, CROW]) for i in range(2)]
        sums = sb("sums", [P, TILES, CROW])
        gsum = sb("gsum", [P, TILES])

        names = """s_wfront s_wexperts s_wback s_cst s_one s_scal s_x s_lnf s_xres s_varf s_rsf s_T1 s_nT1 s_kvq s_kvqe s_sq
            s_kqn s_kvt s_kvm s_qT s_qnT s_kvo s_kvoc s_at0 s_x1 s_x1n s_T2 s_nT2 s_lgm s_lge s_exf s_lgx s_gp s_gTp s_gT
            s_h1 s_h3 s_gb s_gbc s_sil s_t s_h s_hs s_ym s_yT s_yTt s_x2 s_fc
            s_pad s_lnb s_varb s_rsb s_T3 s_nT3 s_q s_k s_v s_p1 s_r1 s_p2 s_p3 s_vp s_qkw s_qk0 s_qk1 s_S s_red s_nmp s_nmt
            s_nmT s_mx0 s_mx1 s_st s_exp s_pv s_oT s_tr s_norm s_aTt s_aT s_wo s_x3 s_y s_ysq s_row s_T4 s_nT4 s_l1 s_l1c
            s_l1x s_ex1 s_prob s_rowd s_mstep s_zero
            s_vart s_rst s_rstep s_tc s_rden s_LTt s_cnt s_tot s_sr s_gtc s_gtt s_eqt s_rc s_slT s_slot s_hot s_list s_keys s_cand s_cnt3 s_set s_step s_gth s_gthc s_low s_diag s_gatec s_fs s_gj s_found s_idx s_bc1 s_ldw s_ldr
            s_cur s_got0 s_got1 s_xet s_xe s_fw0 s_fw1 s_up s_hT s_dn s_ys s_con s_sc s_ec s_sum0 s_sum1 s_sum2 s_sum3 s_fin s_finp s_gsum s_scaled s_out s_fb""".split()
        S = {n: sem(n) for n in names}
        block = ctx.enter_context(nc.Block())
        FW, EW, BW = 16 * 11, 16 * 3, 16 * 7

        def apart(eng):
            eng.nop(nofuse=True)

        def bcast_rows(v, n):
            return v.rearrange("(o n) -> o n", o=1)[0].partition_broadcast(P)

        first, beside = 3, [4] * (U0 - 2) + [3, 2]
        assert first + sum(beside) == FILLS
        fills_of = [range(first + sum(beside[:e]), first + sum(beside[:e + 1])) for e in range(U0)]

        def looped(engine, x_phase, y_phase):
            x_phase(None, None, None, 0)
            y_phase(None, 0, None, None)
            x_phase(0, None, None, 1)
            y_phase(None, 1, 0, None)
            x_phase(1, 0, None, 2)
            y_phase(0, 2, 1, None)
            with engine.Fori(1, BATCH - 2) as i:
                x_phase(i + 1, i, i - 1, i + 2)
                y_phase(i, i + 2, i + 1, i - 1)
            n = BATCH - 1
            x_phase(n, n - 1, n - 2, None)
            y_phase(n - 1, None, n, n - 2)
            x_phase(None, n, n - 1, None)
            y_phase(n, None, None, n - 1)
            x_phase(None, None, n, None)
            y_phase(None, None, None, n)

        @block.sync
        def _(sp):
            sp.dma_start(xin[:], a["L0_attn_x"][0].rearrange("(q p) d -> p q d", p=P)).then_inc(S["s_x"], 16)
            for dst, src in (
                (w_kvq[:, 0:D], a["L0_attn_Wk"]), (w_kvq[:, D:2 * D], a["L0_attn_Wv"]), (w_kvq[:, 2 * D:], a["L0_attn_Wq"]),
                (b_kvq[:, 0:D], bcast_rows(a["L0_attn_bk"], D)), (b_kvq[:, D:2 * D], bcast_rows(a["L0_attn_bv"], D)),
                (b_kvq[:, 2 * D:], bcast_rows(a["L0_attn_bq"], D)),
                (w_o0[:], a["L0_attn_Wo"]), (b_o0[:], bcast_rows(a["L0_attn_bo"], D)), (m_b[:], bcast_rows(a["L0_attn_m"], HEADS)),
                (gate_w[:], a["L0_ffn_gate_w"]), (gate_b[:], bcast_rows(a["L0_ffn_gate_bias"], E0)),
            ):
                sp.dma_start(dst, src).then_inc(S["s_wfront"], 16)
            for dst, src in ((w1, "w1"), (w3, "w3"), (w2, "w2")):
                sp.dma_start(dst[:], a["L0_" + src]).then_inc(S["s_wexperts"], 16)
            sp.dma_start(norm_w[:], bcast_rows(a["L1_ffn_norm_weight"], D)).then_inc(S["s_wback"], 16)
            for dst, name in ((w_q1, "L1_attn_Wq"), (w_k1, "L1_attn_Wk"), (w_v1, "L1_attn_Wv"), (w_o1, "L1_attn_Wo"),
                              (router_w, "L1_ffn_router_weight")):
                sp.dma_start(dst[:], a[name]).then_inc(S["s_wback"], 16)
            sp.dma_start(router_b[:], bcast_rows(a["L1_ffn_router_bias"], E1)).then_inc(S["s_wback"], 16)
            sp.wait_ge(S["s_cst"], 1)
            sp.dma_start(sum_rows.rearrange("(t p) c -> p t c", p=P),
                         zrow[:, None, :].to_broadcast([P, TILES, CROW])).then_inc(S["s_zero"], 16)

            def part_dmas(b):
                for w in range(2):
                    sp.wait_ge(S["s_p3"], 2 * b + w + 1)
                    apart(sp)
                    sp.dma_start(qk_parts[b, w].rearrange("c p t -> p c t"), qkp[:, w]).then_inc(S["s_qkw"], 16)
                sp.wait_ge(S["s_qkw"], 32 * b + 32)
                apart(sp)

            def back_dmas(b, half):
                if isinstance(b, int) and b == 0:
                    sp.wait_ge(S["s_pad"], 3)
                else:
                    sp.wait_ge(S["s_st"], FILLS * b - (1 - half) * FILLS // 2)
                    apart(sp)
                heads = slice(half * HEADS // 2, (half + 1) * HEADS // 2)
                for i in range(PARTS):
                    for j in range(PARTS):
                        r = (i * PARTS + j) * HD
                        for t, w, part in ((QT, 0, i), (KT, 1, j)):
                            sp.dma_start(t[r:r + HD, heads], qk_parts[b, w, part].rearrange("(h d) t -> d h t", d=HD)[:, heads])\
                              .then_inc(S[f"s_qk{half}"], 16)

            def max_dmas(b, half):
                sp.wait_ge(S["s_nmT"], 2 * b + half + 1)
                apart(sp)
                n = HEADS // 2
                for c in range(PARTS):
                    sp.dma_start(QT[MX_ROW + c:MX_ROW + c + 1, half * n:(half + 1) * n], nmT[c * n:(c + 1) * n, half, :])\
                      .then_inc(S[f"s_mx{half}"], 16)

            def row_dmas(b):
                sp.wait_ge(S["s_prob"], b + 1)
                apart(sp)
                sp.dma_start(xn_rows[bass.ts(b, SEQ)].rearrange("(q p) c -> p q c", p=P), row[:]).then_inc(S["s_rowd"], 16)

            def load_x(b):
                sp.wait_ge(S["s_lnf"], b)
                sp.wait_ge(S["s_xres"], b)
                apart(sp)
                sp.dma_start(xin[:], a["L0_attn_x"][b].rearrange("(q p) d -> p q d", p=P)).then_inc(S["s_x"], 16)

            def both(step, b):
                step(b, 0)
                step(b, 1)

            load_x(1)
            part_dmas(0)
            both(back_dmas, 0)
            load_x(2)
            both(max_dmas, 0)
            part_dmas(1)
            both(back_dmas, 1)
            with sp.Fori(1, BATCH - 2) as i:
                load_x(i + 2)
                both(max_dmas, i)
                row_dmas(i - 1)
                part_dmas(i + 1)
                both(back_dmas, i + 1)
            n = BATCH - 1
            both(max_dmas, n - 1)
            row_dmas(n - 2)
            part_dmas(n)
            both(back_dmas, n)
            both(max_dmas, n)
            row_dmas(n - 1)
            row_dmas(n)
            sp.wait_ge(S["s_rowd"], 16 * BATCH)

            sp.wait_ge(S["s_idx"], 1)
            for e in range(4):
                sp.dma_start(lists.rearrange("(q e) (h l) -> e h q l", e=4, l=16)[e], idx[e:P:4]).then_inc(S["s_ldw"], 16)
            sp.dma_start(fb1[:], a["L1_ffn_fc1_bias"]).then_inc(S["s_fb"], 16)
            sp.wait_ge(S["s_ldw"], 64)
            sp.dma_start(idx_pc[:], lists.rearrange("e (p c) -> p e c", c=CC)).then_inc(S["s_ldr"], 16)

            def weights(e, k):
                sp.dma_start(fc1[k][:], a["L1_ffn_fc1_weight"][:, e]).then_inc(S[f"s_fw{k}"], 16)
                sp.dma_start(fc2[k][:], a["L1_ffn_fc2_weight"][:, e]).then_inc(S[f"s_fw{k}"], 16)
                sp.dma_start(fb2[k][:], a["L1_ffn_fc2_bias"][e].partition_broadcast(P)).then_inc(S[f"s_fw{k}"], 16)

            weights(0, 0)
            weights(1, 1)
            with sp.Fori(1, E1 // 2) as i:
                for k in range(2):
                    sp.wait_ge(S["s_ys"], 2 * i + k - 1)
                    apart(sp)
                    weights(2 * i + k, k)
            sp.wait_ge(S["s_sc"], 16 * CC * E1)
            n = TILES // 4
            rows = sum_rows.rearrange("(t p) c -> p t c", p=P)
            for k in range(4):
                sp.dma_start(sums[:, k * n:(k + 1) * n], rows[:, k * n:(k + 1) * n]).then_inc(S[f"s_sum{k}"], 16)
            for k in range(4):
                sp.wait_ge(S["s_fin"], k + 1)
                sp.wait_ge(S["s_finp"], k + 1)
                sp.dma_start(out.rearrange("b (q p) d -> p (b q) d", p=P)[:, k * n:(k + 1) * n], x3[:, k * n:(k + 1) * n]).then_inc(S["s_out"], 16)
            sp.wait_ge(S["s_out"], 64)

        @block.gpsimd
        def _(pool):
            c = [1]

            def const(ins):
                c[0] += 1
                ins.then_inc(S["s_cst"], 1)
                pool.wait_ge(S["s_cst"], c[0])

            pool.memset(zrow[:], 0.0).then_inc(S["s_cst"], 1)
            pool.wait_ge(S["s_cst"], 1)
            for t in (ident, identb):
                const(pool.memset(t[:], 0.0))
                const(pool.affine_select(t[:], t[:], [[-1, P]], ALU.not_equal, 1.0, base=0, channel_multiplier=1))
            const(pool.memset(mask_q[:], 0.0))
            const(pool.affine_select(mask_q[:], mask_q[:], [[-1, P]], ALU.is_ge, MASKED, base=0, channel_multiplier=1))
            const(pool.memset(mask_k[:], 0.0))
            const(pool.affine_select(mask_k[:], mask_k[:], [[1, P]], ALU.is_ge, MASKED, base=0, channel_multiplier=-1))
            const(pool.memset(pick[:], 0.0))
            for part in range(PARTS):
                const(pool.affine_select(pick[:], pick[:], [[-1, E0], [0, P]], ALU.not_equal, 1.0, base=-E0 * part, channel_multiplier=1))
            const(pool.memset(blockdiag[:], 1.0))
            const(pool.affine_select(blockdiag[:], blockdiag[:], [[-HD, HEADS], [0, HD]], ALU.is_ge, 0.0, base=0, channel_multiplier=1))
            const(pool.affine_select(blockdiag[:], blockdiag[:], [[HD, HEADS], [0, HD]], ALU.is_ge, 0.0, base=HD - 1, channel_multiplier=-1))
            const(pool.memset(below[:], 1.0))
            const(pool.affine_select(below[:], below[:], [[1, E0], [-1, E0]], ALU.is_ge, 0.0, base=-1, channel_multiplier=0))
            const(pool.iota(pcol[:], [[1, 1]], base=0, channel_multiplier=1, allow_small_or_imprecise_dtypes=True))
            const(pool.iota(tcol[:], [[1, 8], [8, GJ]], base=0, channel_multiplier=0, allow_small_or_imprecise_dtypes=True))
            const(pool.memset(mhalf[:], -0.5))
            pool.memset(gT[:], 0.0).then_inc(S["s_one"], 1)

            def power(dst, src, ready, done, count):
                pool.wait_ge(S[ready], count)
                pool.tensor_tensor(dst, src, mhalf[:, 0:src.shape[-1]], ALU.pow).then_inc(S[done], 1)

            def gated(f, e):
                pool.wait_ge(S["s_t"], E0 * f + e + 1)
                pool.wait_ge(S["s_gbc"], E0 * f + e + 1)
                pool.wait_ge(S["s_ym"], U0 * f + max(e - 1, 0))
                pool.tensor_tensor(hh[:, e % 2], th[:, e % 2], gb[:, e % 2], ALU.mult).then_inc(S["s_h"], 1)

            def x_phase(f, b, t, g):
                for e in range(U0):
                    if t is not None and e == 5:
                        power(b_rs[:], b_ve[:], "s_vart", "s_rst", 2 * t + 1)
                    if g is not None and e == 3:
                        power(f_rs[:, 0:Q], f_ve[:, 0:Q], "s_varf", "s_rsf", 2 * g + 1)
                    if g is not None and e == 5:
                        pool.wait_ge(S["s_x"], 16 * g + 16)
                        pool.wait_ge(S["s_wfront"], FW)
                        pool.wait_ge(S["s_x1"], g)
                        pool.tensor_tensor(xres[:], xin[:], b_o0[:, None, :].to_broadcast([P, Q, D]), ALU.add).then_inc(S["s_xres"], 1)
                    if t is not None and e == 7:
                        power(b_rs[:], b_ve[:], "s_vart", "s_rst", 2 * t + 2)
                    if f is not None and e < E0:
                        gated(f, e)

            def y_phase(b, f, r, t):
                if r is not None:
                    power(b_rs[:], b_ve[:], "s_varb", "s_rsb", r + 1)
                if r is not None:
                    for w in range(2):
                        pool.wait_ge(S["s_r1"], 2 * r + w + 1)
                        apart(pool)
                        pool.tensor_copy(qkp[:, w, 1], qkr[:, w]).then_inc(S["s_p2"], 1)
                        pool.wait_ge(S["s_p2"], 2 * r + w + 1)
                        pool.tensor_tensor(qkp[:, w, 2], qkr[:, w], qkp[:, w, 1], ALU.subtract).then_inc(S["s_p3"], 1)
                if f is not None:
                    power(f_rs[:, 0:Q], f_ve[:, 0:Q], "s_varf", "s_rsf", 2 * f + 2)

            looped(pool, x_phase, y_phase)
            for m in range(1 - GJ, GJ):
                if m == 1 - GJ:
                    const(pool.memset(same_e[:], 0.0))
                    const(pool.memset(earlier_e[:], 0.0))
                const(pool.affine_select(same_e[:], same_e[:], [[-1, P]], ALU.not_equal, 1.0, base=E1 * m, channel_multiplier=1))
                if m > 0:
                    const(pool.affine_select(earlier_e[:], earlier_e[:], [[-1, P]], ALU.not_equal, 1.0, base=E1 * m, channel_multiplier=1))
            pool.wait_ge(S["s_prob"], BATCH)
            pool.wait_ge(S["s_rowd"], 16 * BATCH)
            pool.memset(ones[:], 1.0).then_inc(S["s_ec"], 1)
            pool.memset(found_high[:], -2.0 ** 15).then_inc(S["s_ec"], 1)
            pool.memset(found_low[:], -2.0 ** 15).then_inc(S["s_ec"], 1)
            pool.memset(target[:], CAP - 0.5).then_inc(S["s_ec"], 1)
            pool.iota(steps3[:], [[1, 3]], base=1, channel_multiplier=0, allow_small_or_imprecise_dtypes=True).then_inc(S["s_ec"], 1)
            pool.tensor_copy(tile_of[:], tcol[:, :, :, None].to_broadcast([P, 8, GJ, E1])).then_inc(S["s_ec"], 1)
            pool.wait_ge(S["s_idx"], 1)
            for k in range(2):
                pool.memset(contrib[k][:], 0.0).then_inc(S["s_ec"], 1)

            def gather(k, c):
                pool.indirect_dma_start(got[k % 2][:, c], None, xn_rows, bass.IndirectOffsetOnAxis(cur[k][:, c:c + 1], 0)).then_inc(S[f"s_got{k % 2}"], 16)

            pool.wait_ge(S["s_zero"], 16)
            for k in range(2):
                pool.wait_ge(S["s_cur"], k + 1)
                for c in range(CC):
                    gather(k, c)

            def pool_expert(e, k, more_rows=True):
                if more_rows:
                    pool.wait_ge(S["s_cur"], e + 3)
                    pool.wait_ge(S["s_xet"], e + 1)
                    pool.wait_ge(S["s_gatec"], e + 1)
                    apart(pool)
                    for c in range(CC):
                        gather((k + 2) % 4, c)
                pool.wait_ge(S["s_con"], e + 1)
                pool.wait_ge(S["s_sc"], 16 * CC * e)
                apart(pool)
                for c in range(CC):
                    pool.indirect_dma_start(sum_rows, bass.IndirectOffsetOnAxis(cur[k][:, c:c + 1], 0), contrib[k % 2][:, c], None,
                                            compute_op=ALU.add).then_inc(S["s_sc"], 16)

            with pool.Fori(0, E1 // 4 - 1) as i:
                for k in range(4):
                    pool_expert(4 * i + k, k)
            for k in range(4):
                pool_expert(E1 - 4 + k, k, k < 2)
            n = TILES // 4
            for k in range(4):
                t = slice(k * n + n // 2, (k + 1) * n)
                pool.wait_ge(S["s_scaled"], k + 1)
                pool.tensor_tensor(x3[:, t], x3[:, t], sums[:, t, 0:D], ALU.add).then_inc(S["s_finp"], 1)

        def scores(pe, b, n, by_key):
            pair, f = divmod(n, 5)
            h = 2 * pair + (f // 2 if f < 4 else 0)
            bank = ba[n % 3]
            if f in (0, 2):
                groups = [(h, 3 if not by_key else 0, 0)]
            elif f in (1, 3):
                groups = [(h, 2, 0), (h, 0, 384)] if not by_key else [(h, 1, 0), (h, 3, 384)]
            else:
                groups = [(h, 1, 0), (h + 1, 1, 256)] if not by_key else [(h, 2, 0), (h + 1, 2, 256)]
            for head, blk, col in groups:
                if by_key:
                    w = SEQ - blk * P
                    pe.matmul(bank[:, col:col + w], lhsT=KT[0:K_ROWS, head, blk * P:(blk + 1) * P],
                              rhs=QT[0:K_ROWS, head, blk * P:], start=True, stop=False)
                    last = pe.matmul(bank[:, col:col + P], lhsT=identb[:], rhs=mask_k[:], start=False, stop=True)
                else:
                    w = (blk + 1) * P
                    pe.matmul(bank[:, col:col + w], lhsT=QT[0:QK_ROWS, head, blk * P:(blk + 1) * P],
                              rhs=KT[0:QK_ROWS, head, 0:w], start=True, stop=False)
                    last = pe.matmul(bank[:, col + w - P:col + w], lhsT=identb[:], rhs=mask_q[:], start=False, stop=True)
            last.then_inc(S["s_st" if by_key else "s_S"], 1)

        def prob_block(h, blk):
            slot, k = (h // 2) % 3, h % 2
            if blk == 0:
                return probs[:, slot, 2 * k, :]
            if blk == 1:
                return probs[:, slot, 2 * k + 1, 0:384]
            if blk == 3:
                return probs[:, slot, 2 * k + 1, 384:512]
            return probs[:, slot, 4, 256 * k:256 * k + 256]

        @block.tensor
        def _(pe):
            def transposes(bank, src, done):
                for q in range(Q):
                    last = pe.transpose(bank[:, q * P:(q + 1) * P], src[:, q], ident[:])
                last.then_inc(S[done], 1)

            def f_turn_x(f):
                pe.wait_ge(S["s_lnf"], f + 1)
                pe.wait_ge(S["s_sil"], U0 * f)
                transposes(fa[0], f_n, "s_T1")

            def f_kvq(f, half):
                pe.wait_ge(S["s_nT1"], f + 1)
                for q in range(2 * half, 2 * half + 2):
                    if q == 0:
                        pe.wait_ge(S["s_hs"], SHARED * f)
                    if q == 3:
                        pe.wait_ge(S["s_kvqe"], Q * f + 1)
                    pe.matmul(fa[(q + 1) % 3][:, 0:3 * D], lhsT=f_nT[:, q * P:(q + 1) * P], rhs=w_kvq[:],
                              start=True, stop=True).then_inc(S["s_kvq"], 1)

            def f_kv(f):
                pe.wait_ge(S["s_kqn"], f + 1)
                pe.wait_ge(S["s_kvqe"], Q * f + Q)
                for q in range(Q):
                    last = pe.matmul(fa[2][:, 0:P], lhsT=kvq[:, q, D:2 * D], rhs=kvq[:, q, 0:D], start=q == 0, stop=q == Q - 1)
                last.then_inc(S["s_kvt"], 1)
                for q in range(Q):
                    last = pe.transpose(fa[0][:, q * P:(q + 1) * P], kvq[:, q, 2 * D:3 * D], ident[:])
                last.then_inc(S["s_qT"], 1)

            def f_kvo(f):
                pe.wait_ge(S["s_kvm"], f + 1)
                pe.matmul(fa[1][:, 0:D], lhsT=kvm[:], rhs=w_o0[:], start=True, stop=True).then_inc(S["s_kvo"], 1)

            def f_out(f):
                pe.wait_ge(S["s_qnT"], f + 1)
                pe.wait_ge(S["s_kvoc"], f + 1)
                for q in range(Q):
                    last = pe.matmul(fa[2][:, q * D:(q + 1) * D], lhsT=qnT[:, q * P:(q + 1) * P], rhs=kvo[:], start=True, stop=True)
                last.then_inc(S["s_at0"], 1)

            def f_turn_x1(f):
                pe.wait_ge(S["s_x1n"], f + 1)
                transposes(fa[0], f_n, "s_T2")

            def f_gate(f):
                pe.wait_ge(S["s_nT2"], f + 1)
                for q in range(Q):
                    last = pe.matmul(fa[1][:, q * E0:(q + 1) * E0], lhsT=f_nT[:, q * P:(q + 1) * P], rhs=gate_w[:], start=True, stop=True)
                last.then_inc(S["s_lgm"], 1)

            def f_turn_gates(f):
                pe.wait_ge(S["s_gp"], f + 1)
                apart(pe)
                for q in range(Q):
                    last = pe.transpose(fa[2][:].bitcast(BF16)[0:PARTS * E0, q * P:(q + 1) * P],
                                        gparts[:, q].rearrange("p c e -> p (c e)"), identb[:])
                last.then_inc(S["s_gTp"], 1)

            def up(b, e):
                if e == 0:
                    pe.wait_ge(S["s_exf"], b + 1)
                else:
                    pe.wait_ge(S["s_sil"], U0 * b + e)
                pe.matmul(fa[0][:], lhsT=w1[:, e], rhs=f_nT[:], start=True, stop=True).then_inc(S["s_h1"], 1)

            def gate_rows(b, e):
                if e == 0:
                    pe.wait_ge(S["s_gT"], b + 1)
                else:
                    pe.wait_ge(S["s_gbc"], E0 * b + e)
                pe.matmul(fa[2][:], lhsT=pick[:, e], rhs=gT[:], start=True, stop=True).then_inc(S["s_gb"], 1)

            def up3(b, e):
                if 0 < e <= E0:
                    pe.wait_ge(S["s_t"], E0 * b + e)
                elif e > E0:
                    pe.wait_ge(S["s_hs"], SHARED * b + e - E0)
                pe.matmul(fa[1][:], lhsT=w3[:, e], rhs=f_nT[:], start=True, stop=True).then_inc(S["s_h3"], 1)

            def down(b, e):
                if e < E0:
                    pe.wait_ge(S["s_h"], E0 * b + e + 1)
                else:
                    pe.wait_ge(S["s_hs"], SHARED * b + e - E0 + 1)
                if e == 0:
                    pe.wait_ge(S["s_yT"], b)
                    pe.wait_ge(S["s_vp"], b)
                pe.matmul(facc[:], lhsT=w2[:, e], rhs=hh[:, e % 2], start=e == 0, stop=e == U0 - 1).then_inc(S["s_ym"], 1)

            def r_turn(r):
                if isinstance(r, int) and r == 0:
                    pe.wait_ge(S["s_wback"], BW)
                pe.wait_ge(S["s_lnb"], r + 1)
                transposes(facc, b_n, "s_T3")

            def r_q(r):
                pe.wait_ge(S["s_nT3"], r + 1)
                pe.matmul(facc[:], lhsT=w_q1[:], rhs=b_nT[:], start=True, stop=True).then_inc(S["s_q"], 1)

            def r_k(r):
                pe.wait_ge(S["s_r1"], 2 * r + 1)
                pe.matmul(facc[:], lhsT=w_k1[:], rhs=b_nT[:], start=True, stop=True).then_inc(S["s_k"], 1)

            def r_v(r):
                pe.wait_ge(S["s_r1"], 2 * r + 2)
                for q in range(Q):
                    last = pe.matmul(facc[:, q * D:(q + 1) * D], lhsT=b_nT[:, q * P:(q + 1) * P], rhs=w_v1[:], start=True, stop=True)
                last.then_inc(S["s_v"], 1)

            def t_turn(t):
                pe.wait_ge(S["s_norm"], 4 * t + 4)
                transposes(bo, ao, "s_aTt")

            def t_out(t):
                pe.wait_ge(S["s_aT"], t + 1)
                for q in range(Q):
                    last = pe.matmul(bo[:, q * D:(q + 1) * D], lhsT=b_nT[:, q * P:(q + 1) * P], rhs=w_o1[:], start=True, stop=True)
                last.then_inc(S["s_wo"], 1)

            def t_turn_row(t):
                pe.wait_ge(S["s_row"], t + 1)
                for q in range(Q):
                    last = pe.transpose(bo[:, q * P:(q + 1) * P], row[:, q, 0:D], ident[:])
                last.then_inc(S["s_T4"], 1)

            def t_router(t):
                pe.wait_ge(S["s_nT4"], t + 1)
                for q in range(Q):
                    last = pe.matmul(bo[:, q * E1:(q + 1) * E1], lhsT=b_nT[:, q * P:(q + 1) * P], rhs=router_w[:], start=True, stop=True)
                last.then_inc(S["s_l1"], 1)

            T_STEPS = {1: t_turn, 2: t_out, 8: t_turn_row, 9: t_router}

            def turn_maxima(b, half):
                pe.wait_ge(S["s_nmp"], 2 * b + half + 1)
                if half == 0:
                    pe.wait_ge(S["s_l1c"], b)
                else:
                    pe.wait_ge(S["s_nmT"], 2 * b + 1)
                apart(pe)
                for q in range(Q):
                    last = pe.transpose(bo[:].bitcast(BF16)[0:PARTS * HEADS // 2, q * P:(q + 1) * P],
                                        nmp[:, half, q].rearrange("p c h -> p (c h)"), identb[:])
                last.then_inc(S["s_nmt"], 1)

            def x_phase(f, b, t, g):
                def fill(n):
                    if b is None:
                        return
                    if n == 0:
                        pe.wait_ge(S["s_qk0"], 16 * 2 * PARTS * PARTS * (b + 1))
                        pe.wait_ge(S["s_exp"], FILLS * b)
                    if n == FILLS // 2:
                        pe.wait_ge(S["s_qk1"], 16 * 2 * PARTS * PARTS * (b + 1))
                    if n >= 3:
                        pe.wait_ge(S["s_red"], FILLS * b + n - 2)
                    scores(pe, b, n, False)

                if isinstance(f, int) and f == 0:
                    pe.wait_ge(S["s_wexperts"], EW)
                fill(0)
                if f is not None:
                    up(f, 0)
                fill(1)
                if f is not None:
                    up3(f, 0)
                fill(2)
                if f is not None:
                    f_turn_gates(f)
                for e in range(U0):
                    fills = iter(fills_of[e])

                    def next_fill():
                        n = next(fills, None)
                        if n is not None:
                            fill(n)

                    next_fill()
                    if f is not None and e + 1 < U0:
                        up(f, e + 1)
                    if f is not None and e == 0:
                        gate_rows(f, 0)
                    next_fill()
                    next_fill()
                    if f is not None and e + 1 < U0:
                        up3(f, e + 1)
                    if f is not None and e + 1 < E0:
                        gate_rows(f, e + 1)
                    if t is not None and e in T_STEPS:
                        T_STEPS[e](t)
                    if f is not None and e > 0:
                        down(f, e - 1)
                    next_fill()
                if b is not None:
                    turn_maxima(b, 0)
                if f is not None:
                    down(f, U0 - 1)
                if g is not None:
                    f_turn_x(g)
                if f is not None:
                    pe.wait_ge(S["s_yT"], f + 1)
                    for q in range(Q):
                        last = pe.transpose(facc[:, q * P:(q + 1) * P], yT[:, q * P:(q + 1) * P], ident[:])
                    last.then_inc(S["s_yTt"], 1)

            def y_phase(b, f, r, t):
                def pair_scores(pair, between=None):
                    if pair == 0:
                        pe.wait_ge(S["s_mx0"], 16 * PARTS * (b + 1))
                        pe.wait_ge(S["s_red"], FILLS * (b + 1))
                    if pair == HEADS // 4:
                        pe.wait_ge(S["s_mx1"], 16 * PARTS * (b + 1))
                    for n in range(5 * pair, 5 * pair + 5):
                        if between and n == 5 * pair + 3:
                            between()
                        if n >= 3:
                            pe.wait_ge(S["s_exp"], FILLS * b + n - 2)
                        scores(pe, b, n, True)

                def outputs(k):
                    pe.wait_ge(S["s_exp"], FILLS * b + 10 * k + 10)
                    if k == 0:
                        pe.wait_ge(S["s_nmT"], 2 * b + 2)
                    else:
                        pe.wait_ge(S["s_norm"], 4 * b + k)
                    for blk in range(Q):
                        for j in range(4):
                            last = pe.matmul(bo[32 * j:32 * j + 32, blk * P:], lhsT=vp[:, blk, 4 * k + j],
                                             rhs=prob_block(4 * k + j, blk), start=blk == 0, stop=blk == Q - 1)
                    last.then_inc(S["s_pv"], 1)

                def turn_outputs(k):
                    pe.wait_ge(S["s_oT"], 4 * b + k + 1)
                    for q in range(Q):
                        last = pe.transpose(bo[:, q * P:(q + 1) * P], oT[:, q * P:(q + 1) * P], ident[:])
                    last.then_inc(S["s_tr"], 1)

                def if_b(step, *args):
                    if b is not None:
                        step(*args)

                def if_f(step):
                    if f is not None:
                        step(f)

                def if_r(step):
                    if r is not None:
                        step(r)

                if_b(lambda: turn_maxima(b, 1))
                if_f(lambda f: f_kvq(f, 0))
                if b is None:
                    if_f(lambda f: f_kvq(f, 1))
                    if_r(r_turn)
                    if_r(r_q)
                else:
                    pair_scores(0, lambda: if_f(lambda f: f_kvq(f, 1)))
                    if_r(r_turn)
                    pair_scores(1, lambda: if_r(r_q))
                    pair_scores(2)
                if_r(r_k)
                if b is not None:
                    outputs(0)
                    pair_scores(3, lambda: turn_outputs(0))
                if_f(f_kv)
                if b is None:
                    if_f(f_kvo)
                    if_f(f_out)
                    if_f(f_turn_x1)
                else:
                    pair_scores(4, lambda: if_f(f_kvo))
                    outputs(1)
                    if_f(f_out)
                    pair_scores(5, lambda: turn_outputs(1))
                    pair_scores(6)
                    outputs(2)
                    pair_scores(7, lambda: if_f(f_turn_x1))
                    turn_outputs(2)
                if_f(f_gate)
                if_r(r_v)
                if b is not None:
                    outputs(3)
                    turn_outputs(3)

            pe.wait_ge(S["s_wfront"], FW)
            pe.wait_ge(S["s_one"], 1)
            looped(pe, x_phase, y_phase)
            pe.wait_ge(S["s_gj"], 1)
            for g in range(8):
                last = pe.transpose(fa[g // 4][:, (g % 4) * P:(g % 4 + 1) * P], logits_gj[:, g], ident[:])
            last.then_inc(S["s_LTt"], 1)

            def across(col, pattern, src, ready, n, done):
                pe.wait_ge(S[ready], n)
                pe.matmul(fa[2][:, col:col + src.shape[-1]], lhsT=pattern[:], rhs=src[:], start=True, stop=True).then_inc(S[done], 1)

            with pe.Fori(0, 8) as i:
                pe.wait_ge(S["s_cnt3"], i + 1)
                across(0, same_e, cnts, "s_cnt", i + 1, "s_tot")
            across(0, same_e, cnt, "s_gth", 1, "s_gthc")
            with pe.Fori(8, 16) as i:
                pe.wait_ge(S["s_cnt3"], i + 1)
                across(0, same_e, cnts, "s_cnt", i + 1, "s_tot")
            across(0, same_e, cnt, "s_gtc", 1, "s_gtt")
            across(0, earlier_e, cnt, "s_gtc", 2, "s_gtt")
            across(0, earlier_e, cnt, "s_gtc", 3, "s_gtt")
            pe.wait_ge(S["s_rc"], 1)
            for g in range(8):
                last = pe.transpose(fa[g // 4][:, (g % 4) * P:(g % 4 + 1) * P], place[:, g * P:(g + 1) * P], ident[:])
            last.then_inc(S["s_slT"], 1)
            lists_of = [ba[0], ba[1], ba[2], bo]
            for half in range(2):
                pe.wait_ge(S["s_hot"], half + 1)
                for c in range(half * W // 2, (half + 1) * W // 2, 4):
                    last = pe.matmul(lists_of[c // 4 % 4][:, 0:P], lhsT=hot_hi[:, c // 4].rearrange("p h e -> p (h e)"),
                                     rhs=hot_lo[:, :, :, c:c + 4].rearrange("p w l e -> p w e l"),
                                     start=c < E1, stop=c >= W - E1)
            last.then_inc(S["s_list"], 1)

            def pe_turn(e, k):
                pe.wait_ge(S[f"s_got{k}"], 8 * CC * (e - k + 2))
                for c in range(CC):
                    last = pe.transpose(fa[0][:, c * P:(c + 1) * P], got[k][:, c, 0:D], ident[:])
                last.then_inc(S["s_xet"], 1)

            def pe_expert(e, k, more=True):
                pe.wait_ge(S["s_xe"], e + 1)
                pe.wait_ge(S[f"s_fw{k}"], 24 * (e - k + 2))
                pe.wait_ge(S["s_hT"], FC * e)
                for f in range(FC):
                    pe.matmul([fa[1], fa[2], ba[0], ba[1]][f][:], lhsT=fc1[k][:, f * P:(f + 1) * P], rhs=xe[k][:], start=True, stop=True)\
                      .then_inc(S["s_up"], 1)
                if more:
                    pe_turn(e + 1, 1 - k)
                pe.wait_ge(S["s_hT"], FC * e + FC)
                pe.wait_ge(S["s_ys"], e)
                for c in range(CC):
                    for f in range(FC):
                        last = pe.matmul(ba[2][:, c * D:(c + 1) * D], lhsT=hT[k][:, f, c * P:(c + 1) * P], rhs=fc2[k][:, f], start=f == 0, stop=f == FC - 1)
                last.then_inc(S["s_dn"], 1)

            pe.wait_ge(S["s_diag"], 4)
            pe_turn(0, 0)
            with pe.Fori(0, E1 // 2 - 1) as i:
                pe_expert(2 * i, 0)
                pe_expert(2 * i + 1, 1)
            pe_expert(E1 - 2, 0)
            pe_expert(E1 - 1, 1, False)

        @block.scalar
        def _(act):
            def copy(dst, src, ready, n, done):
                act.wait_ge(S[ready], n)
                act.activation(dst, src, ACT.Copy).then_inc(S[done], 1)

            act.wait_ge(S["s_wfront"], FW)
            act.activation(inv_scaling[:], m_b[:], ACT.Exp, scale=-1.0).then_inc(S["s_scal"], 1)
            act.wait_ge(S["s_scal"], 3)
            act.activation(inv_scaling[:], inv_scaling[:], ACT.Exp, scale=-float(np.log(SEQ))).then_inc(S["s_scal"], 1)

            def x_phase(f, b, t, g):
                for e in range(U0):
                    if f is not None:
                        act.wait_ge(S["s_h1"], U0 * f + e + 1)
                        if e < 2:
                            act.wait_ge(S["s_hs"], SHARED * f)
                        else:
                            act.wait_ge(S["s_t"], E0 * f + e - 1)
                        act.activation(sil[:, e % 2], fa[0][:], ACT.Silu).then_inc(S["s_sil"], 1)
                    if f is not None and e == 0:
                        copy(gT[0:PARTS * E0, :], fa[2][:].bitcast(BF16)[0:PARTS * E0, 0:SEQ], "s_gTp", f + 1, "s_gT")
                    if f is not None and e < E0:
                        act.wait_ge(S["s_h"], E0 * f + max(e - 1, 0))
                        copy(gb[:, e % 2], fa[2][:], "s_gb", E0 * f + e + 1, "s_gbc")
                    if t is not None:
                        if e == 1:
                            copy(b_nT[:], bo[:], "s_aTt", t + 1, "s_aT")
                        if e == 5:
                            act.wait_ge(S["s_y"], t + 1)
                            for q in range(Q):
                                act.activation(b_n[:, q], row[:, q, 0:D], ACT.Square, accum_out=ysq[:, q:q + 1]).then_inc(S["s_ysq"], 1)
                        if e == 9:
                            copy(b_nT[:], bo[:], "s_T4", t + 1, "s_nT4")
                if b is not None:
                    copy(nmT[:, 0], bo[:].bitcast(BF16)[0:PARTS * HEADS // 2, 0:SEQ], "s_nmt", 2 * b + 1, "s_nmT")
                if f is not None:
                    copy(yT[:], facc[:], "s_ym", U0 * f + U0, "s_yT")
                if g is not None:
                    copy(f_nT[:], fa[0][:], "s_T1", g + 1, "s_nT1")

            def y_phase(b, f, r, t):
                def exps(pair):
                    if b is None:
                        return
                    for f_ in range(5):
                        n = 5 * pair + f_
                        act.wait_ge(S["s_st"], FILLS * b + n + 1)
                        if f_ == 0:
                            act.wait_ge(S["s_pv"], 4 * b + max(pair - 1, 0) // 2)
                        act.activation(probs[:, pair % 3, f_], ba[n % 3][:], ACT.Exp, scale=SCALE).then_inc(S["s_exp"], 1)

                if t is not None:
                    act.wait_ge(S["s_l1x"], t + 1)
                    act.activation(l1[:], l1[:], ACT.Exp).then_inc(S["s_ex1"], 1)
                if b is not None:
                    copy(nmT[:, 1], bo[:].bitcast(BF16)[0:PARTS * HEADS // 2, 0:SEQ], "s_nmt", 2 * b + 2, "s_nmT")
                exps(0)
                if r is not None:
                    copy(b_nT[:], facc[:], "s_T3", r + 1, "s_nT3")
                if f is not None:
                    act.wait_ge(S["s_kvqe"], Q * f + Q)
                    act.activation(sq[:].rearrange("p q (w d) -> p q w d", w=2), kvq[:].rearrange("p q (w d) -> p q w d", w=3)[:, :, 0:3:2],
                                   ACT.Square).then_inc(S["s_sq"], 1)
                exps(1)
                if r is not None:
                    act.wait_ge(S["s_qkw"], 32 * r)
                    copy(qkp[:, 0, 0], facc[:], "s_q", r + 1, "s_p1")
                exps(2)
                if r is not None:
                    copy(qkp[:, 1, 0], facc[:], "s_k", r + 1, "s_p1")
                exps(3)
                if f is not None:
                    copy(qnT[:], fa[0][:], "s_qT", f + 1, "s_qnT")
                exps(4)
                if f is not None:
                    copy(kvo[:], fa[1][:, 0:D], "s_kvo", f + 1, "s_kvoc")
                exps(5)
                exps(6)
                if f is not None:
                    copy(f_nT[:], fa[0][:], "s_T2", f + 1, "s_nT2")
                exps(7)
                if f is not None:
                    act.wait_ge(S["s_lgx"], f + 1)
                    act.activation(sc[:], lg[:], ACT.Exp).then_inc(S["s_exf"], 1)
                if r is not None:
                    act.wait_ge(S["s_pv"], 4 * r)
                    copy(vp[:, :, :, 0:HD], facc[:].rearrange("p (q h d) -> p q h d", q=Q, h=HEADS), "s_v", r + 1, "s_vp")
            looped(act, x_phase, y_phase)
            act.wait_ge(S["s_prob"], BATCH)
            act.wait_ge(S["s_rowd"], 16 * BATCH)
            for first, data in ((0, high16), (8, low16)):
                with act.Fori(first, first + 8) as i:
                    act.wait_ge(S["s_cand"], i + 1)
                    act.activation(signs[:], data[:], ACT.Sign, bias=minus3[:], accum_out=cnts[:, 2:3]).then_inc(S["s_cnt3"], 1)
            act.wait_ge(S["s_fb"], 16)

            def turned(e, k):
                act.activation(fb1c[k][:], fb1[:, e], ACT.Copy).then_inc(S["s_bc1"], 1)
                copy(xe[k][:], fa[0][:], "s_xet", e + 1, "s_xe")

            def act_expert(e, k, more=True):
                act.wait_ge(S["s_bc1"], e + 1)
                for f in range(FC):
                    act.wait_ge(S["s_up"], FC * e + f + 1)
                    act.activation(hT[k][:, f], [fa[1], fa[2], ba[0], ba[1]][f][:], ACT.Gelu, bias=fb1c[k][:, f:f + 1]).then_inc(S["s_hT"], 1)
                if more:
                    turned(e + 1, 1 - k)

            turned(0, 0)
            with act.Fori(0, E1 // 2 - 1) as i:
                act_expert(2 * i, 0)
                act_expert(2 * i + 1, 1)
            act_expert(E1 - 2, 0)
            act_expert(E1 - 1, 1, False)
            n = TILES // 4
            for k in range(4):
                act.wait_ge(S["s_gsum"], k + 1)
                for m in range(k * n + n // 2, (k + 1) * n):
                    last = act.activation(sums[:, m, 0:D], sums[:, m, 0:D], ACT.Copy, scale=gsum[:, m:m + 1])
                last.then_inc(S["s_scaled"], 1)

        @block.vector
        def _(dve):
            class Steps:

                def __init__(self, name, per_batch):
                    self.sem, self.per, self.n, self.b, self.paired = S[name], per_batch, 0, 0, False

                def start(self, b):
                    assert self.n in (0, self.per), self.n
                    self.b, self.n = b, 0

                def __call__(self, ins, wait=True):
                    self.n += 1
                    ins.then_inc(self.sem, 1)
                    if wait:
                        dve.wait_ge(self.sem, self.b * self.per + self.n)
                        apart(dve)

                def last(self):
                    dve.wait_ge(self.sem, self.b * self.per + self.n)
                    apart(dve)

                def halves(self, op):
                    for half in range(2):
                        if self.paired or half:
                            dve.wait_ge(self.sem, self.b * self.per + self.n - 1)
                            apart(dve)
                        self.n += 1
                        op(slice(half * Q // 2, (half + 1) * Q // 2)).then_inc(self.sem, 1)
                    self.paired = True

                def join(self):
                    self.paired = False
                    dve.wait_ge(self.sem, self.b * self.per + self.n)
                    apart(dve)

            fc, mc, rc, tc = Steps("s_fc", 67), Steps("s_mstep", 6), Steps("s_rstep", 8), Steps("s_tc", 11)

            def stats(step, x, st, mv):
                for q in range(Q):
                    step(dve.bn_stats(st[:, q], x[:, q]), q == Q - 1)
                for q in range(Q):
                    step(dve.bn_aggr(mv[:, q], st[:, q]), q == Q - 1)

            def center(dst, x, mv, rs, done):
                for q in range(Q):
                    last = dve.tensor_scalar(dst(q), x[:, q], mv[:, q, 0:1], rs[:, q:q + 1], ALU.subtract, ALU.mult)
                last.then_inc(S[done], 1)

            dve.memset(vp[:], 0.0).then_inc(S["s_pad"], 1)
            dve.memset(KT[64:96], 1.0).then_inc(S["s_pad"], 1)
            dve.wait_ge(S["s_pad"], 2)
            dve.memset(vp[:, :, :, HD:HD + 1], 1.0).then_inc(S["s_pad"], 1)
            dve.wait_ge(S["s_wfront"], FW)
            dve.wait_ge(S["s_scal"], 1)
            dve.tensor_scalar(inv_scaling[:], inv_scaling[:], 1.0, None, ALU.add).then_inc(S["s_scal"], 1)
            dve.wait_ge(S["s_scal"], 2)
            dve.reciprocal(inv_scaling[:], inv_scaling[:]).then_inc(S["s_scal"], 1)
            dve.wait_ge(S["s_scal"], 4)
            dve.wait_ge(S["s_one"], 1)
            dve.tensor_tensor(kv_scale[:], blockdiag[:], inv_scaling[:, :, None].to_broadcast([P, HEADS, HD]), ALU.mult).then_inc(S["s_scal"], 1)
            dve.wait_ge(S["s_scal"], 5)

            def f_norm(f):
                fc.start(f)
                dve.wait_ge(S["s_x"], 16 * f + 16)
                stats(fc, xin, f_st, f_mv)
                dve.tensor_scalar(f_ve[:, 0:Q], f_mv[:, :, 1], EPS, None, ALU.add).then_inc(S["s_varf"], 1)

            def f_center(f):
                dve.wait_ge(S["s_rsf"], 2 * f + 1)
                center(lambda q: f_n[:, q], xin, f_mv, f_rs, "s_lnf")

            def f_bias(f, half):
                for q in range(2 * half, 2 * half + 2):
                    dve.wait_ge(S["s_kvq"], Q * f + q + 1)
                    dve.tensor_tensor(kvq[:, q], fa[(q + 1) % 3][:, 0:3 * D], b_kvq[:], ALU.add).then_inc(S["s_kvqe"], 1)

            def f_l2(f):
                dve.wait_ge(S["s_sq"], f + 1)
                fc.halves(lambda q: dve.tensor_reduce(n2[:, q], sq[:, q].rearrange("p q (g d) -> p (q g) d", d=HD), X, ALU.add))
                fc.halves(lambda q: dve.tensor_scalar(n2[:, q], n2[:, q], L2_EPS_SQ, None, ALU.max))
                fc.halves(lambda q: dve.tensor_scalar(rn[:, q].bitcast(I32), n2[:, q].bitcast(I32), -0.5, float(0x5F3759DF), ALU.mult, ALU.add))
                f_newton(1)

            def f_newton(steps):
                for _ in range(steps):
                    fc.halves(lambda q: dve.scalar_tensor_tensor(rt[:, q], n2[:, q], -0.5, rn[:, q], ALU.mult, ALU.mult))
                    fc.halves(lambda q: dve.tensor_tensor(rt[:, q], rt[:, q], rn[:, q], ALU.mult))
                    fc.halves(lambda q: dve.scalar_tensor_tensor(rn[:, q], rt[:, q], 1.5, rn[:, q], ALU.add, ALU.mult))

            def f_scale(f):
                f_newton(2)
                fc.join()
                for w in range(2):
                    heads = kvq[:, :, 2 * w * D:(2 * w + 1) * D].rearrange("p q (h d) -> p q h d", d=HD)
                    last = dve.tensor_tensor(heads, heads, rn[:, :, w * HEADS:(w + 1) * HEADS, None].to_broadcast([P, Q, HEADS, HD]), ALU.mult)
                last.then_inc(S["s_kqn"], 1)

            def f_kvm(f):
                dve.wait_ge(S["s_kvt"], f + 1)
                dve.tensor_tensor(kvm[:], fa[2][:, 0:P], kv_scale[:].rearrange("p h d -> p (h d)"), ALU.mult).then_inc(S["s_kvm"], 1)

            def f_x1(f):
                dve.wait_ge(S["s_at0"], f + 1)
                dve.wait_ge(S["s_xres"], f + 1)
                dve.tensor_tensor(x1[:], fa[2][:].rearrange("p (q d) -> p q d", q=Q), xres[:], ALU.add).then_inc(S["s_x1"], 1)
                dve.wait_ge(S["s_x1"], f + 1)
                apart(dve)
                stats(fc, x1, f_st, f_mv)
                dve.tensor_scalar(f_ve[:, 0:Q], f_mv[:, :, 1], EPS, None, ALU.add).then_inc(S["s_varf"], 1)
                dve.wait_ge(S["s_rsf"], 2 * f + 2)
                center(lambda q: f_n[:, q], x1, f_mv, f_rs, "s_x1n")

            def f_logits(f):
                dve.wait_ge(S["s_lgm"], f + 1)
                dve.tensor_copy(lg[:], fa[1][:, 0:Q * E0].rearrange("p (q e) -> p q e", q=Q)).then_inc(S["s_lge"], 1)
                dve.wait_ge(S["s_lge"], f + 1)
                fc(dve.tensor_reduce(lm[:], lg[:], X, ALU.max))
                dve.tensor_tensor(lg[:], lg[:], lm[:, :, None].to_broadcast([P, Q, E0]), ALU.subtract).then_inc(S["s_lgx"], 1)

            def f_gates(f):
                dve.wait_ge(S["s_exf"], f + 1)
                bc = lambda t, q: t[:, q, :, None].to_broadcast([P, Q // 2, E0, E0])
                fc.halves(lambda q: dve.tensor_reduce(ls[:, q], sc[:, q], X, ALU.add))
                fc.halves(lambda q: dve.reciprocal(ls[:, q], ls[:, q]))
                fc.halves(lambda q: dve.tensor_tensor(sc[:, q], sc[:, q], ls[:, q, None].to_broadcast([P, Q // 2, E0]), ALU.mult))
                fc.halves(lambda q: dve.tensor_tensor(bs[:, q], sc[:, q], gate_b[:, None, :].to_broadcast([P, Q // 2, E0]), ALU.add))
                others = lambda q: bs[:, q, None, :].to_broadcast([P, Q // 2, E0, E0])
                fc.halves(lambda q: dve.tensor_tensor(eq[:, q], others(q), bc(bs, q), ALU.is_equal))
                fc.halves(lambda q: dve.tensor_tensor(gt[:, q], others(q), bc(bs, q), ALU.is_gt))

            def f_rank(f):
                fc.halves(lambda q: dve.tensor_tensor(eq[:, q], eq[:, q], below[:, None].to_broadcast([P, Q // 2, E0, E0]), ALU.mult))
                fc.halves(lambda q: dve.tensor_tensor(gt[:, q], gt[:, q], eq[:, q], ALU.add))
                fc.halves(lambda q: dve.tensor_reduce(rank[:, q], gt[:, q], X, ALU.add))
                fc.halves(lambda q: dve.scalar_tensor_tensor(gates[:, q], rank[:, q], TOPK - 0.5, sc[:, q], ALU.is_lt, ALU.mult))
                fc.halves(lambda q: dve.tensor_copy(gparts[:, q, 0], gates[:, q]))
                fc.halves(lambda q: dve.tensor_tensor(gres[:, q], gates[:, q], gparts[:, q, 0], ALU.subtract))
                fc.halves(lambda q: dve.tensor_copy(gparts[:, q, 1], gres[:, q]))
                fc.join()
                dve.tensor_tensor(gparts[:, :, 2], gres[:], gparts[:, :, 1], ALU.subtract).then_inc(S["s_gp"], 1)

            def product(f, e):
                dve.wait_ge(S["s_sil"], U0 * f + e + 1)
                dve.wait_ge(S["s_h3"], U0 * f + e + 1)
                if e < E0:
                    dve.wait_ge(S["s_h"], E0 * f + max(e - 1, 0))
                    dve.tensor_tensor(th[:, e % 2], sil[:, e % 2], fa[1][:], ALU.mult).then_inc(S["s_t"], 1)
                else:
                    dve.wait_ge(S["s_ym"], U0 * f + e - 1)
                    dve.tensor_tensor(hh[:, e % 2], sil[:, e % 2], fa[1][:], ALU.mult).then_inc(S["s_hs"], 1)

            def maxima(b, n):
                pair, f = divmod(n, 5)
                h, bank = 2 * pair + (f // 2 if f < 4 else 0), ba[n % 3]
                dve.wait_ge(S["s_S"], FILLS * b + n + 1)
                if f in (0, 2):
                    last = dve.tensor_reduce(nm[:, 3, h:h + 1], bank[:], X, ALU.max, negate=True)
                elif f in (1, 3):
                    dve.tensor_reduce(nm[:, 2, h:h + 1], bank[:, 0:384], X, ALU.max, negate=True)
                    last = dve.tensor_reduce(nm[:, 0, h:h + 1], bank[:, 384:512], X, ALU.max, negate=True)
                else:
                    last = dve.tensor_reduce(nm[:, 1, h:h + 2], bank[:].rearrange("p (h k) -> p h k", h=2), X, ALU.max, negate=True)
                last.then_inc(S["s_red"], 1)

            def x3_of(b):
                return x3[:, b * Q:(b + 1) * Q] if isinstance(b, int) else x3[:, bass.ts(b, Q)]

            def t_x3(t):
                tc.start(t)
                dve.wait_ge(S["s_wo"], t + 1)
                x3t = x3_of(t)
                dve.tensor_tensor(x3t, bo[:].rearrange("p (q d) -> p q d", q=Q), x3t, ALU.add).then_inc(S["s_x3"], 1)

            def t_stats(t):
                dve.wait_ge(S["s_x3"], t + 1)
                apart(dve)
                stats(tc, x3_of(t), b_st, b_mv)
                dve.tensor_scalar(b_ve[:], b_mv[:, :, 1], EPS, None, ALU.add).then_inc(S["s_vart"], 1)

            def t_center(t):
                dve.wait_ge(S["s_rst"], 2 * t + 1)
                dve.wait_ge(S["s_rowd"], 16 * t)
                center(lambda q: row[:, q, 0:D], x3_of(t), b_mv, b_rs, "s_y")

            def t_square(t):
                dve.wait_ge(S["s_ysq"], Q * t + Q)
                dve.tensor_scalar(b_ve[:], ysq[:], 1.0 / D, EPS, ALU.mult, ALU.add).then_inc(S["s_vart"], 1)

            def t_rms(t):
                dve.wait_ge(S["s_rst"], 2 * t + 2)
                dve.wait_ge(S["s_y"], t + 1)
                for q in range(Q):
                    last = dve.scalar_tensor_tensor(row[:, q, 0:D], row[:, q, 0:D], b_rs[:, q:q + 1], norm_w[:], ALU.mult, ALU.mult)
                last.then_inc(S["s_row"], 1)

            def t_logits(t):
                dve.wait_ge(S["s_l1"], t + 1)
                lb = logits_flat[:, t * Q:(t + 1) * Q] if isinstance(t, int) else logits_flat[:, bass.ts(t, Q)]
                dve.tensor_tensor(lb, bo[:, 0:Q * E1].rearrange("p (q e) -> p q e", q=Q),
                                  router_b[:, None, :].to_broadcast([P, Q, E1]), ALU.add).then_inc(S["s_l1c"], 1)
                dve.wait_ge(S["s_l1c"], t + 1)
                apart(dve)
                tc(dve.tensor_reduce(l1m[:], lb, X, ALU.max))
                dve.tensor_tensor(l1[:], lb, l1m[:, :, None].to_broadcast([P, Q, E1]), ALU.subtract).then_inc(S["s_l1x"], 1)

            def t_probs(t):
                dve.wait_ge(S["s_ex1"], t + 1)
                tc(dve.tensor_reduce(l1m[:], l1[:], X, ALU.add))
                tc(dve.reciprocal(l1m[:], l1m[:]))
                dve.tensor_tensor(row[:, :, D:], l1[:], l1m[:, :, None].to_broadcast([P, Q, E1]), ALU.mult).then_inc(S["s_prob"], 1)

            T_STEPS = {3: t_x3, 4: t_stats, 5: t_center, 6: t_square, 7: t_rms}

            def x_phase(f, b, t, g):
                def max_parts(half, step):
                    heads = slice(half * HEADS // 2, (half + 1) * HEADS // 2)
                    if step == 0:
                        dve.wait_ge(S["s_red"], FILLS * b + (half + 1) * FILLS // 2)
                        mc(dve.tensor_copy(nmp[:, half, :, 0], nm[:, :, heads]), False)
                    elif step == 1:
                        mc.last()
                        mc(dve.tensor_tensor(nmr[:, :, heads], nm[:, :, heads], nmp[:, half, :, 0], ALU.subtract), False)
                    elif step == 2:
                        mc.last()
                        mc(dve.tensor_copy(nmp[:, half, :, 1], nmr[:, :, heads]), False)
                    else:
                        mc.last()
                        dve.tensor_tensor(nmp[:, half, :, 2], nmr[:, :, heads], nmp[:, half, :, 1], ALU.subtract).then_inc(S["s_nmp"], 1)

                if b is not None:
                    mc.start(b)
                    for n in range(first):
                        maxima(b, n)
                for e in range(U0):
                    if f is not None:
                        product(f, e)
                    if t is not None and e in T_STEPS:
                        T_STEPS[e](t)
                    if g is not None and e == 2:
                        f_norm(g)
                    if g is not None and e == 8:
                        f_center(g)
                    if b is not None:
                        for n in fills_of[e]:
                            maxima(b, n)
                        if 5 <= e < 9:
                            max_parts(0, e - 5)
                if t is not None:
                    t_logits(t)
                if b is not None:
                    for step in range(4):
                        max_parts(1, step)
                if f is not None:
                    dve.wait_ge(S["s_yTt"], f + 1)
                    dve.tensor_tensor(x3_of(f), facc[:].rearrange("p (q d) -> p q d", q=Q), x1[:], ALU.add).then_inc(S["s_x2"], 1)

            def r_norm(r):
                rc.start(r)
                if isinstance(r, int) and r == 0:
                    dve.wait_ge(S["s_wback"], BW)
                dve.wait_ge(S["s_x2"], r + 1)
                apart(dve)
                stats(rc, x3_of(r), b_st, b_mv)
                dve.tensor_scalar(b_ve[:], b_mv[:, :, 1], EPS, None, ALU.add).then_inc(S["s_varb"], 1)

            def r_center(r):
                dve.wait_ge(S["s_rsb"], r + 1)
                center(lambda q: b_n[:, q], x3_of(r), b_mv, b_rs, "s_lnb")

            def r_rest(r, w):
                dve.wait_ge(S["s_p1"], 2 * r + w + 1)
                dve.tensor_tensor(qkr[:, w], facc[:], qkp[:, w, 0], ALU.subtract).then_inc(S["s_r1"], 1)

            def y_phase(b, f, r, t):
                def outputs(k):
                    if b is None:
                        return
                    dve.wait_ge(S["s_pv"], 4 * b + k + 1)
                    dve.tensor_copy(oT[:], bo[:]).then_inc(S["s_oT"], 1)

                def norm(k):
                    if b is None:
                        return
                    dve.wait_ge(S["s_tr"], 4 * b + k + 1)
                    o4 = bo[:].rearrange("p (q j r) -> p q j r", q=Q, j=4)
                    dve.reciprocal(rden[:], o4[:, :, :, HD]).then_inc(S["s_rden"], 1)
                    dve.wait_ge(S["s_rden"], 4 * b + k + 1)
                    dve.tensor_tensor(ao[:, :, 4 * k * HD:4 * (k + 1) * HD].rearrange("p q (j d) -> p q j d", d=HD),
                                      o4[:, :, :, 0:HD], rden[:, :, :, None].to_broadcast([P, Q, 4, HD]), ALU.mult).then_inc(S["s_norm"], 1)

                def if_f(step):
                    if f is not None:
                        step(f)

                def if_r(step, *w):
                    if r is not None:
                        step(r, *w)

                if_r(r_norm)
                if_f(lambda f: f_bias(f, 0))
                if_r(r_center)
                if_f(lambda f: f_bias(f, 1))
                if t is not None:
                    t_probs(t)
                if_f(f_l2)
                if_r(r_rest, 0)
                if_f(f_scale)
                if_r(r_rest, 1)
                outputs(0)
                norm(0)
                if_f(f_kvm)
                outputs(1)
                norm(1)
                if_f(f_x1)
                outputs(2)
                norm(2)
                if_f(f_logits)
                if_f(f_gates)
                outputs(3)
                if_f(f_rank)
                norm(3)

            looped(dve, x_phase, y_phase)
            dve.wait_ge(S["s_prob"], BATCH)
            dve.wait_ge(S["s_rowd"], 16 * BATCH)
            dve.tensor_copy(logits_gj[:].rearrange("p g (j e) -> p g j e", j=GJ),
                            logits_flat[:].rearrange("p (j g) e -> p g j e", g=8)).then_inc(S["s_gj"], 1)
            ks = Steps("s_keys", 9)
            ks.start(0)
            ks(dve.tensor_reduce(own4[:], ident[:].rearrange("p (h e) -> p e h", e=4), X, ALU.add))
            dve.wait_ge(S["s_LTt"], 1)
            ks(dve.tensor_scalar(LT[:, 0:512], fa[0][:], 0.0, None, ALU.add), False)
            ks(dve.tensor_scalar(LT[:, 512:], fa[1][:], 0.0, None, ALU.add))
            dve.wait_ge(S["s_ec"], 6)
            LOW31 = 2 ** 31 - 1
            ks(dve.tensor_scalar(half_i[:], LT[:].bitcast(I32), 31, LOW31, ALU.arith_shift_right, ALU.bitwise_and))
            ks(dve.tensor_tensor(keys[:], LT[:].bitcast(I32), half_i[:], ALU.bitwise_xor))
            ks(dve.tensor_scalar(half_i[:], keys[:], 16, None, ALU.arith_shift_right))
            ks(dve.tensor_copy(high16[:], half_i[:]))
            ks(dve.tensor_scalar(half_i[:], keys[:], 2 ** 16 - 1, None, ALU.bitwise_and))
            ks(dve.tensor_copy(low[:], half_i[:]))
            sr = Steps("s_sr", 3)

            def digits(first, data, key):
                with dve.Fori(first, first + 8) as i:
                    sr.start(i)
                    sr(dve.tensor_scalar(cand[:], steps3[:], step[:], key[:], ALU.mult, ALU.add))
                    dve.tensor_scalar(minus3[:], cand[:, 2:3], -1.0, 0.5, ALU.mult, ALU.add).then_inc(S["s_cand"], 1)
                    for k in range(2):
                        last = dve.tensor_scalar(passed[:, k], data[:], cand[:, k:k + 1], None, ALU.is_ge, ALU.add, accum_out=cnts[:, k:k + 1])
                    last.then_inc(S["s_cnt"], 1)
                    dve.wait_ge(S["s_tot"], i + 1)
                    sr(dve.scalar_tensor_tensor(okm[:], fa[2][:, 0:3], 0.0, targets[:], ALU.add, ALU.is_ge, accum_out=digit[:]))
                    sr(dve.scalar_tensor_tensor(key[:], digit[:], step[:], key[:], ALU.mult, ALU.add))
                    dve.tensor_scalar(step[:], step[:], 0.25, None, ALU.mult).then_inc(S["s_step"], 1)
                    dve.wait_ge(S["s_step"], i + 2 + first // 8)
                    apart(dve)

            def set_targets():
                dve.tensor_scalar(targets[:, 0:2], ones[:, 0:2], target[:], None, ALU.mult).then_inc(S["s_set"], 1)
                dve.tensor_scalar(targets[:, 2:3], target[:], 2.0, -float(TOK), ALU.mult, ALU.add).then_inc(S["s_set"], 1)

            set_targets()
            dve.memset(step[:], 2.0 ** 14).then_inc(S["s_step"], 1)
            dve.wait_ge(S["s_step"], 1)
            digits(0, high16, found_high)
            ls_ = Steps("s_low", 3)
            ls_.start(0)
            dve.tensor_scalar(passed[:, 0], high16[:], found_high[:], None, ALU.is_gt, ALU.add, accum_out=cnt[:]).then_inc(S["s_gth"], 1)
            dve.memset(step[:], 2.0 ** 14).then_inc(S["s_step"], 1)
            dve.wait_ge(S["s_gth"], 1)
            apart(dve)
            ls_(dve.scalar_tensor_tensor(low[:], high16[:], found_high[:], low[:], ALU.is_equal, ALU.mult))
            ls_(dve.tensor_scalar(low16[:], low[:], -2.0 ** 15, None, ALU.add))
            dve.wait_ge(S["s_gthc"], 1)
            ls_(dve.scalar_tensor_tensor(target[:], fa[2][:, 0:1], -1.0, target[:], ALU.mult, ALU.add))
            set_targets()
            dve.wait_ge(S["s_set"], 4)
            dve.wait_ge(S["s_step"], 10)
            digits(8, low16, found_low)
            ec = Steps("s_eqt", 15)
            ec.start(0)
            ec(dve.tensor_copy(thr_hi[:], found_high[:]))
            ec(dve.tensor_scalar(found_low[:], found_low[:], 2.0 ** 15, None, ALU.add))
            ec(dve.tensor_copy(thr_lo[:], found_low[:]))
            ec(dve.scalar_tensor_tensor(bits[:], thr_hi[:], 16, thr_lo[:], ALU.logical_shift_left, ALU.bitwise_or))
            ec(dve.tensor_scalar(flip[:], bits[:], 31, LOW31, ALU.arith_shift_right, ALU.bitwise_and))
            ec(dve.tensor_tensor(bits[:], bits[:], flip[:], ALU.bitwise_xor))
            thr = bits[:].bitcast(F32)
            dve.tensor_scalar(above_t[:], LT[:], thr, None, ALU.is_gt, ALU.add, accum_out=cnt[:]).then_inc(S["s_gtc"], 1)
            ec(dve.tensor_scalar(equal_t[:], LT[:], thr, None, ALU.is_equal, ALU.add, accum_out=off_eq[:]))
            dve.wait_ge(S["s_gtt"], 1)
            ec(dve.tensor_scalar(more[:], fa[2][:, 0:1], -1.0, float(CAP), ALU.mult, ALU.add))
            dve.tensor_copy(cnt[:], off_eq[:]).then_inc(S["s_gtc"], 1)
            dve.wait_ge(S["s_gtt"], 2)
            ec(dve.tensor_copy(off_eq[:], fa[2][:, 0:1]))
            ec(dve.tensor_tensor_scan(place[:], ones[:], equal_t[:], off_eq[:], ALU.mult, ALU.add))
            ec(dve.scalar_tensor_tensor(equal_t[:], place[:], more[:], equal_t[:], ALU.is_le, ALU.mult))
            dve.scalar_tensor_tensor(chosen[:], above_t[:], 0.0, equal_t[:], ALU.add, ALU.add, accum_out=cnt[:]).then_inc(S["s_gtc"], 1)
            dve.wait_ge(S["s_gtt"], 3)
            ec(dve.tensor_copy(off_sel[:], fa[2][:, 0:1]))
            ec(dve.tensor_tensor_scan(place[:], ones[:], chosen[:], off_sel[:], ALU.mult, ALU.add))
            dve.tensor_tensor(place[:], place[:], chosen[:], ALU.mult).then_inc(S["s_rc"], 1)
            dve.wait_ge(S["s_slT"], 1)
            sl = Steps("s_slot", 6)
            slot_i = keys
            for half in range(2):
                sl(dve.tensor_scalar(slot_i[:, half * 512:(half + 1) * 512], fa[half][:], -1.0, None, ALU.add), half == 1)
            sl(dve.tensor_scalar(half_i[:], slot_i[:], 4, None, ALU.arith_shift_right))
            sl(dve.tensor_copy(hi[:], half_i[:]))
            sl(dve.tensor_scalar(half_i[:], slot_i[:], 15, None, ALU.bitwise_and))
            sl(dve.tensor_copy(lo[:], half_i[:]))
            tiles_ = tile_of[:].rearrange("p g j e -> p (g j e)")
            for half in range(2):
                c = slice(half * W // 2, (half + 1) * W // 2)
                for h in range(CAP // 16):
                    dve.tensor_scalar(hot_hi[:, half * W // 8:(half + 1) * W // 8, h], hi[:, c].rearrange("p (n e) -> p n e", e=4),
                                      float(h), None, ALU.is_equal)
                for l in range(16):
                    dve.tensor_scalar(hot_lo[:, 0, l, c], lo[:, c], float(l), pcol[:], ALU.is_equal, ALU.mult)
                    last = dve.scalar_tensor_tensor(hot_lo[:, 1, l, c], lo[:, c], float(l), tiles_[:, c], ALU.is_equal, ALU.mult)
                last.then_inc(S["s_hot"], 1)
            dve.wait_ge(S["s_list"], 1)
            for q, bank in enumerate([ba[0], ba[1], ba[2], bo]):
                dve.tensor_tensor(diag[:, q], bank[:, 0:P].rearrange("p (w e l) -> p w e l", w=2, e=4),
                                  own4[:, None, :, None].to_broadcast([P, 2, 4, 16]), ALU.mult).then_inc(S["s_diag"], 1)
            dve.wait_ge(S["s_diag"], 4)
            dve.tensor_reduce(found[:], diag[:].rearrange("p q w e l -> p (q w) l e"), X, ALU.add).then_inc(S["s_found"], 1)
            dve.wait_ge(S["s_found"], 1)
            dve.scalar_tensor_tensor(idx[:], found[:, :, 1], float(P), found[:, :, 0], ALU.mult, ALU.add).then_inc(S["s_idx"], 1)

            def dve_expert(e, k, refill=True):
                dve.wait_ge(S[f"s_got{k % 2}"], 8 * CC * (e - k % 2 + 2))
                dve.tensor_copy(gate[k % 2][:], got[k % 2][:, :, D + e]).then_inc(S["s_gatec"], 1)
                dve.wait_ge(S["s_dn"], e + 1)
                dve.wait_ge(S[f"s_fw{k % 2}"], 24 * (e - k % 2 + 2))
                dve.tensor_tensor(ysum[k % 2][:], ba[2][:].rearrange("p (c d) -> p c d", c=CC), fb2[k % 2][:, None, :].to_broadcast([P, CC, D]), ALU.add)\
                   .then_inc(S["s_ys"], 1)
                dve.wait_ge(S["s_ys"], e + 1)
                dve.wait_ge(S["s_gatec"], e + 1)
                if not isinstance(e, int) or e >= 2:
                    dve.wait_ge(S["s_sc"], 16 * CC * (e - 1))
                    apart(dve)
                dve.tensor_tensor(contrib[k % 2][:, :, 0:D], ysum[k % 2][:], gate[k % 2][:, :, None].to_broadcast([P, CC, D]), ALU.mult)
                dve.tensor_copy(contrib[k % 2][:, :, D], gate[k % 2][:]).then_inc(S["s_con"], 1)
                if refill:
                    dve.wait_ge(S["s_sc"], 16 * CC * e)
                    apart(dve)
                    dve.tensor_copy(cur[(k + 3) % 4][:], idx_pc[:, e + 3]).then_inc(S["s_cur"], 1)

            dve.wait_ge(S["s_ldr"], 16)
            for e in range(3):
                dve.tensor_copy(cur[e][:], idx_pc[:, e]).then_inc(S["s_cur"], 1)
            dve.wait_ge(S["s_ec"], 8)
            dve_expert(0, 0)
            dve_expert(1, 1)
            dve_expert(2, 2)
            dve_expert(3, 3)
            with dve.Fori(1, E1 // 4 - 1) as i:
                for k in range(4):
                    dve_expert(4 * i + k, k)
            for k in range(4):
                dve_expert(E1 - 4 + k, k, k < 1)
            fs = Steps("s_fs", 4)
            n = TILES // 4
            for k in range(4):
                dve.wait_ge(S[f"s_sum{k}"], 16)
                t = slice(k * n, (k + 1) * n)
                fs(dve.scalar_tensor_tensor(gsum[:, t], sums[:, t, D], 0.0, sums[:, t, D], ALU.is_le, ALU.add))
                dve.reciprocal(gsum[:, t], gsum[:, t]).then_inc(S["s_gsum"], 1)
                dve.wait_ge(S["s_gsum"], k + 1)
                for m in range(k * n, k * n + n // 2):
                    last = dve.scalar_tensor_tensor(x3[:, m], sums[:, m, 0:D], gsum[:, m:m + 1], x3[:, m], ALU.mult, ALU.add)
                last.then_inc(S["s_fin"], 1)


def layout(i):
    i = {n: np.asarray(v) for n, v in i.items()}
    o = dict(i)
    o["L0_ffn_gate_w"] = i["L0_ffn_gate_w"].T
    for n in ("Wq", "Wk", "Wv", "Wo"):
        o["L1_attn_" + n] = i["L1_attn_" + n].T
    for n in ("w1", "w3"):
        routed = i["L0_ffn_" + n].transpose(2, 0, 1)
        shared = i["L0_ffn_s" + n].reshape(SHARED, P, D).transpose(2, 0, 1)
        o["L0_" + n] = np.concatenate([routed, shared], axis=1)
        del o["L0_ffn_" + n], o["L0_ffn_s" + n]
    routed = i["L0_ffn_w2"].transpose(2, 0, 1)
    shared = i["L0_ffn_sw2"].T.reshape(SHARED, P, D).transpose(1, 0, 2)
    o["L0_w2"] = np.concatenate([routed, shared], axis=1)
    del o["L0_ffn_w2"], o["L0_ffn_sw2"]
    o["L1_ffn_router_weight"] = i["L1_ffn_router_weight"].T
    o["L1_ffn_fc1_weight"] = i["L1_ffn_fc1_weight"].transpose(2, 0, 1)
    o["L1_ffn_fc1_bias"] = i["L1_ffn_fc1_bias"].reshape(E1, FC, P).transpose(2, 0, 1)
    o["L1_ffn_fc2_weight"] = i["L1_ffn_fc2_weight"].reshape(E1, D, FC, P).transpose(3, 0, 2, 1)
    return {n: np.ascontiguousarray(v) for n, v in o.items()}


def kernel(**inputs):
    import concourse.bacc as bacc
    from concourse.bass_utils import run_bass_kernel_spmd

    nc = bacc.Bacc("TRN2", target_bir_lowering=False, num_devices=1)
    arrays = layout(inputs)
    a = {n: nc.dram_tensor("in_" + n, v.shape, mybir.dt.from_np(v.dtype), kind="ExternalInput").ap() for n, v in arrays.items()}
    out = nc.dram_tensor("out", (BATCH, SEQ, D), F32, kind="ExternalOutput").ap()
    build_kernel(nc, a, out)
    r = run_bass_kernel_spmd(nc, [{"in_" + n: v for n, v in arrays.items()}], core_ids=[0])
    return r.results[0]["out"]
```
